# Optimizing a Trainium2 kernel written in Bass

```python
import numpy as np
import jax
import jax.numpy as jnp

def _softmax(x, axis=-1):
    return jax.nn.softmax(x, axis=axis)

def _gelu(x):
    return jax.nn.gelu(x, approximate=True)

def _silu(x):
    return jax.nn.silu(x)

def _sigmoid(x):
    return jax.nn.sigmoid(x)

def _layernorm(x, axis=-1, eps=1e-05):
    m = jnp.mean(x, axis=axis, keepdims=True)
    v = jnp.var(x, axis=axis, keepdims=True)
    return (x - m) / jnp.sqrt(v + eps)

def _scatter_add(tgt, idx, src, axis=0):
    return tgt.at[idx].add(src)

def _segment_sum(src, seg, n):
    return jax.ops.segment_sum(src, seg, n)
kernel_name = 'mk_perceiver_d4_seqx_r4_264e28'

def setup_inputs(seed: int=0):
    np.random.seed(seed)
    _w = jnp.asarray

    def _rec_inputs():
        import jax
        import jax.numpy as jnp
        _rk = jax.random.key(seed)
        x = -0.0003929 + 0.9999 * jax.random.normal(jax.random.fold_in(_rk, 1), (1, 128, 256), jnp.float32)
        _lenS = 128 - jax.random.randint(jax.random.fold_in(_rk, 7), (1,), 0, max(1, 128 // 4) + 1, jnp.int32)
        _lenS2 = 12544 - jax.random.randint(jax.random.fold_in(_rk, 8), (1,), 0, max(1, 12544 // 4) + 1, jnp.int32)
        _ctx_512P = jax.random.normal(jax.random.fold_in(_rk, 11), (1, 16, 128), jnp.float32)
        _ctx_512c = jax.random.dirichlet(jax.random.fold_in(_rk, 511), 0.3 * jnp.ones((16,), jnp.float32), (1, 12544))
        _ctx_512t = jnp.einsum('bsk,bkd->bsd', _ctx_512c, _ctx_512P)
        _ctx_512t = _ctx_512t * jax.lax.rsqrt(jnp.mean(jnp.square(_ctx_512t)) + 1e-12) * 0.953939
        ctx_512 = -1.39393e-06 + 0.999914 * (_ctx_512t + 0.3 * jax.random.normal(jax.random.fold_in(_rk, 611), (1, 12544, 128), jnp.float32))
        itok_BxS2xS_0_7 = jax.random.randint(jax.random.fold_in(_rk, 12), (1, 12544, 128), 0, 8, jnp.int32)
        return (x, ctx_512, itok_BxS2xS_0_7)
    x, ctx_512, itok_BxS2xS_0_7 = _rec_inputs()

    def _L0_xattn_setup():
        import jax, jax.numpy as jnp
        import numpy as np
        HEADS = 16
        D_MODEL = 256
        IMG_MODEL = 128
        D_K = D_MODEL // HEADS
        key = jax.random.key(seed)
        ks = jax.random.split(key, 12)
        B, LQ, LKV = (8, 512, 256)
        s_dm = 1.0 / np.sqrt(D_MODEL)
        s_im = 1.0 / np.sqrt(IMG_MODEL)
        return {'q': jax.random.normal(ks[0], (B, LQ, D_MODEL), jnp.float32), 'k': jax.random.normal(ks[1], (B, LKV, IMG_MODEL), jnp.float32), 'v': jax.random.normal(ks[2], (B, LKV, IMG_MODEL), jnp.float32), 'Wq': jax.random.normal(ks[3], (D_MODEL, D_MODEL), jnp.float32) * s_dm, 'bq': jnp.zeros((D_MODEL,), jnp.float32), 'Wk': jax.random.normal(ks[4], (IMG_MODEL, D_MODEL), jnp.float32) * s_im, 'bk': jnp.zeros((D_MODEL,), jnp.float32), 'Wv': jax.random.normal(ks[5], (IMG_MODEL, D_MODEL), jnp.float32) * s_im, 'bv': jnp.zeros((D_MODEL,), jnp.float32), 'Wo': jax.random.normal(ks[6], (D_MODEL, D_MODEL), jnp.float32) * s_dm, 'bo': jnp.zeros((D_MODEL,), jnp.float32)}
    _L0_xattn_all = _L0_xattn_setup()
    _L0_xattn_in = {k: v for k, v in _L0_xattn_all.items() if k in ('Wq', 'bq', 'Wk', 'bk', 'Wv', 'bv', 'Wo', 'bo')}
    del _L0_xattn_all

    def _L0_attn_setup():
        import jax, jax.numpy as jnp
        import numpy as np
        DIM = 256
        NH = 16
        HD = DIM // NH
        NT = max(1, int(NH * 0.25))
        NS = NH - NT
        SCALE = HD ** (-0.5)
        key = jax.random.key(seed)
        ks = jax.random.split(key, 8)
        B, T = (2, 512)
        init = 0.02
        return {'x': jax.random.normal(ks[0], (B, T, DIM), dtype=jnp.float32), 'Wqt': jax.random.normal(ks[1], (DIM, NT * HD), dtype=jnp.float32) * init, 'Wkt': jax.random.normal(ks[2], (DIM, NT * HD), dtype=jnp.float32) * init, 'Wqs': jax.random.normal(ks[3], (DIM, NS * HD), dtype=jnp.float32) * init, 'Wks': jax.random.normal(ks[4], (DIM, NS * HD), dtype=jnp.float32) * init, 'Wv': jax.random.normal(ks[5], (DIM, DIM), dtype=jnp.float32) * init, 'Wout': jax.random.normal(ks[6], (DIM, DIM), dtype=jnp.float32) * init, 'bout': jnp.zeros((DIM,), dtype=jnp.float32), 'w_sigma': jnp.zeros((1,), dtype=jnp.float32)}
    _L0_attn_all = _L0_attn_setup()
    _L0_attn_in = {k: v for k, v in _L0_attn_all.items() if k in ('Wqt', 'Wkt', 'Wqs', 'Wks', 'Wv', 'Wout', 'bout', 'w_sigma')}
    del _L0_attn_all

    def _L0_ffn_setup():
        import jax, jax.numpy as jnp
        import numpy as np
        BLOCK = 32
        W_BITS = 4
        ACT_BITS = 16

        def act_qdq(x):
            qmax = 2.0 ** (ACT_BITS - 1) - 1.0
            scale = jnp.maximum(jnp.max(jnp.abs(x)) / qmax, 1e-12)
            return jnp.clip(jnp.round(x / scale), -qmax - 1.0, qmax) * scale

        def fixed_qdq_u16(x):
            scale = 1.0 / 65536.0
            return jnp.clip(jnp.round(x / scale), 0.0, 65535.0) * scale

        def lpbq_dequant(w):
            O, I = w.shape
            qmax = 2.0 ** (W_BITS - 1) - 1.0
            wb = w.reshape(O, I // BLOCK, BLOCK)
            s = jnp.maximum(jnp.max(jnp.abs(wb), axis=-1, keepdims=True) / qmax, 1e-12)
            wq = jnp.clip(jnp.round(wb / s), -qmax - 1.0, qmax) * s
            return wq.reshape(O, I)
        key = jax.random.key(seed)
        k1, k2, k3, k4 = jax.random.split(key, 4)
        B, S, H, I = (2, 1024, 256, 768)
        x = jax.random.normal(k1, (B, S, H), jnp.float32)
        w_gate = jax.random.normal(k2, (I, H), jnp.float32) * 0.02
        w_up = jax.random.normal(k3, (I, H), jnp.float32) * 0.02
        w_down = jax.random.normal(k4, (H, I), jnp.float32) * 0.02
        return {'x': x, 'w_gate': w_gate, 'w_up': w_up, 'w_down': w_down}
    _L0_ffn_all = _L0_ffn_setup()
    _L0_ffn_in = {k: v for k, v in _L0_ffn_all.items() if k in ('w_gate', 'w_up', 'w_down')}
    del _L0_ffn_all

    def _L1_xattn_setup():
        import jax, jax.numpy as jnp
        import numpy as np
        NUM_HEADS = 16
        HEAD_DIM = 64
        Q_DIM = 256
        KV_DIM = 128
        INNER = NUM_HEADS * HEAD_DIM
        key = jax.random.key(seed)
        ks = jax.random.split(key, 7)
        B, N, M = (32, 128, 512)
        q = jax.random.normal(ks[0], (B, N, Q_DIM), dtype=jnp.float32)
        kv = jax.random.normal(ks[1], (B, M, KV_DIM), dtype=jnp.float32)
        Wq = jax.random.normal(ks[2], (Q_DIM, INNER), dtype=jnp.float32) / np.sqrt(Q_DIM)
        Wk = jax.random.normal(ks[3], (KV_DIM, INNER), dtype=jnp.float32) / np.sqrt(KV_DIM)
        Wv = jax.random.normal(ks[4], (KV_DIM, INNER), dtype=jnp.float32) / np.sqrt(KV_DIM)
        Wo = jax.random.normal(ks[5], (INNER, Q_DIM), dtype=jnp.float32) / np.sqrt(INNER)
        bo = jax.random.normal(ks[6], (Q_DIM,), dtype=jnp.float32) * 0.01
        return {'q': q, 'kv': kv, 'Wq': Wq, 'Wk': Wk, 'Wv': Wv, 'Wo': Wo, 'bo': bo}
    _L1_xattn_all = _L1_xattn_setup()
    _L1_xattn_in = {k: v for k, v in _L1_xattn_all.items() if k in ('Wq', 'Wk', 'Wv', 'Wo', 'bo')}
    del _L1_xattn_all

    def _L1_attn_setup():
        import jax, jax.numpy as jnp
        import numpy as np
        key = jax.random.key(seed)
        ks = jax.random.split(key, 5)
        B, S, D = (2, 512, 256)
        scale = 0.02
        return {'x': jax.random.normal(ks[0], (B, S, D), dtype=jnp.float32), 'q_proj_weight': jax.random.normal(ks[1], (D, D), dtype=jnp.float32) * scale, 'k_proj_weight': jax.random.normal(ks[2], (D, D), dtype=jnp.float32) * scale, 'v_proj_weight': jax.random.normal(ks[3], (D, D), dtype=jnp.float32) * scale, 'o_proj_weight': jax.random.normal(ks[4], (D, D), dtype=jnp.float32) * scale}
    _L1_attn_all = _L1_attn_setup()
    _L1_attn_in = {k: v for k, v in _L1_attn_all.items() if k in ('q_proj_weight', 'k_proj_weight', 'v_proj_weight', 'o_proj_weight')}
    del _L1_attn_all

    def _L1_ffn_setup():
        import jax, jax.numpy as jnp
        import numpy as np
        D_IN, D_HID = (256, 1024)

        def _ternary(key, shape):
            return jax.random.randint(key, shape, -1, 2).astype(jnp.float32)

        def _tlin(x, w, s):
            return jnp.einsum('bsi,oi->bso', x, w) * s
        key = jax.random.key(seed)
        ks = jax.random.split(key, 12)
        inv = lambda fan: 1.0 / np.sqrt(fan).astype(np.float32)
        return {'x': jax.random.normal(ks[0], (4, 512, D_IN), dtype=jnp.float32), 'w1_w': _ternary(ks[1], (D_HID, D_IN)), 'w1_s': jax.random.uniform(ks[2], (D_HID,), dtype=jnp.float32) * inv(D_IN), 'w2_w': _ternary(ks[3], (D_HID, D_IN)), 'w2_s': jax.random.uniform(ks[4], (D_HID,), dtype=jnp.float32) * inv(D_IN), 'h1_w': _ternary(ks[5], (D_HID, D_HID)), 'h1_s': jax.random.uniform(ks[6], (D_HID,), dtype=jnp.float32) * inv(D_HID), 'h2_w': _ternary(ks[7], (D_HID, D_HID)), 'h2_s': jax.random.uniform(ks[8], (D_HID,), dtype=jnp.float32) * inv(D_HID), 'w3_w': _ternary(ks[9], (D_IN, D_HID)), 'w3_s': jax.random.uniform(ks[10], (D_IN,), dtype=jnp.float32) * inv(D_HID)}
    _L1_ffn_all = _L1_ffn_setup()
    _L1_ffn_in = {k: v for k, v in _L1_ffn_all.items() if k in ('w1_w', 'w1_s', 'w2_w', 'w2_s', 'h1_w', 'h1_s', 'h2_w', 'h2_s', 'w3_w', 'w3_s')}
    del _L1_ffn_all

    def _L2_xattn_setup():
        import jax, jax.numpy as jnp
        import numpy as np
        DIM = 256
        LATENT_DIM = 128
        NUM_HEADS = 16
        HEAD_DIM = DIM // NUM_HEADS
        SCALE = HEAD_DIM ** (-0.5)
        key = jax.random.key(seed)
        k1, k2, k3, k4, k5 = jax.random.split(key, 5)
        B, xN, zN = (2, 512, 512)
        x = jax.random.normal(k1, (B, xN, DIM), dtype=jnp.float32)
        z = jax.random.normal(k2, (B, zN, LATENT_DIM), dtype=jnp.float32)
        Wq = jax.random.normal(k3, (DIM, DIM), dtype=jnp.float32) * DIM ** (-0.5)
        Wkv = jax.random.normal(k4, (2 * DIM, LATENT_DIM), dtype=jnp.float32) * LATENT_DIM ** (-0.5)
        Wo = jax.random.normal(k5, (DIM, DIM), dtype=jnp.float32) * DIM ** (-0.5)
        return {'x': x, 'z': z, 'Wq': Wq, 'Wkv': Wkv, 'Wo': Wo}
    _L2_xattn_all = _L2_xattn_setup()
    _L2_xattn_in = {k: v for k, v in _L2_xattn_all.items() if k in ('Wq', 'Wkv', 'Wo')}
    del _L2_xattn_all

    def _L2_attn_setup():
        import jax, jax.numpy as jnp
        import numpy as np
        N_EMBD = 256
        N_HEAD = 16
        HEAD_SIZE = 64
        LN_EPS = 0.001
        key = jax.random.key(seed)
        ks = jax.random.split(key, 7)
        B, S, D, H, E = (4, 512, N_EMBD, N_HEAD, HEAD_SIZE)
        x = jax.random.normal(ks[0], (B, S, D), dtype=jnp.float32)
        scale = 1.0 / np.sqrt(D)
        Wq = jax.random.normal(ks[1], (H, D, E), dtype=jnp.float32) * scale
        Wk = jax.random.normal(ks[2], (H, D, E), dtype=jnp.float32) * scale
        Wv = jax.random.normal(ks[3], (H, D, E), dtype=jnp.float32) * scale
        Wo = jax.random.normal(ks[4], (H * E, D), dtype=jnp.float32) * scale
        gamma = jnp.ones((D,), dtype=jnp.float32)
        beta = jnp.zeros((D,), dtype=jnp.float32)
        return {'x': x, 'Wq': Wq, 'Wk': Wk, 'Wv': Wv, 'Wo': Wo, 'gamma': gamma, 'beta': beta}
    _L2_attn_all = _L2_attn_setup()
    _L2_attn_in = {k: v for k, v in _L2_attn_all.items() if k in ('Wq', 'Wk', 'Wv', 'Wo', 'gamma', 'beta')}
    del _L2_attn_all

    def _L2_ffn_setup():
        import jax, jax.numpy as jnp
        import numpy as np
        B, S, D_IN, D_OUT = (16, 1024, 256, 256)
        ACT_BITS = 8
        QB = float(2 ** (ACT_BITS - 1) - 1)
        key = jax.random.key(seed)
        k1, k2, k3 = jax.random.split(key, 3)
        x = jax.random.normal(k1, (B, S, D_IN), dtype=jnp.float32)
        ternary_weight = jax.random.randint(k2, (D_OUT, D_IN), 0, 3, dtype=jnp.int32)
        bias = jax.random.normal(k3, (D_OUT,), dtype=jnp.float32)
        act_scale = (jnp.max(jnp.abs(x)) / QB).astype(jnp.float32)
        return {'x': x, 'ternary_weight': ternary_weight, 'bias': bias, 'act_scale': act_scale}
    _L2_ffn_all = _L2_ffn_setup()
    _L2_ffn_in = {k: v for k, v in _L2_ffn_all.items() if k in ('ternary_weight', 'bias', 'act_scale')}
    del _L2_ffn_all

    def _L3_xattn_setup():
        import jax, jax.numpy as jnp
        import numpy as np
        key = jax.random.key(seed)
        k1, k2, k3, k4, k5 = jax.random.split(key, 5)
        B, K, S, E, I, D = (4, 2, 128, 8, 256, 512)
        x = jax.random.normal(k1, (B, S, I), dtype=jnp.float32)
        weights = jax.random.uniform(k2, (B, K, S), dtype=jnp.float32)
        ensembles = jax.random.randint(k3, (B, K, S), 0, E, dtype=jnp.int64)
        lim1 = float(np.sqrt(6.0 / (D + I)))
        proj_in = jax.random.uniform(k4, (E, D, I), dtype=jnp.float32, minval=-lim1, maxval=lim1)
        proj_out = jax.random.uniform(k5, (E, I, D), dtype=jnp.float32, minval=-lim1, maxval=lim1)
        return {'x': x, 'weights': weights, 'ensembles': ensembles, 'proj_in': proj_in, 'proj_out': proj_out}
    _L3_xattn_all = _L3_xattn_setup()
    _L3_xattn_in = {k: v for k, v in _L3_xattn_all.items() if k in ('proj_in', 'proj_out')}
    del _L3_xattn_all

    def _L3_attn_setup():
        import jax, jax.numpy as jnp
        import numpy as np
        MODEL_DIM = 256
        NUM_HEADS = 16
        HEAD_DIM = MODEL_DIM // NUM_HEADS
        EPS = 1e-12
        CHUNK = 128

        def _pos_elu(t):
            return jax.nn.elu(t) + 1.0

        def _linear_attention(q, k, v):
            b, h, l, d = q.shape
            nc = l // CHUNK
            qc = jnp.moveaxis(q.reshape(b, h, nc, CHUNK, d), 2, 0)
            kc = jnp.moveaxis(k.reshape(b, h, nc, CHUNK, d), 2, 0)
            vc = jnp.moveaxis(v.reshape(b, h, nc, CHUNK, d), 2, 0)
            mask = jnp.tril(jnp.ones((CHUNK, CHUNK), dtype=q.dtype))

            def step(carry, inp):
                S, z = carry
                qb, kb, vb = inp
                scores = jnp.einsum('bhcd,bhsd->bhcs', qb, kb) * mask
                num = jnp.einsum('bhcd,bhde->bhce', qb, S) + jnp.einsum('bhcs,bhse->bhce', scores, vb)
                den = jnp.einsum('bhcd,bhd->bhc', qb, z) + scores.sum(-1)
                out = num / den[..., None] + EPS
                S = S + jnp.einsum('bhsd,bhse->bhde', kb, vb)
                z = z + kb.sum(axis=2)
                return ((S, z), out)
            S0 = jnp.zeros((b, h, d, d), dtype=q.dtype)
            z0 = jnp.zeros((b, h, d), dtype=q.dtype)
            _, outs = jax.lax.scan(step, (S0, z0), (qc, kc, vc))
            return jnp.moveaxis(outs, 0, 1).transpose(0, 3, 1, 2, 4).reshape(b, h * 0 + l // l, 0, 0) if False else outs
        key = jax.random.key(seed)
        kx, kq, kk, kv, ko = jax.random.split(key, 5)
        b, l = (4, 1024)
        x = jax.random.normal(kx, (b, l, MODEL_DIM), dtype=jnp.float32)
        Wq = 0.02 * jax.random.normal(kq, (MODEL_DIM, MODEL_DIM), dtype=jnp.float32)
        Wk = 0.02 * jax.random.normal(kk, (MODEL_DIM, MODEL_DIM), dtype=jnp.float32)
        Wv = 0.02 * jax.random.normal(kv, (MODEL_DIM, MODEL_DIM), dtype=jnp.float32)
        Wo = 0.02 * jax.random.normal(ko, (MODEL_DIM, MODEL_DIM), dtype=jnp.float32)
        return {'x': x, 'Wq': Wq, 'Wk': Wk, 'Wv': Wv, 'Wo': Wo}
    _L3_attn_all = _L3_attn_setup()
    _L3_attn_in = {k: v for k, v in _L3_attn_all.items() if k in ('Wq', 'Wk', 'Wv', 'Wo')}
    del _L3_attn_all

    def _L3_ffn_setup():
        import jax, jax.numpy as jnp
        import numpy as np
        B, S, DIM = (4, 512, 256)
        E, K, HID = (8, 2, 1024)
        key = jax.random.key(seed)
        ks = jax.random.split(key, 8)
        init = lambda k, sh: jax.random.normal(k, sh, jnp.float32) * 0.02
        return {'x': jax.random.normal(ks[0], (B, S, DIM), jnp.float32), 'gate_w': init(ks[1], (DIM, E)), 'gate_b': jnp.zeros((E,), jnp.float32), 'w1': init(ks[2], (E, DIM, HID)), 'b1': jnp.zeros((E, HID), jnp.float32), 'w2': init(ks[3], (E, HID, DIM)), 'b2': jnp.zeros((E, DIM), jnp.float32), 'ws1': init(ks[4], (DIM, HID)), 'bs1': jnp.zeros((HID,), jnp.float32), 'ws2': init(ks[5], (HID, DIM)), 'bs2': jnp.zeros((DIM,), jnp.float32)}
    _L3_ffn_all = _L3_ffn_setup()
    _L3_ffn_in = {k: v for k, v in _L3_ffn_all.items() if k in ('gate_w', 'gate_b', 'w1', 'b1', 'w2', 'b2', 'ws1', 'bs1', 'ws2', 'bs2')}
    del _L3_ffn_all
    return {'x': x, 'ctx_512': ctx_512, 'itok_BxS2xS_0_7': itok_BxS2xS_0_7, 'L0_xattn_Wq': _L0_xattn_in['Wq'], 'L0_xattn_bq': _L0_xattn_in['bq'], 'L0_xattn_Wk': _L0_xattn_in['Wk'], 'L0_xattn_bk': _L0_xattn_in['bk'], 'L0_xattn_Wv': _L0_xattn_in['Wv'], 'L0_xattn_bv': _L0_xattn_in['bv'], 'L0_xattn_Wo': _L0_xattn_in['Wo'], 'L0_xattn_bo': _L0_xattn_in['bo'], 'L0_attn_Wqt': _L0_attn_in['Wqt'], 'L0_attn_Wkt': _L0_attn_in['Wkt'], 'L0_attn_Wqs': _L0_attn_in['Wqs'], 'L0_attn_Wks': _L0_attn_in['Wks'], 'L0_attn_Wv': _L0_attn_in['Wv'], 'L0_attn_Wout': _L0_attn_in['Wout'], 'L0_attn_bout': _L0_attn_in['bout'], 'L0_attn_w_sigma': _L0_attn_in['w_sigma'], 'L0_ffn_w_gate': _L0_ffn_in['w_gate'], 'L0_ffn_w_up': _L0_ffn_in['w_up'], 'L0_ffn_w_down': _L0_ffn_in['w_down'], 'L1_xattn_Wq': _L1_xattn_in['Wq'], 'L1_xattn_Wk': _L1_xattn_in['Wk'], 'L1_xattn_Wv': _L1_xattn_in['Wv'], 'L1_xattn_Wo': _L1_xattn_in['Wo'], 'L1_xattn_bo': _L1_xattn_in['bo'], 'L1_attn_q_proj_weight': _L1_attn_in['q_proj_weight'], 'L1_attn_k_proj_weight': _L1_attn_in['k_proj_weight'], 'L1_attn_v_proj_weight': _L1_attn_in['v_proj_weight'], 'L1_attn_o_proj_weight': _L1_attn_in['o_proj_weight'], 'L1_ffn_w1_w': _L1_ffn_in['w1_w'], 'L1_ffn_w1_s': _L1_ffn_in['w1_s'], 'L1_ffn_w2_w': _L1_ffn_in['w2_w'], 'L1_ffn_w2_s': _L1_ffn_in['w2_s'], 'L1_ffn_h1_w': _L1_ffn_in['h1_w'], 'L1_ffn_h1_s': _L1_ffn_in['h1_s'], 'L1_ffn_h2_w': _L1_ffn_in['h2_w'], 'L1_ffn_h2_s': _L1_ffn_in['h2_s'], 'L1_ffn_w3_w': _L1_ffn_in['w3_w'], 'L1_ffn_w3_s': _L1_ffn_in['w3_s'], 'L2_xattn_Wq': _L2_xattn_in['Wq'], 'L2_xattn_Wkv': _L2_xattn_in['Wkv'], 'L2_xattn_Wo': _L2_xattn_in['Wo'], 'L2_attn_Wq': _L2_attn_in['Wq'], 'L2_attn_Wk': _L2_attn_in['Wk'], 'L2_attn_Wv': _L2_attn_in['Wv'], 'L2_attn_Wo': _L2_attn_in['Wo'], 'L2_attn_gamma': _L2_attn_in['gamma'], 'L2_attn_beta': _L2_attn_in['beta'], 'L2_ffn_ternary_weight': _L2_ffn_in['ternary_weight'], 'L2_ffn_bias': _L2_ffn_in['bias'], 'L2_ffn_act_scale': _L2_ffn_in['act_scale'], 'L3_xattn_proj_in': _L3_xattn_in['proj_in'], 'L3_xattn_proj_out': _L3_xattn_in['proj_out'], 'L3_attn_Wq': _L3_attn_in['Wq'], 'L3_attn_Wk': _L3_attn_in['Wk'], 'L3_attn_Wv': _L3_attn_in['Wv'], 'L3_attn_Wo': _L3_attn_in['Wo'], 'L3_ffn_gate_w': _L3_ffn_in['gate_w'], 'L3_ffn_gate_b': _L3_ffn_in['gate_b'], 'L3_ffn_w1': _L3_ffn_in['w1'], 'L3_ffn_b1': _L3_ffn_in['b1'], 'L3_ffn_w2': _L3_ffn_in['w2'], 'L3_ffn_b2': _L3_ffn_in['b2'], 'L3_ffn_ws1': _L3_ffn_in['ws1'], 'L3_ffn_bs1': _L3_ffn_in['bs1'], 'L3_ffn_ws2': _L3_ffn_in['ws2'], 'L3_ffn_bs2': _L3_ffn_in['bs2']}

def reference(x, ctx_512, itok_BxS2xS_0_7, L0_xattn_Wq, L0_xattn_bq, L0_xattn_Wk, L0_xattn_bk, L0_xattn_Wv, L0_xattn_bv, L0_xattn_Wo, L0_xattn_bo, L0_attn_Wqt, L0_attn_Wkt, L0_attn_Wqs, L0_attn_Wks, L0_attn_Wv, L0_attn_Wout, L0_attn_bout, L0_attn_w_sigma, L0_ffn_w_gate, L0_ffn_w_up, L0_ffn_w_down, L1_xattn_Wq, L1_xattn_Wk, L1_xattn_Wv, L1_xattn_Wo, L1_xattn_bo, L1_attn_q_proj_weight, L1_attn_k_proj_weight, L1_attn_v_proj_weight, L1_attn_o_proj_weight, L1_ffn_w1_w, L1_ffn_w1_s, L1_ffn_w2_w, L1_ffn_w2_s, L1_ffn_h1_w, L1_ffn_h1_s, L1_ffn_h2_w, L1_ffn_h2_s, L1_ffn_w3_w, L1_ffn_w3_s, L2_xattn_Wq, L2_xattn_Wkv, L2_xattn_Wo, L2_attn_Wq, L2_attn_Wk, L2_attn_Wv, L2_attn_Wo, L2_attn_gamma, L2_attn_beta, L2_ffn_ternary_weight, L2_ffn_bias, L2_ffn_act_scale, L3_xattn_proj_in, L3_xattn_proj_out, L3_attn_Wq, L3_attn_Wk, L3_attn_Wv, L3_attn_Wo, L3_ffn_gate_w, L3_ffn_gate_b, L3_ffn_w1, L3_ffn_b1, L3_ffn_w2, L3_ffn_b2, L3_ffn_ws1, L3_ffn_bs1, L3_ffn_ws2, L3_ffn_bs2):
    import jax
    import jax.numpy as jnp

    def _L0_xattn_ref(q, k, v, Wq, bq, Wk, bk, Wv, bv, Wo, bo):
        import jax, jax.numpy as jnp
        import numpy as np
        HEADS = 16
        D_MODEL = 256
        IMG_MODEL = 128
        D_K = D_MODEL // HEADS
        B, LQ, _ = q.shape
        LKV = k.shape[1]
        qh = (q @ Wq + bq).reshape(B, LQ, HEADS, D_K).transpose(0, 2, 1, 3)
        kh = (k @ Wk + bk).reshape(B, LKV, HEADS, D_K).transpose(0, 2, 1, 3)
        vh = (v @ Wv + bv).reshape(B, LKV, HEADS, D_K).transpose(0, 2, 1, 3)
        scale = 1.0 / np.sqrt(D_K)
        scores = jnp.einsum('bhqd,bhkd->bhqk', qh, kh) * scale
        attn = jax.nn.softmax(scores, axis=-1)
        out = jnp.einsum('bhqk,bhkd->bhqd', attn, vh)
        concat = out.transpose(0, 2, 1, 3).reshape(B, LQ, D_MODEL)
        return concat @ Wo + bo

    def _L0_attn_ref(x, Wqt, Wkt, Wqs, Wks, Wv, Wout, bout, w_sigma):
        import jax, jax.numpy as jnp
        import numpy as np
        DIM = 256
        NH = 16
        HD = DIM // NH
        NT = max(1, int(NH * 0.25))
        NS = NH - NT
        SCALE = HD ** (-0.5)
        B, T, D = x.shape
        Qt = (x @ Wqt).reshape(B, T, NT, HD)
        Kt = (x @ Wkt).reshape(B, T, NT, HD)
        Qs = (x @ Wqs).reshape(B, T, NS, HD)
        Ks = (x @ Wks).reshape(B, T, NS, HD)
        st = jnp.einsum('bthd,bshd->bths', Qt, Kt)
        ss = jnp.einsum('bthd,bshd->bths', Qs, Ks)
        sig = jax.nn.sigmoid(w_sigma)
        score = jnp.concatenate([-sig * st, ss], axis=2) * SCALE
        attn = jax.nn.softmax(score, axis=-1)
        V = (x @ Wv).reshape(B, T, NH, HD)
        ctx = jnp.einsum('bths,bshd->bthd', attn, V).reshape(B, T, D)
        return ctx @ Wout + bout

    def _L0_ffn_ref(x, w_gate, w_up, w_down):
        import jax, jax.numpy as jnp
        import numpy as np
        BLOCK = 32
        W_BITS = 4
        ACT_BITS = 16

        def act_qdq(x):
            qmax = 2.0 ** (ACT_BITS - 1) - 1.0
            scale = jnp.maximum(jnp.max(jnp.abs(x)) / qmax, 1e-12)
            return jnp.clip(jnp.round(x / scale), -qmax - 1.0, qmax) * scale

        def fixed_qdq_u16(x):
            scale = 1.0 / 65536.0
            return jnp.clip(jnp.round(x / scale), 0.0, 65535.0) * scale

        def lpbq_dequant(w):
            O, I = w.shape
            qmax = 2.0 ** (W_BITS - 1) - 1.0
            wb = w.reshape(O, I // BLOCK, BLOCK)
            s = jnp.maximum(jnp.max(jnp.abs(wb), axis=-1, keepdims=True) / qmax, 1e-12)
            wq = jnp.clip(jnp.round(wb / s), -qmax - 1.0, qmax) * s
            return wq.reshape(O, I)
        x = act_qdq(x)
        up = act_qdq(x @ lpbq_dequant(w_up).T)
        gate = act_qdq(x @ lpbq_dequant(w_gate).T)
        sig = fixed_qdq_u16(jax.nn.sigmoid(gate))
        gate = act_qdq(gate * sig)
        o = act_qdq(gate * up)
        return o @ lpbq_dequant(w_down).T

    def _L1_xattn_ref(q, kv, Wq, Wk, Wv, Wo, bo):
        import jax, jax.numpy as jnp
        import numpy as np
        NUM_HEADS = 16
        HEAD_DIM = 64
        Q_DIM = 256
        KV_DIM = 128
        INNER = NUM_HEADS * HEAD_DIM
        B, N, _ = q.shape
        M = kv.shape[1]
        scale = HEAD_DIM ** (-0.5)
        qh = (q @ Wq).reshape(B, N, NUM_HEADS, HEAD_DIM).transpose(0, 2, 1, 3)
        kh = (kv @ Wk).reshape(B, M, NUM_HEADS, HEAD_DIM).transpose(0, 2, 1, 3)
        vh = (kv @ Wv).reshape(B, M, NUM_HEADS, HEAD_DIM).transpose(0, 2, 1, 3)
        scores = jnp.einsum('bhnd,bhmd->bhnm', qh, kh) * scale
        attn = jax.nn.softmax(scores, axis=-1)
        out = jnp.einsum('bhnm,bhmd->bhnd', attn, vh)
        out = out.transpose(0, 2, 1, 3).reshape(B, N, INNER)
        return out @ Wo + bo

    def _L1_attn_ref(x, q_proj_weight, k_proj_weight, v_proj_weight, o_proj_weight):
        import jax, jax.numpy as jnp
        import numpy as np
        num_heads = 16
        B, S, d_in = x.shape
        d_k = q_proj_weight.shape[0]
        head_size = d_k // num_heads

        def split_heads(t):
            return t.reshape(B, S, num_heads, head_size).transpose(0, 2, 1, 3)
        q = split_heads(jnp.einsum('bsd,kd->bsk', x, q_proj_weight))
        k = split_heads(jnp.einsum('bsd,kd->bsk', x, k_proj_weight))
        v = split_heads(jnp.einsum('bsd,kd->bsk', x, v_proj_weight))
        scale = jnp.float32(head_size) ** (-0.5)
        scores = jnp.einsum('bhtc,bhkc->bhtk', q, k) * scale
        causal = jnp.tril(jnp.ones((S, S), dtype=bool))
        scores = jnp.where(causal, scores, -jnp.inf)
        attn = jax.nn.softmax(scores, axis=-1)
        out = jnp.einsum('bhtk,bhkc->bhtc', attn, v)
        out = out.transpose(0, 2, 1, 3).reshape(B, S, d_k)
        return jnp.einsum('bsv,dv->bsd', out, o_proj_weight)

    def _L1_ffn_ref(x, w1_w, w1_s, w2_w, w2_s, h1_w, h1_s, h2_w, h2_s, w3_w, w3_s):
        import jax, jax.numpy as jnp
        import numpy as np
        D_IN, D_HID = (256, 1024)

        def _ternary(key, shape):
            return jax.random.randint(key, shape, -1, 2).astype(jnp.float32)

        def _tlin(x, w, s):
            return jnp.einsum('bsi,oi->bso', x, w) * s
        h = jax.nn.silu(_tlin(x, w1_w, w1_s)) * _tlin(x, w2_w, w2_s)
        h = jax.nn.gelu(_tlin(h, h1_w, h1_s), approximate=False)
        h = jax.nn.gelu(_tlin(h, h2_w, h2_s), approximate=False)
        return _tlin(h, w3_w, w3_s)

    def _L2_xattn_ref(x, z, Wq, Wkv, Wo):
        import jax, jax.numpy as jnp
        import numpy as np
        DIM = 256
        LATENT_DIM = 128
        NUM_HEADS = 16
        HEAD_DIM = DIM // NUM_HEADS
        SCALE = HEAD_DIM ** (-0.5)
        B, xN, _ = x.shape
        _, zN, _ = z.shape
        Q = (x @ Wq.T).reshape(B, xN, NUM_HEADS, HEAD_DIM)
        KV = (z @ Wkv.T).reshape(B, zN, 2, NUM_HEADS, HEAD_DIM)
        K = KV[:, :, 0]
        V = KV[:, :, 1]
        attn = jnp.einsum('bqhd,bkhd->bhqk', Q, K) * SCALE
        attn = jax.nn.softmax(attn, axis=-1)
        O = jnp.einsum('bhqk,bkhd->bqhd', attn, V).reshape(B, xN, DIM)
        return O @ Wo.T

    def _L2_attn_ref(x, Wq, Wk, Wv, Wo, gamma, beta):
        import jax, jax.numpy as jnp
        import numpy as np
        N_EMBD = 256
        N_HEAD = 16
        HEAD_SIZE = 64
        LN_EPS = 0.001
        B, S, D = x.shape
        H, _, E = Wq.shape
        q = jnp.einsum('bsd,hde->bhse', x, Wq)
        k = jnp.einsum('bsd,hde->bhse', x, Wk)
        v = jnp.einsum('bsd,hde->bhse', x, Wv)
        scores = jnp.einsum('bhse,bhte->bhst', q, k)
        causal = jnp.tril(jnp.ones((S, S), dtype=bool))
        scores = jnp.where(causal, scores / jnp.sqrt(jnp.float32(E)), jnp.float32(-jnp.inf))
        attn = jax.nn.softmax(scores, axis=-1)
        out = jnp.einsum('bhst,bhte->bhse', attn, v)
        heads = out.transpose(0, 2, 1, 3).reshape(B, S, H * E)
        y = x + heads @ Wo
        mu = jnp.mean(y, axis=-1, keepdims=True)
        var = jnp.mean(jnp.square(y - mu), axis=-1, keepdims=True)
        y = (y - mu) * jax.lax.rsqrt(var + LN_EPS) * gamma + beta
        return y

    def _L2_ffn_ref(x, ternary_weight, bias, act_scale):
        import jax, jax.numpy as jnp
        import numpy as np
        B, S, D_IN, D_OUT = (16, 1024, 256, 256)
        ACT_BITS = 8
        QB = float(2 ** (ACT_BITS - 1) - 1)
        scale = jnp.maximum(act_scale, 1e-05)
        x_int = jnp.clip(jnp.round(x / scale), -QB, QB)
        x_dq = jnp.nan_to_num(x_int * scale, nan=0.0, posinf=10000.0, neginf=-10000.0)
        w = ternary_weight.astype(jnp.float32) - 1.0
        return jnp.einsum('bsi,oi->bso', x_dq, w) + bias

    def _L3_xattn_ref(x, weights, ensembles, proj_in, proj_out):
        import jax, jax.numpy as jnp
        import numpy as np
        E = proj_in.shape[0]
        h = jax.nn.relu(jnp.einsum('edi,bsi->bsed', proj_in, x))
        o = jnp.einsum('eid,bsed->bsei', proj_out, h)
        onehot = jax.nn.one_hot(ensembles, E, dtype=x.dtype)
        gate = jnp.einsum('bks,bkse->bse', weights, onehot)
        return jnp.einsum('bsei,bse->bsi', o, gate)

    def _L3_attn_ref(x, Wq, Wk, Wv, Wo):
        import jax, jax.numpy as jnp
        import numpy as np
        MODEL_DIM = 256
        NUM_HEADS = 16
        HEAD_DIM = MODEL_DIM // NUM_HEADS
        EPS = 1e-12
        CHUNK = 128

        def _pos_elu(t):
            return jax.nn.elu(t) + 1.0

        def _linear_attention(q, k, v):
            b, h, l, d = q.shape
            nc = l // CHUNK
            qc = jnp.moveaxis(q.reshape(b, h, nc, CHUNK, d), 2, 0)
            kc = jnp.moveaxis(k.reshape(b, h, nc, CHUNK, d), 2, 0)
            vc = jnp.moveaxis(v.reshape(b, h, nc, CHUNK, d), 2, 0)
            mask = jnp.tril(jnp.ones((CHUNK, CHUNK), dtype=q.dtype))

            def step(carry, inp):
                S, z = carry
                qb, kb, vb = inp
                scores = jnp.einsum('bhcd,bhsd->bhcs', qb, kb) * mask
                num = jnp.einsum('bhcd,bhde->bhce', qb, S) + jnp.einsum('bhcs,bhse->bhce', scores, vb)
                den = jnp.einsum('bhcd,bhd->bhc', qb, z) + scores.sum(-1)
                out = num / den[..., None] + EPS
                S = S + jnp.einsum('bhsd,bhse->bhde', kb, vb)
                z = z + kb.sum(axis=2)
                return ((S, z), out)
            S0 = jnp.zeros((b, h, d, d), dtype=q.dtype)
            z0 = jnp.zeros((b, h, d), dtype=q.dtype)
            _, outs = jax.lax.scan(step, (S0, z0), (qc, kc, vc))
            return jnp.moveaxis(outs, 0, 1).transpose(0, 3, 1, 2, 4).reshape(b, h * 0 + l // l, 0, 0) if False else outs
        b, l, D = x.shape
        h, d = (NUM_HEADS, HEAD_DIM)
        q = (x @ Wq.T).reshape(b, l, h, d).transpose(0, 2, 1, 3)
        k = (x @ Wk.T).reshape(b, l, h, d).transpose(0, 2, 1, 3)
        v = (x @ Wv.T).reshape(b, l, h, d).transpose(0, 2, 1, 3)
        q = _pos_elu(q)
        k = _pos_elu(k)
        outs = _linear_attention(q, k, v)
        nc = l // CHUNK
        attn = outs.transpose(1, 0, 3, 2, 4).reshape(b, l, D)
        return attn @ Wo.T

    def _L3_ffn_ref(x, gate_w, gate_b, w1, b1, w2, b2, ws1, bs1, ws2, bs2):
        import jax, jax.numpy as jnp
        import numpy as np
        B, S, DIM = (4, 512, 256)
        E, K, HID = (8, 2, 1024)
        orig_shape = x.shape
        xf = x.reshape(-1, DIM)
        logits = xf @ gate_w + gate_b
        top_w, top_i = jax.lax.top_k(logits, K)
        gw = jax.nn.softmax(top_w, axis=-1).astype(xf.dtype)
        combine = (gw[:, :, None] * jax.nn.one_hot(top_i, E, dtype=xf.dtype)).sum(axis=1)
        out = jnp.zeros_like(xf)
        for e in range(E):
            h = jax.nn.gelu(xf @ w1[e] + b1[e], approximate=False)
            out = out + combine[:, e:e + 1] * (h @ w2[e] + b2[e])
        shared = jax.nn.gelu(xf @ ws1 + bs1, approximate=False) @ ws2 + bs2
        return (out + shared).reshape(orig_shape)
    x = x + _L0_xattn_ref(_layernorm(x, axis=-1), ctx_512, ctx_512, L0_xattn_Wq, L0_xattn_bq, L0_xattn_Wk, L0_xattn_bk, L0_xattn_Wv, L0_xattn_bv, L0_xattn_Wo, L0_xattn_bo)
    x = x + _L0_attn_ref(_layernorm(x, axis=-1), L0_attn_Wqt, L0_attn_Wkt, L0_attn_Wqs, L0_attn_Wks, L0_attn_Wv, L0_attn_Wout, L0_attn_bout, L0_attn_w_sigma)
    x = x + _L0_ffn_ref(_layernorm(x, axis=-1), L0_ffn_w_gate, L0_ffn_w_up, L0_ffn_w_down)
    x = x + _L1_xattn_ref(_layernorm(x, axis=-1), ctx_512, L1_xattn_Wq, L1_xattn_Wk, L1_xattn_Wv, L1_xattn_Wo, L1_xattn_bo)
    x = x + _L1_attn_ref(_layernorm(x, axis=-1), L1_attn_q_proj_weight, L1_attn_k_proj_weight, L1_attn_v_proj_weight, L1_attn_o_proj_weight)
    x = x + _L1_ffn_ref(_layernorm(x, axis=-1), L1_ffn_w1_w, L1_ffn_w1_s, L1_ffn_w2_w, L1_ffn_w2_s, L1_ffn_h1_w, L1_ffn_h1_s, L1_ffn_h2_w, L1_ffn_h2_s, L1_ffn_w3_w, L1_ffn_w3_s)
    x = x + _L2_xattn_ref(_layernorm(x, axis=-1), ctx_512, L2_xattn_Wq, L2_xattn_Wkv, L2_xattn_Wo)
    x = x + _L2_attn_ref(_layernorm(x, axis=-1), L2_attn_Wq, L2_attn_Wk, L2_attn_Wv, L2_attn_Wo, L2_attn_gamma, L2_attn_beta)
    x = x + _L2_ffn_ref(_layernorm(x, axis=-1), L2_ffn_ternary_weight, L2_ffn_bias, L2_ffn_act_scale)
    x = x + _L3_xattn_ref(_layernorm(x, axis=-1), ctx_512, itok_BxS2xS_0_7, L3_xattn_proj_in, L3_xattn_proj_out)
    x = x + _L3_attn_ref(_layernorm(x, axis=-1), L3_attn_Wq, L3_attn_Wk, L3_attn_Wv, L3_attn_Wo)
    x = x + _L3_ffn_ref(_layernorm(x, axis=-1), L3_ffn_gate_w, L3_ffn_gate_b, L3_ffn_w1, L3_ffn_b1, L3_ffn_w2, L3_ffn_b2, L3_ffn_ws1, L3_ffn_bs1, L3_ffn_ws2, L3_ffn_bs2)
    return x

_drawn_inputs = setup_inputs


def setup_inputs(seed=0):
    import zlib

    import numpy as np

    out = dict(_drawn_inputs(seed))
    spreads = {'L0_xattn_bq': (0.0, 0.1),
     'L0_xattn_bk': (0.0, 0.1),
     'L0_xattn_bv': (0.0, 0.1),
     'L0_xattn_bo': (0.0, 0.1),
     'L0_attn_bout': (0.0, 0.1),
     'L2_attn_gamma': (1.0, 0.2),
     'L2_attn_beta': (0.0, 0.1),
     'L3_ffn_gate_b': (0.0, 0.1),
     'L3_ffn_b1': (0.0, 0.1),
     'L3_ffn_b2': (0.0, 0.1),
     'L3_ffn_bs1': (0.0, 0.1),
     'L3_ffn_bs2': (0.0, 0.1)}
    factors = {}
    for name, (base, spread) in spreads.items():
        noise = np.random.default_rng([zlib.crc32(name.encode()), seed]).standard_normal(out[name].shape)
        drawn = base * np.exp(spread * noise) if base else spread * noise
        out[name] = jnp.asarray(drawn.astype(out[name].dtype))
    for name, factor in factors.items():
        out[name] = (out[name] * factor).astype(out[name].dtype)
    return out
```

```python
from contextlib import ExitStack

import numpy as np

import concourse.bass as bass
from concourse import mybir

ALU = mybir.AluOpType
ACT = mybir.ActivationFunctionType
AX = mybir.AxisListType
F32 = mybir.dt.float32
F16 = mybir.dt.float16
BF16 = mybir.dt.bfloat16
I32 = mybir.dt.int32
U32 = mybir.dt.uint32
RMAX = bass.bass_isa.ReduceOp.max

P = 128
DM = 256
KD = DM // P
HEADS = 16
KEYS = 12544
CD = 128
KT = KEYS // P
GROUPS = 4
HPG = HEADS // GROUPS
GW = HPG * P
ITERS = 7
TPI = KT // ITERS
KPI = KEYS // ITERS
PAIRS = TPI // 2
MCHUNK = 448
MCPI = KPI // MCHUNK
MUPI = MCPI * HPG
UW = CD + 1
P_SLOT = [0, 1, 2, 3, 0, 1, 2]
UNITS_AFTER = [3, 2, 2, 2, 2, 2, 3]
GHALF = MCHUNK // 2
VW = 17
V_CHUNKS = [(0, 8), (8, 14)]
EXPERTS = 8
GATE_STEPS = 2 * EXPERTS
HID = 1024
FT = HID // P
L0_HID = 768
XHID = 512
QBLOCK = 32
MAGIC = 12582912.0
MASKED = -1e30
FLT_MAX = 3.4028234663852886e38
PIECE = 2048
RING_A = 6
RING_B = 12
FREE_FROM = 24

XATTN = {"L0_xattn": 16, "L1_xattn": 64, "L2_xattn": 16}
SATTN = {"L0_attn": 16, "L1_attn": 16, "L2_attn": 64}
LAYERS = ["L0_xattn", "L0_attn", "L0_ffn", "L1_xattn", "L1_attn", "L1_ffn",
          "L2_xattn", "L2_attn", "L2_ffn", "L3_xattn", "L3_attn", "L3_ffn"]

PIECES = [
    ("L0_xattn", [("L0x_q", 0, P, 512), ("L0x_v", 512, P, 256), ("L0x_o", 768, P, 512)]),
    ("L0_xattn", [("L0x_kT", 0, 16, 2048)]),
    ("L0_attn", [("L0a_w", 0, P, 2048)]),
    ("L0_ffn", [("L0f_gate", 0, P, 1536)]),
    ("L0_ffn", [("L0f_up", 0, P, 1536)]),
    ("L0_ffn", [("L0f_down", 0, P, 1536)]),
    ("L1_xattn", [("L1x_q", 0, P, 2048)]),
    ("L1_xattn", [("L1x_kT", 0, 64, 2048)]),
    ("L1_xattn", [("L1x_v", 0, P, 1024)]),
    ("L1_xattn", [("L1x_o", 0, P, 2048)]),
    ("L1_attn", [("L1a_w", 0, P, 2048)]),
    ("L1_ffn", [("L1f_w1", 0, P, 2048)]),
    ("L1_ffn", [("L1f_w2", 0, P, 2048)]),
    *[("L1_ffn", [(f"L1f_h1_{i}", 0, P, 2048)]) for i in range(4)],
    *[("L1_ffn", [(f"L1f_h2_{i}", 0, P, 2048)]) for i in range(4)],
    ("L1_ffn", [("L1f_w3", 0, P, 2048)]),
    ("L2_xattn", [("L2x_q", 0, P, 512), ("L2x_v", 512, P, 256), ("L2x_o", 768, P, 512)]),
    ("L2_xattn", [("L2x_kT", 0, 16, 2048)]),
    *[("L2_attn", [(f"L2a_{n}", 0, P, 2048)]) for n in "qkvo"],
    ("L2_ffn", [("L2f_w", 0, P, 512)]),
    *[("L3_xattn", [(f"L3x_in{e}", 0, P, 1024), (f"L3x_out{e}", 1024, P, 1024)]) for e in range(EXPERTS)],
    ("L3_attn", [("L3a_w", 0, P, 2048)]),
    *[("L3_ffn", [(f"L3f_w{w}_{e}", 0, P, 2048)]) for e in range(EXPERTS + 1) for w in (1, 2)],
]

ROWS = {"bq": 256, "L0x_bo": 256, "bout": 256, "L1x_bo": 256, "L2f_bias": 256, "gate_b": 8}
ROW_AT = {n: sum(list(ROWS.values())[:i]) for i, n in enumerate(ROWS)}
COLS = {"w1_s": FT, "w2_s": FT, "h1_s": FT, "h2_s": FT, "b1": FT * (EXPERTS + 1), "w_gate": KD * EXPERTS}
COL_AT = {n: sum(list(COLS.values())[:i]) for i, n in enumerate(COLS)}
N_ROW, N_COL = sum(ROWS.values()), sum(COLS.values())
WIDE = ["w3_s", "gamma", "beta", "bv"]


def ceil_div(a, b):
    return -(-a // b)


def build_program(nc, dram, out, layers=LAYERS):
    ctx = ExitStack()
    with ctx:
        def sb(name, shape, dt=F32):
            return ctx.enter_context(nc.sbuf_tensor(name, shape, dt))

        sems = {}

        def sem(name):
            if name not in sems:
                sems[name] = ctx.enter_context(nc.semaphore(name))
            return sems[name]

        ctx_mem = sb("ctx_mem", [P, 2 * KEYS // 2 + KT * UW])
        ctxT_hi = ctx_mem[:, 0:KEYS // 2].bitcast(F16)
        ctxT_lo = ctx_mem[:, KEYS // 2:KEYS].bitcast(F16)
        ctx_flat = ctx_mem[:, KEYS:]
        ctx_rows = ctx_mem[:, KEYS:].rearrange("p (t c) -> p t c", c=UW)
        ring_a = sb("weight_ring", [P, RING_A, PIECE])
        work = sb("work", [P, 9216])
        gate_ctx = sb("gate_ctx", [P, 2, GHALF])
        gate_tok = sb("gate_tok", [P, 2, GHALF], I32)
        gate_part = sb("gate_part", [P, EXPERTS, 2 * GROUPS * ITERS])
        gate = sb("gate", [P, EXPERTS])
        wv_hi = sb("wv_hi", [P, DM], F16)
        wv_lo = sb("wv_lo", [P, DM], F16)
        x = sb("x", [P, DM])
        xn = sb("xn", [P, DM])
        y = sb("y", [P, DM])
        xnT = sb("xnT", [P, KD, P])
        ident = sb("ident", [P, P])
        causal = sb("causal", [P, P])
        keep_T = sb("keep_T", [P, P])
        ones_row = sb("ones_row", [1, P])
        ones_hpg = sb("ones_hpg", [HPG, P], BF16)
        iota8 = sb("iota8", [P, EXPERTS])
        minus_half = sb("minus_half", [P, 1])
        rows = sb("rows", [1, N_ROW])
        cols = sb("cols", [P, N_COL])
        wide = sb("wide", [P, len(WIDE), DM])
        b2 = sb("b2", [EXPERTS + 1, DM])
        bkT = sb("bkT", [16, HEADS])
        w_sigma = sb("w_sigma", [P, 1])
        act_scale = sb("act_scale", [P, 1])
        tiny = sb("tiny", [P, 160])
        stats, mv = tiny[:, 0:6], tiny[:, 6:8]
        veps, rstd = tiny[:, 8:9], tiny[:, 9:10]
        mx_group, neg_max = tiny[:, 10:14], tiny[:, 14:18]
        rden = tiny[:, 18:34]
        mx16, den16 = tiny[:, 34:50], tiny[:, 50:66]
        sig = tiny[:, 66:70]
        amax, qs, qinv = tiny[:, 70:75], tiny[:, 75:80], tiny[:, 80:85]
        amax_all = tiny[:, 85:90]
        top8 = tiny[:, 90:98]
        top_w = tiny[:, 98:102]
        combine = tiny[:, 102:102 + EXPERTS + 1]
        qscale = tiny[:, 112:114]
        key_bias_score = tiny[:, 116:132]
        logits = tiny[:, 132:140]
        pick = tiny[:, 140:148]
        top_i = sb("top_i", [P, 8], U32)
        top_if = sb("top_if", [P, 8])
        mx_part = sb("mx_part", [P, HPG, MCPI * ITERS])
        bias_rows = sb("bias_rows", [HPG, HPG, P], BF16)
        l0_quant = gate_part[:, :, :].rearrange("p e c -> p (e c)")[:, 0:3 * 1536 // QBLOCK]
        combine_T = work[0:EXPERTS + 1, 8192:8192 + P]
        ps = ctx.enter_context(nc.psum_tensor("ps", [P, 8, 512], F32))

        probs = work[:, 0:4096].rearrange("p (s c) -> p s c", s=4)
        u_norm = work[:, 4096:6144]
        x_qT = work[:, 4096:6144]
        q_hi = work[:, 6144:7168].bitcast(F16)
        q_lo = work[:, 7168:8192].bitcast(F16)
        u_T = work[:, 0:2048]
        gate_junk = work[:, 8192:8192 + 2 * GHALF].rearrange("p (s c) -> p s c", s=2)
        v_ring = work[:, 8192:8192 + TPI * HPG * VW].rearrange("p (t h c) -> p t h c", t=TPI, h=HPG)
        u_raw = work[:, 4096:4608].rearrange("p (g q) -> p g q", g=GROUPS)
        a_qT, a_kT = work[:, 0:2048], work[:, 2048:4096]
        a_v = work[:, 4096:5120]
        a_p, a_pT = work[:, 5120:7168], work[:, 7168:9216]
        o_sb = work[:, 2048:3072]
        o_T = work[:, 3072:4096]
        stage = work[:, 0:2 * KPI].rearrange("p (s c) -> p s c", s=2)

        def l0_wT(m):
            return work[:, m * 1536:(m + 1) * 1536].rearrange("p (k n) -> p k n", k=KD)

        l0_down = work[:, 3072:4608].rearrange("p (k n) -> p k n", k=6)
        l0_gate, l0_up = work[:, 4608:5376], work[:, 5376:6144]
        l0_h = work[:, 6144:6912]
        l0_hT = work[:, 6912:7680]
        l0_tmp = work[:, 7680:9216]
        f_a, f_b, f_c = work[:, 0:1024], work[:, 1024:2048], work[:, 2048:3072]
        f_d = work[:, 3072:4096]
        l2f_w = work[:, 0:512].rearrange("p (k n) -> p k n", k=KD)
        e_relu = work[:, 0:1024].rearrange("p (s n) -> p s n", s=2)
        m_h = work[:, 0:2048].rearrange("p (s n) -> p s n", s=2)
        scratch = work[:, 8192:9216]

        block = ctx.enter_context(nc.Block())

        x_layers = [n for n in layers if n in XATTN]
        v_layers = [n for n in x_layers if XATTN[n] == 16]
        u_layers = [n for n in x_layers if XATTN[n] == 64]
        tails = [n for n in layers if n in XATTN or n in SATTN or n == "L3_attn"]
        ln_at = {}
        for n in layers:
            ln_at[n] = len(ln_at)
            if n == "L2_attn":
                ln_at["L2_attn/post"] = len(ln_at)
        q_users = [n for n in layers if n in XATTN or n in SATTN or n == "L3_attn"]
        kv_users = [n for n in layers if n in SATTN or n == "L3_attn"]
        pieces = [p for p in PIECES if p[0] in layers]
        of_layer = {n: [i for i, p in enumerate(pieces) if p[0] == n] for n in layers}
        free_from = min([i for i, p in enumerate(pieces) if PIECES.index(p) >= FREE_FROM], default=len(pieces))
        has_gate = "L3_xattn" in layers
        gate_rider = "L1_xattn" if "L1_xattn" in layers else None

        slot_of, last_in, before = [], {}, []
        for i in range(len(pieces)):
            if i < free_from:
                s = i % RING_A
            else:
                k = i - free_from
                order = [(free_from + j) % RING_A for j in range(RING_A)] + [RING_A + j for j in range(RING_B)]
                s = order[k % len(order)]
            slot_of.append(s)
            before.append(last_in.get(s))
            last_in[s] = i
        arrivals, slot_count = [], {}
        for i, (_, parts) in enumerate(pieces):
            slot_count[slot_of[i]] = slot_count.get(slot_of[i], 0) + 16 * len(parts)
            arrivals.append(slot_count[slot_of[i]])

        def slot(i):
            s = slot_of[i]
            if s < RING_A:
                return ring_a[:, s, :]
            return ctx_mem[:, (s - RING_A) * PIECE:(s - RING_A + 1) * PIECE]

        def piece_arrived(eng, i):
            eng.wait_ge(sem(f"piece_in_slot{slot_of[i]}"), arrivals[i])

        def last_use(i):
            layer = pieces[i][0]
            k = i - of_layer[layer][0]
            if layer in tails:
                return sem("y_in_psum"), tails.index(layer) + 1
            if layer == "L1_ffn" and k < 2:
                return sem("swiglu_in_psum"), k + 1
            if layer == "L1_ffn" and k < 10:
                return sem("hidden_in_psum"), (k - 2) // 2 + 1
            if layer == "L3_xattn":
                return sem("expert_down"), k + 1
            if layer == "L3_ffn":
                return (sem("moe_down"), k // 2 + 1) if k % 2 else (sem("moe_up"), k + 2)
            return {"L0_ffn": sem("l0_ffn_y"), "L1_ffn": sem("l1_ffn_y"), "L2_ffn": sem("l2_ffn_y")}[layer], 1

        def v_count(name, g, i):
            return ((v_layers.index(name) * GROUPS + g) * ITERS + i) * len(V_CHUNKS)

        def counted(names, layer, per=1):
            return names.index(layer) * per

        @block.sync
        def _(sp):
            def load_piece(i):
                if before[i] is not None:
                    sp.wait_ge(*last_use(before[i]))
                if slot_of[i] >= RING_A and x_layers:
                    sp.wait_ge(sem("u_done"), GROUPS * len(x_layers))
                for name, at, r, c in pieces[i][1]:
                    dst = slot(i)[0:r, at:at + c]
                    if name == "L2f_w":
                        dst = dst.bitcast(I32)
                    sp.dma_start(dst, dram[name]).then_inc(sem(f"piece_in_slot{slot_of[i]}"), 16)

            sp.dma_start(x[:, :], dram["x"]).then_inc(sem("x_loaded"), 16)
            consts = [(rows[:, :], "rows"), (cols[:, :], "cols"), (b2[:, :], "b2"), (bkT[:, :], "bkT")]
            for dst, name in consts:
                sp.dma_start(dst, dram[name]).then_inc(sem("consts_loaded"), 16)
            for i, name in enumerate(WIDE):
                sp.dma_start(wide[:, i, :], dram[name].partition_broadcast(P)).then_inc(sem("consts_loaded"), 16)
            for dst, name in ((w_sigma, "w_sigma"), (act_scale, "act_scale")):
                sp.dma_start(dst[:, :], dram[name].partition_broadcast(P)).then_inc(sem("consts_loaded"), 16)
            first = min(2, len(pieces))
            for i in range(first):
                load_piece(i)
            if x_layers:
                for c in range(ITERS):
                    if c >= 2:
                        sp.wait_ge(sem("ctx_low_made"), c - 1)
                    sp.dma_start(stage[:, c % 2, :], dram["ctxT"][:, c * KPI:(c + 1) * KPI]).then_inc(
                        sem(f"ctxT_staged{c % 2}"), 16)
            done = min(RING_A, len(pieces))
            for i in range(first, done):
                load_piece(i)
            if u_layers:
                for c in range(ITERS):
                    sp.dma_start(ctx_rows[:, c * TPI:(c + 1) * TPI, 0:CD], dram["ctx_rows"][:, c * TPI:(c + 1) * TPI, :]
                                 ).then_inc(sem("ctx_rows_loaded"), 16)

            def stream_gate():
                with sp.Fori(0, GROUPS * ITERS) as u:
                    for s in range(2):
                        sp.wait_ge(sem("gate_sums"), u * GATE_STEPS + (s + 1) * EXPERTS)
                        for dst, name in ((gate_ctx, "ctxT"), (gate_tok, "tokT")):
                            sp.dma_start(dst[:, s, :], dram[name][:, bass.ds(u * MCHUNK + s * GHALF, GHALF)]
                                         ).then_inc(sem(f"gate_in_slot{s}"), 16)

            stop = min(of_layer[gate_rider][-1] + 3, len(pieces)) if gate_rider else done
            for i in range(done, stop):
                load_piece(i)
            if has_gate:
                stream_gate()
            for i in range(max(done, stop), len(pieces)):
                load_piece(i)
            sp.wait_ge(sem("x_final"), 1)
            sp.dma_start(out, x[:, :]).then_inc(sem("stored"), 16)
            sp.wait_ge(sem("stored"), 16)

        @block.gpsimd
        def _(pool):
            made = [0]

            def chained(ins):
                made[0] += 1
                ins.then_inc(sem("pool_step"), 1)
                pool.wait_ge(sem("pool_step"), made[0])

            chained(pool.memset(ident[:, :], 0.0))
            chained(pool.memset(causal[:, :], 0.0))
            chained(pool.memset(keep_T[:, :], 1.0))
            pool.memset(minus_half[:, :], -0.5).then_inc(sem("pool_consts"), 1)
            pool.memset(ones_row[:, :], 1.0).then_inc(sem("pool_consts"), 1)
            pool.memset(ones_hpg[:, :], 1.0).then_inc(sem("pool_consts"), 1)
            pool.iota(iota8[:, :], [[1, EXPERTS]], base=0, channel_multiplier=0,
                      allow_small_or_imprecise_dtypes=True).then_inc(sem("pool_consts"), 1)
            pool.affine_select(out=ident[:, :], in_=ident[:, :], compare_op=ALU.not_equal, fill=1.0, base=0,
                               pattern=[[-1, P]], channel_multiplier=1).then_inc(sem("pool_consts"), 1)
            pool.affine_select(out=causal[:, :], in_=causal[:, :], compare_op=ALU.is_ge, fill=MASKED, base=0,
                               pattern=[[-1, P]], channel_multiplier=1).then_inc(sem("pool_consts"), 1)
            pool.affine_select(out=keep_T[:, :], in_=keep_T[:, :], compare_op=ALU.is_ge, fill=0.0, base=0,
                               pattern=[[1, P]], channel_multiplier=-1).then_inc(sem("pool_consts"), 1)

            def layernorm(name):
                pool.wait_ge(sem("var_ready"), ln_at[name] + 1)
                eps = 1e-3 if name == "L2_attn/post" else 1e-5
                chained(pool.tensor_scalar(veps, mv[:, 1:2], eps, None, ALU.add))
                pool.tensor_tensor(rstd, veps, minus_half[:, :], ALU.pow).then_inc(sem("rstd_ready"), 1)

            pool.wait_ge(sem("pool_consts"), 7)
            for name in layers:
                layernorm(name)
                if name == "L2_attn":
                    layernorm("L2_attn/post")
                if name == "L0_ffn":
                    for z in range(5):
                        pool.wait_ge(sem("amax_ready"), z + 1)
                        pool.partition_all_reduce(amax_all[:, z:z + 1], amax[:, z:z + 1], P, RMAX
                                                  ).then_inc(sem("amax_all_ready"), 1)

        @block.tensor
        def _(pe):
            def transpose_xn(name):
                pe.wait_ge(sem("xn_ready"), layers.index(name) + 1)
                for k in range(KD):
                    last = pe.transpose(ps[:, 0, k * P:(k + 1) * P], xn[:, k * P:(k + 1) * P], ident[:, :])
                last.then_inc(sem("xnT_in_psum"), 1)
                pe.wait_ge(sem("xnT_ready"), layers.index(name) + 1)

            def heads_T(w, d, banks, done, bias=None):
                for h in range(HEADS):
                    dst = ps[0:d, banks[h // 4], (h % 4) * P:(h % 4 + 1) * P]
                    for k in range(KD):
                        last = pe.matmul(dst, w[:, k, h * d:(h + 1) * d], xnT[:, k, :], start=(k == 0),
                                         stop=(k == KD - 1 and bias is None))
                    if bias is not None:
                        last = pe.matmul(dst, bias[:, h * d:(h + 1) * d], ones_row[:, :], start=False, stop=True)
                    if h % 4 == 3:
                        last.then_inc(sem(done), 1)
                return last

            def output_tail(name, d, w_o, bias):
                t = tails.index(name)
                nk = HEADS * d // P
                pe.wait_ge(sem("o_ready"), t + 1)
                for k in range(nk):
                    last = pe.transpose(ps[:, 6 + k // 4, (k % 4) * P:(k % 4 + 1) * P],
                                        o_sb[:, k * P:(k + 1) * P], ident[:, :])
                last.then_inc(sem("oT_in_psum"), 1)
                pe.wait_ge(sem("oT_ready"), t + 1)
                if bias is not None:
                    pe.matmul(ps[:, 0, 0:DM], ones_row[:, :], bias, start=True, stop=False)
                for k in range(nk):
                    last = pe.matmul(ps[:, 0, 0:DM], o_T[:, k * P:(k + 1) * P], w_o[:, k, :],
                                     start=(k == 0 and bias is None), stop=(k == nk - 1))
                last.then_inc(sem("y_in_psum"), 1)

            def row(name):
                return rows[:, ROW_AT[name]:ROW_AT[name] + ROWS[name]]

            def cross_attention(name):
                d = XATTN[name]
                n = x_layers.index(name)
                q_base = counted(q_users, name, 4)
                pcs = of_layer[name]
                if len(pcs) == 2:
                    q_piece, k_piece = pcs
                    w = slot(q_piece)
                    w_q = w[:, 0:512].rearrange("p (k n) -> p k n", k=KD)
                    w_v, w_o = w[:, 512:768], w[:, 768:1280].rearrange("p (k n) -> p k n", k=2)
                else:
                    q_piece, k_piece, v_piece, o_piece = pcs
                    w_q = slot(q_piece).rearrange("p (k n) -> p k n", k=KD)
                    w_v, w_o = slot(v_piece)[:, 0:1024], slot(o_piece).rearrange("p (k n) -> p k n", k=8)
                first_x = name == "L0_xattn"
                transpose_xn(name)
                piece_arrived(pe, q_piece)
                last = heads_T(w_q, d, (2, 3, 4, 5), "qT_in_psum", row("bq") if first_x else None)
                piece_arrived(pe, k_piece)
                w_kT = slot(k_piece)[0:d, :]
                for h in range(HEADS):
                    if h % 4 == 0:
                        pe.wait_ge(sem("qT_ready"), q_base + h // 4 + 1)
                    last = pe.matmul(ps[:, (0, 1, 6, 7)[h // 4], (h % 4) * P:(h % 4 + 1) * P],
                                     w_kT[:, h * P:(h + 1) * P], x_qT[0:d, h * P:(h + 1) * P], start=True, stop=True)
                    if h % 4 == 3:
                        last.then_inc(sem("absorbed_in_psum"), 1)
                if first_x:
                    for h in range(HEADS):
                        last = pe.matmul(ps[:, 2, h:h + 1], x_qT[0:d, h * P:(h + 1) * P], bkT[:, h:h + 1],
                                         start=True, stop=True)
                    last.then_inc(sem("key_bias_in_psum"), 1)
                pe.wait_ge(sem("q_low_ready"), 4 * (n + 1))
                pe.wait_ge(sem("q_high_ready"), 4 * (n + 1))

                def max_unit(g, i, u, count):
                    c, hh = u // HPG, u % HPG
                    pe.wait_ge(sem("max_slots_free"), count + u + 1)
                    pe.matmul(ps[:, u % 2, 0:MCHUNK], q_hi[:, bass.ds(g * GW + hh * P, P)],
                              ctxT_hi[:, bass.ds(i * KPI + c * MCHUNK, MCHUNK)], start=True, stop=True
                              ).then_inc(sem("max_scores_ready"), 1)

                def bias_transpose(g):
                    pe.wait_ge(sem("neg_max_ready"), n * GROUPS + g + 1)
                    pe.transpose(ps[0:HPG, 0, 0:P], neg_max, ident[:, :]).then_inc(sem("neg_max_T"), 1)

                def score_pair(g, i, j, count):
                    back = {0: 1, 1: 3}.get(j, 2)
                    pe.wait_ge(sem("pair_exp_done"), count + j + 2 - back + 1)
                    for t in range(2):
                        dst = ps[:, 2 + 2 * (j % 2) + t, :]
                        key = i * KPI + (2 * j + t) * P
                        hi, lo = ctxT_hi[:, bass.ds(key, P)], ctxT_lo[:, bass.ds(key, P)]
                        qh, ql = q_hi[:, bass.ds(g * GW, GW)], q_lo[:, bass.ds(g * GW, GW)]
                        pe.matmul(dst, hi, qh, start=True, stop=False)
                        pe.matmul(dst, hi, ql, start=False, stop=False)
                        pe.matmul(dst, lo, qh, start=False, stop=False)
                        last = pe.matmul(dst, ones_hpg[:, :], bias_rows[:, :, :].rearrange("p a b -> p (a b)"),
                                         start=False, stop=True)
                    last.then_inc(sem("pair_scores_ready"), 1)

                def sum_pair(i, j, count):
                    pe.wait_ge(sem("pair_exp_done"), count + j + 3)
                    for t in range(2):
                        for hh in range(HPG):
                            last = pe.matmul(ps[:, 6 + hh // 2, (hh % 2) * UW:(hh % 2 + 1) * UW],
                                             probs[:, P_SLOT[j], t * GW + hh * P:t * GW + (hh + 1) * P],
                                             ctx_flat[:, bass.ds((i * TPI + 2 * j + t) * UW, UW)],
                                             start=False, stop=False, skip_group_check=True)
                    last.then_inc(sem("pair_summed"), 1)

                def project_values(g, i, c, vcount):
                    pe.wait_ge(sem("values_ready"), vcount + c + 1)
                    a, b = V_CHUNKS[c]
                    for t in range(a, b):
                        dst = ps[:, 7, (t - a) * 64:(t - a + 1) * 64]
                        key = (i * TPI + t) * P
                        hi, lo = ctxT_hi[:, bass.ds(key, P)], ctxT_lo[:, bass.ds(key, P)]
                        cols_g = bass.ds(g * HPG * 16, HPG * 16)
                        pe.matmul(dst, hi, wv_hi[:, cols_g], start=True, stop=False)
                        pe.matmul(dst, hi, wv_lo[:, cols_g], start=False, stop=False)
                        last = pe.matmul(dst, lo, wv_hi[:, cols_g], start=False, stop=True)
                    last.then_inc(sem("values_in_psum"), 1)

                def sum_pair_values(j, count, vcount):
                    pe.wait_ge(sem("pair_exp_done"), count + j + 3)
                    for c, (a, b) in enumerate(V_CHUNKS):
                        if a == 2 * j:
                            pe.wait_ge(sem("values_ready"), vcount + c + 2)
                    for t in range(2):
                        for hh in range(HPG):
                            last = pe.matmul(ps[32 * hh:32 * hh + VW, 6, 0:P], v_ring[:, 2 * j + t, hh, :],
                                             probs[:, P_SLOT[j], t * GW + hh * P:t * GW + (hh + 1) * P],
                                             start=False, stop=False, skip_group_check=True)
                    last.then_inc(sem("pair_summed"), 1)

                def keys_loop(sum_group, max_group):
                    with pe.Fori(0, ITERS) as i:
                        if max_group is not None:
                            mcount = (max_group * ITERS + i) * MUPI + n * GROUPS * ITERS * MUPI
                            if n == 0 and sum_group is None:
                                pe.wait_ge(sem("ctx_low_made"), i + 1)
                        if sum_group is None:
                            for u in range(MUPI):
                                max_unit(max_group, i, u, mcount)
                        else:
                            count = (sum_group * ITERS + i) * PAIRS + n * GROUPS * ITERS * PAIRS
                            u = 0
                            pe.wait_ge(sem("bias_rows_ready"), n * GROUPS + sum_group + 1)
                            pe.wait_ge(sem("u_cleared"), n * GROUPS + sum_group + 1)
                            vcount = v_count(name, sum_group, i) if d == 16 else 0

                            def sum_up(j):
                                if d == 16:
                                    sum_pair_values(j, count, vcount)
                                else:
                                    sum_pair(i, j, count)

                            if d == 16:
                                project_values(sum_group, i, 0, vcount)
                            for j in range(PAIRS):
                                score_pair(sum_group, i, j, count)
                                if j >= 1:
                                    sum_up(j - 1)
                                if d == 16 and j == 2:
                                    project_values(sum_group, i, 1, vcount)
                                if max_group is not None:
                                    for _ in range(UNITS_AFTER[j]):
                                        max_unit(max_group, i, u, mcount)
                                        u += 1
                            sum_up(PAIRS - 1)

                keys_loop(None, 0)
                if d == 64:
                    pe.wait_ge(sem("ctx_rows_loaded"), 16 * ITERS)
                pe.wait_ge(sem("ones_column"), n + 1)
                if d == 16:
                    pe.wait_ge(sem("wv_high_ready"), v_layers.index(name) + 1)
                    pe.wait_ge(sem("wv_low_ready"), v_layers.index(name) + 1)
                with pe.Fori(0, GROUPS - 1) as g:
                    bias_transpose(g)
                    keys_loop(g, g + 1)
                bias_transpose(GROUPS - 1)
                keys_loop(GROUPS - 1, None)

                if d == 16:
                    for g in range(GROUPS):
                        pe.wait_ge(sem("u_done"), n * GROUPS + g + 1)
                        last = pe.transpose(ps[:, 0, g * P:(g + 1) * P], u_raw[:, g, :], ident[:, :])
                    last.then_inc(sem("o_in_psum"), 1)
                else:
                    for b in range(4):
                        pe.wait_ge(sem("u_done"), n * GROUPS + b + 1)
                        for hh in range(4):
                            h = 4 * b + hh
                            last = pe.transpose(ps[:, 2 + b, hh * P:(hh + 1) * P], u_norm[:, h * P:(h + 1) * P],
                                                ident[:, :])
                        last.then_inc(sem("uT_in_psum"), 1)
                    piece_arrived(pe, v_piece)
                    for h in range(HEADS):
                        if h % 4 == 0:
                            pe.wait_ge(sem("uT_ready"), 4 * u_layers.index(name) + h // 4 + 1)
                        at = h * d
                        last = pe.matmul(ps[:, at // 512, at % 512:at % 512 + d], u_T[:, h * P:(h + 1) * P],
                                         w_v[:, at:at + d], start=True, stop=True)
                    last.then_inc(sem("o_in_psum"), 1)
                    piece_arrived(pe, o_piece)
                bias = {"L0_xattn": "L0x_bo", "L1_xattn": "L1x_bo"}.get(name)
                output_tail(name, d, w_o, row(bias) if bias else None)

            def self_attention(name):
                d = SATTN[name] if name in SATTN else 16
                q_base = counted(q_users, name, 4)
                k_base = counted(kv_users, name, 4)
                a = kv_users.index(name)
                pcs = of_layer[name]
                width = HEADS * d
                if len(pcs) == 1:
                    w = slot(pcs[0]).rearrange("p (m k n) -> p m k n", m=4, k=KD)
                    w_q, w_k, w_v, w_o = (w[:, m] for m in range(4))
                    p_q = p_k = p_v = p_o = pcs[0]
                else:
                    w_q, w_k, w_v = (slot(p).rearrange("p (k n) -> p k n", k=KD) for p in pcs[:3])
                    w_o = slot(pcs[3]).rearrange("p (k n) -> p k n", k=8)
                    p_q, p_k, p_v, p_o = pcs
                transpose_xn(name)
                piece_arrived(pe, p_q)
                heads_T(w_q, d, (2, 3, 4, 5), "qT_in_psum")
                piece_arrived(pe, p_k)
                heads_T(w_k, d, (0, 1, 6, 7), "kT_in_psum")
                piece_arrived(pe, p_v)
                linear = name == "L3_attn"
                if linear:
                    pe.wait_ge(sem("qT_ready_linear"), 4)
                else:
                    pe.wait_ge(sem("qT_ready"), q_base + 4)
                for c in range(ceil_div(width, 512)):
                    w_c = min(512, width)
                    for k in range(KD):
                        last = pe.matmul(ps[:, 2 + c, 0:w_c], xnT[:, k, :], w_v[:, k, c * 512:c * 512 + w_c],
                                         start=(k == 0), stop=(k == KD - 1))
                last.then_inc(sem("v_in_psum"), 1)
                if linear:
                    pe.wait_ge(sem("kT_ready_linear"), 4)
                else:
                    pe.wait_ge(sem("kT_ready"), k_base + 4)
                for h in range(HEADS):
                    qh, kh = a_qT[0:d, h * P:(h + 1) * P], a_kT[0:d, h * P:(h + 1) * P]
                    dst = ps[:, 4 + h // 4, (h % 4) * P:(h % 4 + 1) * P]
                    last = pe.matmul(dst, kh if linear else qh, qh if linear else kh, start=True, stop=True)
                    if h % 4 == 3:
                        last.then_inc(sem("scores_in_psum"), 1)
                if linear:
                    pe.wait_ge(sem("v_ready_linear"), 1)
                    pe.wait_ge(sem("masked_ready"), 4)
                    for h in range(HEADS):
                        last = pe.matmul(ps[:, 0, h * (d + 1):(h + 1) * (d + 1)], a_p[:, h * P:(h + 1) * P],
                                         a_v[:, h * (d + 1):(h + 1) * (d + 1)], start=True, stop=True)
                    last.then_inc(sem("o_in_psum"), 1)
                else:
                    pe.wait_ge(sem("v_ready"), a + 1)
                    for b in range(4):
                        pe.wait_ge(sem("p_ready"), 4 * a + b + 1)
                        for hh in range(4):
                            h = 4 * b + hh
                            last = pe.transpose(ps[:, b, hh * P:(hh + 1) * P], a_p[:, h * P:(h + 1) * P], ident[:, :])
                        last.then_inc(sem("pT_in_psum"), 1)
                    for h in range(HEADS):
                        if h % 4 == 0:
                            pe.wait_ge(sem("pT_ready"), 4 * a + h // 4 + 1)
                        at = h * d
                        last = pe.matmul(ps[:, 4 + at // 512, at % 512:at % 512 + d], a_pT[:, h * P:(h + 1) * P],
                                         a_v[:, at:at + d], start=True, stop=True)
                    last.then_inc(sem("o_in_psum"), 1)
                piece_arrived(pe, p_o)
                output_tail(name, d, w_o, row("bout") if name == "L0_attn" else None)

            def l0_ffn():
                g_piece, u_piece, d_piece = of_layer["L0_ffn"]
                if ln_at["L0_ffn"]:
                    pe.wait_ge(sem("x_updated"), ln_at["L0_ffn"])
                for m in range(2):
                    pe.wait_ge(sem("w_quantised"), m + 1)
                    wq = slot((g_piece, u_piece)[m])[:, 0:1536].rearrange("p (o i) -> p o i", o=6)
                    for k in range(KD):
                        for o in range(6):
                            at = o * P
                            last = pe.transpose(ps[:, 2 * (2 * m + k) % 8 + at // 512, at % 512:at % 512 + P],
                                                wq[:, o, k * P:(k + 1) * P], ident[:, :])
                        last.then_inc(sem("wT_in_psum"), 1)
                pe.wait_ge(sem("w_quantised"), 3)
                pe.wait_ge(sem("wT_copied"), 2)
                wq = slot(d_piece)[:, 0:1536].rearrange("p (o i) -> p o i", o=2)
                for k in range(6):
                    for o in range(2):
                        at = k * DM + o * P
                        last = pe.transpose(ps[:, at // 512, at % 512:at % 512 + P],
                                            wq[:, o, k * P:(k + 1) * P], ident[:, :])
                last.then_inc(sem("wT_in_psum"), 1)
                pe.wait_ge(sem("wT_copied"), 5)
                transpose_xn("L0_ffn")
                for m in range(2):
                    for at, c in ((0, 512), (512, 256)):
                        for k in range(KD):
                            last = pe.matmul(ps[:, 2 + 2 * m + at // 512, 0:c], xnT[:, k, :],
                                             l0_wT(m)[:, k, at:at + c], start=(k == 0), stop=(k == KD - 1))
                    last.then_inc(sem("gate_up_in_psum"), 1)
                pe.wait_ge(sem("l0_h_ready"), 1)
                for k in range(6):
                    last = pe.transpose(ps[:, 6 + k // 4, (k % 4) * P:(k % 4 + 1) * P], l0_h[:, k * P:(k + 1) * P],
                                        ident[:, :])
                last.then_inc(sem("l0_hT_in_psum"), 1)
                pe.wait_ge(sem("l0_hT_ready"), 1)
                for k in range(6):
                    last = pe.matmul(ps[:, 0, 0:DM], l0_hT[:, k * P:(k + 1) * P], l0_down[:, k, :], start=(k == 0),
                                     stop=(k == 5))
                last.then_inc(sem("l0_ffn_y"), 1)

            def l1_ffn():
                pcs = of_layer["L1_ffn"]
                transpose_xn("L1_ffn")
                for m in range(2):
                    piece_arrived(pe, pcs[m])
                    w = slot(pcs[m]).rearrange("p (k n) -> p k n", k=KD)
                    for f in range(FT):
                        for k in range(KD):
                            last = pe.matmul(ps[:, 2 + 2 * m + f // 4, (f % 4) * P:(f % 4 + 1) * P],
                                             w[:, k, f * P:(f + 1) * P], xnT[:, k, :], start=(k == 0), stop=(k == KD - 1))
                    last.then_inc(sem("swiglu_in_psum"), 1)
                pe.wait_ge(sem("swiglu_ready"), 1)
                src = f_a
                for m, (banks, dst) in enumerate((((6, 7), f_b), ((2, 3), f_a))):
                    if m:
                        pe.wait_ge(sem("gelu_ready"), FT)
                    for f in range(FT):
                        piece = pcs[2 + 4 * m + f // 2]
                        if f % 2 == 0:
                            piece_arrived(pe, piece)
                        w = slot(piece).rearrange("p (k n) -> p k n", k=FT)
                        for k in range(FT):
                            last = pe.matmul(ps[:, banks[f // 4], (f % 4) * P:(f % 4 + 1) * P],
                                             w[:, k, (f % 2) * P:(f % 2 + 1) * P], src[:, k * P:(k + 1) * P],
                                             start=(k == 0), stop=(k == FT - 1))
                        if f % 4 == 3:
                            last.then_inc(sem("hidden_in_psum"), 1)
                    src = dst
                pe.wait_ge(sem("gelu_ready"), 2 * FT)
                piece_arrived(pe, pcs[10])
                w = slot(pcs[10]).rearrange("p (k n) -> p k n", k=FT)
                for k in range(FT):
                    last = pe.matmul(ps[:, 0, 0:DM], f_a[:, k * P:(k + 1) * P], w[:, k, :], start=(k == 0),
                                     stop=(k == FT - 1))
                last.then_inc(sem("l1_ffn_y"), 1)

            def l2_ffn():
                transpose_xn("L2_ffn")
                pe.wait_ge(sem("l2f_w_ready"), 1)
                pe.matmul(ps[:, 0, 0:DM], ones_row[:, :], row("L2f_bias"), start=True, stop=False)
                for k in range(KD):
                    last = pe.matmul(ps[:, 0, 0:DM], xnT[:, k, :], l2f_w[:, k, :], start=False, stop=(k == KD - 1))
                last.then_inc(sem("l2_ffn_y"), 1)

            def l3_xattn():
                pcs = of_layer["L3_xattn"]
                transpose_xn("L3_xattn")
                nh = XHID // P

                def up(e):
                    piece_arrived(pe, pcs[e])
                    w = slot(pcs[e])[:, 0:1024].rearrange("p (k n) -> p k n", k=KD)
                    if e >= 2:
                        pe.wait_ge(sem("relu_ready"), e - 1)
                    for f in range(nh):
                        for k in range(KD):
                            last = pe.matmul(ps[:, 2 + e % 2, f * P:(f + 1) * P], w[:, k, f * P:(f + 1) * P],
                                             xnT[:, k, :], start=(k == 0), stop=(k == KD - 1))
                    last.then_inc(sem("expert_up"), 1)

                def down(e):
                    w = slot(pcs[e])[:, 1024:2048].rearrange("p (k n) -> p k n", k=nh)
                    pe.wait_ge(sem("relu_ready"), e + 1)
                    if e >= 2:
                        pe.wait_ge(sem("expert_added"), e - 1)
                    for k in range(nh):
                        last = pe.matmul(ps[:, 4 + e % 2, 0:DM], e_relu[:, e % 2, k * P:(k + 1) * P], w[:, k, :],
                                         start=(k == 0), stop=(k == nh - 1))
                    last.then_inc(sem("expert_down"), 1)

                for e in range(EXPERTS + 1):
                    if e < EXPERTS:
                        up(e)
                    if e >= 1:
                        down(e - 1)

            def l3_ffn():
                pcs = of_layer["L3_ffn"]
                transpose_xn("L3_ffn")
                w_gate = cols[:, COL_AT["w_gate"]:COL_AT["w_gate"] + KD * EXPERTS].rearrange("p (k n) -> p k n", k=KD)
                pe.matmul(ps[:, 1, 0:EXPERTS], ones_row[:, :], row("gate_b"), start=True, stop=False)
                for k in range(KD):
                    last = pe.matmul(ps[:, 1, 0:EXPERTS], xnT[:, k, :], w_gate[:, k, :], start=False, stop=(k == KD - 1))
                last.then_inc(sem("logits_in_psum"), 1)

                def up(e):
                    piece_arrived(pe, pcs[2 * e])
                    w = slot(pcs[2 * e]).rearrange("p (k n) -> p k n", k=KD)
                    for f in range(FT):
                        if e >= 2 and f % 4 == 0:
                            pe.wait_ge(sem("moe_gelu_ready"), FT * (e - 2) + f + 4)
                        for k in range(KD):
                            last = pe.matmul(ps[:, 2 + 2 * (e % 2) + f // 4, (f % 4) * P:(f % 4 + 1) * P],
                                             w[:, k, f * P:(f + 1) * P], xnT[:, k, :], start=(k == 0), stop=(k == KD - 1))
                        if f % 4 == 3:
                            last.then_inc(sem("moe_up"), 1)

                def down(e):
                    piece_arrived(pe, pcs[2 * e + 1])
                    w = slot(pcs[2 * e + 1]).rearrange("p (k n) -> p k n", k=FT)
                    if e >= 2:
                        pe.wait_ge(sem("moe_added"), e - 1)
                    for k in range(FT):
                        pe.wait_ge(sem("moe_gelu_ready"), FT * e + k + 1)
                        last = pe.matmul(ps[:, 6 + e % 2, 0:DM], m_h[:, e % 2, k * P:(k + 1) * P], w[:, k, :],
                                         start=(k == 0), stop=(k == FT - 1))
                    last.then_inc(sem("moe_down"), 1)

                for e in range(EXPERTS + 2):
                    if e < EXPERTS + 1:
                        up(e)
                    if e == 1:
                        pe.wait_ge(sem("combine_ready"), 1)
                        pe.transpose(ps[0:EXPERTS + 1, 1, 0:P], combine, ident[:, :]).then_inc(sem("combine_T_psum"), 1)
                        pe.wait_ge(sem("combine_T_ready"), 1)
                        pe.matmul(ps[:, 1, 0:DM], combine_T[:, :], b2[:, :], start=True, stop=True
                                  ).then_inc(sem("moe_bias"), 1)
                    if e >= 1:
                        down(e - 1)

            pe.wait_ge(sem("consts_loaded"), 16 * 10)
            pe.wait_ge(sem("pool_consts"), 7)
            if x_layers:
                pe.sem_inc(sem("pair_summed"), PAIRS)
            for name in layers:
                if name in XATTN:
                    cross_attention(name)
                elif name in SATTN or name == "L3_attn":
                    self_attention(name)
                else:
                    {"L0_ffn": l0_ffn, "L1_ffn": l1_ffn, "L2_ffn": l2_ffn, "L3_xattn": l3_xattn,
                     "L3_ffn": l3_ffn}[name]()

        @block.scalar
        def _(act):
            def heads_T_out(name, d, scale_of):
                q_base = counted(q_users, name, 4)
                dst = x_qT if name in XATTN else a_qT
                for b in range(4):
                    act.wait_ge(sem("qT_in_psum"), q_base + b + 1)
                    act.activation(dst[0:d, b * 512:(b + 1) * 512], ps[0:d, 2 + b, :], ACT.Identity, scale=scale_of(b)
                                   ).then_inc(sem("qT_ready"), 1)

            def cross_attention(name):
                d = XATTN[name]
                n = x_layers.index(name)
                heads_T_out(name, d, lambda b: d ** -0.5)
                for b in range(4):
                    act.wait_ge(sem("absorbed_in_psum"), 4 * n + b + 1)
                    act.activation(q_hi[:, b * 512:(b + 1) * 512], ps[:, (0, 1, 6, 7)[b], :], ACT.Copy
                                   ).then_inc(sem("q_high_ready"), 1)
                if d == 16:
                    piece = of_layer[name][0]
                    piece_arrived(act, piece)
                    act.activation(wv_hi[:, :], slot(piece)[:, 512:768], ACT.Copy).then_inc(sem("wv_high_ready"), 1)
                if n == 0:
                    act.sem_inc(sem("pair_exp_done"), 2)
                    for c in range(ITERS):
                        act.wait_ge(sem(f"ctxT_staged{c % 2}"), 16 * (c // 2 + 1))
                        act.activation(ctxT_hi[:, c * KPI:(c + 1) * KPI], stage[:, c % 2, :], ACT.Copy
                                       ).then_inc(sem("ctx_high_made"), 1)

                def exp_loop(g):
                    with act.Fori(0, ITERS) as i:
                        count = (g * ITERS + i) * PAIRS + n * GROUPS * ITERS * PAIRS
                        for j in range(PAIRS):
                            act.wait_ge(sem("pair_scores_ready"), count + j + 1)
                            back = {0: 3, 1: 3, 2: 3, 3: 7, 4: 4, 5: 4, 6: 4}[j]
                            act.wait_ge(sem("pair_summed"), count + j + 1 + PAIRS - back)
                            act.activation(probs[:, P_SLOT[j], :].rearrange("p (t c) -> p t c", t=2),
                                           ps[:, 2 + 2 * (j % 2):4 + 2 * (j % 2), :], ACT.Exp
                                           ).then_inc(sem("pair_exp_done"), 1)

                with act.Fori(0, GROUPS) as g:
                    exp_loop(g)
                for b in range(4 if d == 64 else 0):
                    act.wait_ge(sem("uT_in_psum"), 4 * u_layers.index(name) + b + 1)
                    act.activation(u_T[:, b * 512:(b + 1) * 512], ps[:, 2 + b, :], ACT.Copy
                                   ).then_inc(sem("uT_ready"), 1)

            def self_attention(name):
                d = SATTN[name] if name in SATTN else 16
                a = kv_users.index(name)
                if name == "L3_attn":
                    q_base = counted(q_users, name, 4)
                    k_base = counted(kv_users, name, 4)
                    for m, dst in enumerate((a_qT, a_kT)):
                        for b in range(4):
                            act.wait_ge(sem("neg_part_ready"), 4 * m + b + 1)
                            part = dst[0:d, b * 512:(b + 1) * 512]
                            act.activation(part, part, ACT.Exp).then_inc(sem("exp_part_ready"), 1)
                    return
                if name == "L0_attn":
                    act.wait_ge(sem("consts_loaded"), 16 * 10)
                    act.activation(sig[:, 0:1], w_sigma[:, :], ACT.Exp, scale=-1.0).then_inc(sem("sigma_exp"), 1)
                    act.wait_ge(sem("sigma_scale"), 1)
                heads_T_out(name, d, lambda b: sig[0:d, 3:4] if (name == "L0_attn" and b == 0) else d ** -0.5)
                act.wait_ge(sem("v_in_psum"), a + 1)
                width = HEADS * d
                if width <= 512:
                    act.activation(a_v[:, 0:width], ps[:, 2, 0:width], ACT.Copy).then_inc(sem("v_ready"), 1)
                else:
                    act.activation(a_v[:, 0:width].rearrange("p (b c) -> p b c", b=2), ps[:, 2:4, :], ACT.Copy
                                   ).then_inc(sem("v_ready"), 1)
                for b in range(4):
                    act.wait_ge(sem("shifted_ready"), 4 * a + b + 1)
                    part = a_p[:, b * 512:(b + 1) * 512]
                    act.activation(part, part, ACT.Exp).then_inc(sem("p_ready"), 1)
                for b in range(4):
                    act.wait_ge(sem("pT_in_psum"), 4 * a + b + 1)
                    act.activation(a_pT[:, b * 512:(b + 1) * 512], ps[:, b, :], ACT.Copy).then_inc(sem("pT_ready"), 1)

            def l0_ffn():
                act.wait_ge(sem("l0_gate_ready"), 1)
                act.activation(l0_tmp[:, 0:768], l0_gate, ACT.Exp, scale=-1.0).then_inc(sem("l0_exp_ready"), 1)

            def l1_ffn():
                s = cols[:, COL_AT["w1_s"]:COL_AT["w1_s"] + FT]
                act.wait_ge(sem("w1_scaled"), 1)
                act.activation(f_c, f_b, ACT.Exp, scale=-1.0).then_inc(sem("silu_exp"), 1)
                for m, (banks, dst, sc) in enumerate((((6, 7), f_b, "h1_s"), ((2, 3), f_a, "h2_s"))):
                    for f in range(FT):
                        if f % 4 == 0:
                            act.wait_ge(sem("hidden_in_psum"), 2 * m + f // 4 + 1)
                        act.activation(dst[:, f * P:(f + 1) * P], ps[:, banks[f // 4], (f % 4) * P:(f % 4 + 1) * P],
                                       ACT.Gelu, scale=cols[:, COL_AT[sc] + f:COL_AT[sc] + f + 1]
                                       ).then_inc(sem("gelu_ready"), 1)

            def l3_xattn():
                for e in range(EXPERTS):
                    act.wait_ge(sem("expert_up"), e + 1)
                    if e >= 2:
                        act.wait_ge(sem("expert_down"), e - 1)
                    act.activation(e_relu[:, e % 2, :], ps[:, 2 + e % 2, :], ACT.Relu).then_inc(sem("relu_ready"), 1)

            def l3_ffn():
                act.wait_ge(sem("top_diff"), 1)
                act.activation(top_w[:, 1:2], top_w[:, 0:1], ACT.Exp).then_inc(sem("top_exp"), 1)
                for e in range(EXPERTS + 1):
                    if e >= 2:
                        act.wait_ge(sem("moe_down"), e - 1)
                    for f in range(FT):
                        if f % 4 == 0:
                            act.wait_ge(sem("moe_up"), 2 * e + f // 4 + 1)
                        at = COL_AT["b1"] + e * FT + f
                        act.activation(m_h[:, e % 2, f * P:(f + 1) * P],
                                       ps[:, 2 + 2 * (e % 2) + f // 4, (f % 4) * P:(f % 4 + 1) * P], ACT.Gelu,
                                       bias=cols[:, at:at + 1]).then_inc(sem("moe_gelu_ready"), 1)

            for name in layers:
                if name in XATTN:
                    cross_attention(name)
                elif name in SATTN or name == "L3_attn":
                    self_attention(name)
                elif name != "L2_ffn":
                    {"L0_ffn": l0_ffn, "L1_ffn": l1_ffn, "L3_xattn": l3_xattn, "L3_ffn": l3_ffn}[name]()

        @block.vector
        def _(dve):
            steps = [0]
            updates = [0]

            def chained(ins):
                steps[0] += 1
                ins.then_inc(sem("dve_step"), 1)
                dve.wait_ge(sem("dve_step"), steps[0])

            def normalise(name, src):
                chained(dve.bn_stats(stats, src))
                dve.bn_aggr(mv, stats).then_inc(sem("var_ready"), 1)
                dve.wait_ge(sem("rstd_ready"), ln_at[name] + 1)
                dve.wait_ge(sem("var_ready"), ln_at[name] + 1)
                return dve.tensor_scalar(xn[:, :], src, mv[:, 0:1], rstd, ALU.subtract, ALU.mult)

            def transposed(name):
                dve.wait_ge(sem("xnT_in_psum"), layers.index(name) + 1)
                dve.tensor_copy(xnT[:, :, :],
                                ps[:, 0, 0:DM].rearrange("p (k n) -> p k n", k=KD)).then_inc(sem("xnT_ready"), 1)

            def ln(name):
                normalise(name, x[:, :]).then_inc(sem("xn_ready"), 1)
                transposed(name)

            def add_y(name_sem, value):
                dve.wait_ge(sem(name_sem), value)
                updates[0] += 1
                dve.tensor_tensor(x[:, :], x[:, :], ps[:, 0, 0:DM], ALU.add).then_inc(sem("x_updated"), 1)
                dve.wait_ge(sem("x_updated"), updates[0])

            def output_tail(name, d):
                t = tails.index(name)
                width = HEADS * d
                dve.wait_ge(sem("oT_in_psum"), t + 1)
                if width <= 512:
                    dve.tensor_copy(o_T[:, 0:width], ps[:, 6, 0:width]).then_inc(sem("oT_ready"), 1)
                else:
                    dve.tensor_copy(o_T.rearrange("p (b c) -> p b c", b=2), ps[:, 6:8, :]).then_inc(sem("oT_ready"), 1)
                if name == "L2_attn":
                    dve.wait_ge(sem("y_in_psum"), t + 1)
                    chained(dve.tensor_tensor(y[:, :], xn[:, :], ps[:, 0, 0:DM], ALU.add))
                    chained(normalise("L2_attn/post", y[:, :]))
                    chained(dve.tensor_tensor(y[:, :], xn[:, :], wide[:, 1, :], ALU.mult))
                    chained(dve.tensor_tensor(y[:, :], y[:, :], wide[:, 2, :], ALU.add))
                    chained(dve.tensor_tensor(x[:, :], x[:, :], y[:, :], ALU.add))
                else:
                    add_y("y_in_psum", t + 1)

            def gate_chunk(u):
                for s in range(2):
                    dve.wait_ge(sem(f"gate_in_slot{s}"), u * 32 + 32)
                    for e in range(EXPERTS):
                        k = s * EXPERTS + e
                        dve.wait_ge(sem("gate_sums"), u * GATE_STEPS + GATE_STEPS + k - 1)
                        dve.scalar_tensor_tensor(gate_junk[:, k % 2, :], gate_tok[:, s, :], float(e),
                                                 gate_ctx[:, s, :], ALU.is_equal, ALU.mult,
                                                 accum_out=gate_part[:, e, bass.ds(u * 2 + s, 1)]
                                                 ).then_inc(sem("gate_sums"), 1)

            def cross_attention(name):
                d = XATTN[name]
                n = x_layers.index(name)
                ln(name)
                for b in range(4):
                    dve.wait_ge(sem("q_high_ready"), 4 * n + b + 1)
                    part = slice(b * 512, (b + 1) * 512)
                    dve.tensor_tensor(q_lo[:, part], ps[:, (0, 1, 6, 7)[b], :], q_hi[:, part], ALU.subtract
                                      ).then_inc(sem("q_low_ready"), 1)
                first_x = name == "L0_xattn"
                if first_x:
                    dve.wait_ge(sem("key_bias_in_psum"), 1)
                    chained(dve.tensor_copy(key_bias_score, ps[:, 2, 0:HEADS]))
                if d == 16:
                    piece = of_layer[name][0]
                    dve.wait_ge(sem("wv_high_ready"), v_layers.index(name) + 1)
                    dve.tensor_tensor(wv_lo[:, :], slot(piece)[:, 512:768], wv_hi[:, :], ALU.subtract
                                      ).then_inc(sem("wv_low_ready"), 1)
                    dve.memset(v_ring[:, :, :, VW - 1:VW], 1.0).then_inc(sem("ones_column"), 1)
                    if name == v_layers[0]:
                        dve.sem_inc(sem("values_ready"), 1)
                else:
                    dve.memset(ctx_rows[:, :, CD:UW], 1.0).then_inc(sem("ones_column"), 1)
                if n == 0:
                    dve.sem_inc(sem("max_slots_free"), 2)
                    for c in range(ITERS):
                        dve.wait_ge(sem("ctx_high_made"), c + 1)
                        part = slice(c * KPI, (c + 1) * KPI)
                        dve.tensor_tensor(ctxT_lo[:, part], stage[:, c % 2, :], ctxT_hi[:, part], ALU.subtract
                                          ).then_inc(sem("ctx_low_made"), 1)

                def copy_values(c, vcount):
                    a, b = V_CHUNKS[c]
                    dve.wait_ge(sem("values_in_psum"), vcount + c + 1)
                    dve.tensor_copy(v_ring[:, a:b, :, 0:16].rearrange("p t h c -> p (t h) c"),
                                    ps[:, 7, 0:(b - a) * 64].rearrange("p (t c) -> p t c", c=16)
                                    ).then_inc(sem("values_ready"), 1)

                def keys_loop(sum_group, max_group):
                    if max_group is None and d != 16:
                        return
                    with dve.Fori(0, ITERS) as i:
                        if sum_group is not None and d == 16:
                            vcount = v_count(name, sum_group, i)
                            copy_values(0, vcount)
                        if max_group is not None:
                            count = (max_group * ITERS + i) * MUPI + n * GROUPS * ITERS * MUPI
                        for u in range(MUPI):
                            if sum_group is not None and d == 16 and u == UNITS_AFTER[0] + UNITS_AFTER[1]:
                                copy_values(1, vcount)
                            if max_group is None:
                                continue
                            c, hh = u // HPG, u % HPG
                            dve.wait_ge(sem("max_scores_ready"), count + u + 1)
                            dve.tensor_reduce(mx_part[:, hh, bass.ds(i * MCPI + c, 1)], ps[:, u % 2, 0:MCHUNK],
                                              AX.X, ALU.max).then_inc(sem("max_slots_free"), 1)
                        if name == gate_rider and has_gate:
                            gate_chunk(max_group * ITERS + i)

                def start_group(g):
                    dve.wait_ge(sem("max_slots_free"), (n * GROUPS + g + 1) * ITERS * MUPI + 2)
                    dve.tensor_reduce(mx_group, mx_part[:, :, :], AX.X, ALU.max).then_inc(sem("group_max"), 1)
                    dve.wait_ge(sem("group_max"), n * GROUPS + g + 1)
                    if first_x:
                        kb = key_bias_score[:, bass.ds(g * HPG, HPG)]
                        dve.tensor_tensor(mx_group, mx_group, kb, ALU.add).then_inc(sem("with_key_bias"), 1)
                        dve.wait_ge(sem("with_key_bias"), g + 1)
                        dve.tensor_tensor(neg_max, kb, mx_group, ALU.subtract).then_inc(sem("neg_max_ready"), 1)
                    else:
                        dve.tensor_scalar(neg_max, mx_group, -1.0, None, ALU.mult).then_inc(sem("neg_max_ready"), 1)
                    dve.memset(ps[:, 6, 0:P] if d == 16 else ps[:, 6:8, 0:2 * UW], 0.0).then_inc(sem("u_cleared"), 1)
                    dve.wait_ge(sem("neg_max_T"), n * GROUPS + g + 1)
                    dve.tensor_tensor(bias_rows[:, :, :],
                                      ps[0:HPG, 0, 0:P].unsqueeze(1).broadcast_to([HPG, HPG, P]),
                                      ident[0:HPG, 0:HPG].unsqueeze(2).broadcast_to([HPG, HPG, P]), ALU.mult
                                      ).then_inc(sem("bias_rows_ready"), 1)

                def end_group(g):
                    dve.wait_ge(sem("pair_summed"), (n * GROUPS + g + 1) * ITERS * PAIRS + PAIRS)
                    if d == 16:
                        dve.tensor_copy(u_raw[:, bass.ds(g, 1), :].rearrange("p g q -> p (g q)"), ps[:, 6, 0:P]
                                        ).then_inc(sem("u_done"), 1)
                        return
                    den = ps[:, 6:8, 0:2 * UW].rearrange("p b (h c) -> p b h c", c=UW)[:, :, :, CD]
                    dve.reciprocal(rden[:, 0:HPG].rearrange("p (b h) -> p b h", b=2), den).then_inc(sem("rden_ready"), 1)
                    dve.wait_ge(sem("rden_ready"), u_layers.index(name) * GROUPS + g + 1)
                    for hh in range(HPG):
                        last = dve.tensor_scalar(u_norm[:, bass.ds(g * GW + hh * P, P)],
                                                 ps[:, 6 + hh // 2, (hh % 2) * UW:(hh % 2) * UW + CD],
                                                 rden[:, hh:hh + 1], None, ALU.mult)
                    last.then_inc(sem("u_done"), 1)

                keys_loop(None, 0)
                if n == 0 and "L0_ffn" in layers:
                    quantise_weights()
                with dve.Fori(0, GROUPS - 1) as g:
                    start_group(g)
                    keys_loop(g, g + 1)
                    end_group(g)
                start_group(GROUPS - 1)
                keys_loop(GROUPS - 1, None)
                end_group(GROUPS - 1)
                dve.wait_ge(sem("o_in_psum"), tails.index(name) + 1)
                if d == 16:
                    sums = ps[:, 0, :].rearrange("p (h c) -> p h c", c=32)
                    ov = o_sb[:, 0:DM].rearrange("p (h c) -> p h c", c=16)
                    chained(dve.reciprocal(rden, sums[:, :, VW - 1]))
                    last = dve.tensor_tensor(ov, sums[:, :, 0:16], rden.unsqueeze(2).broadcast_to([P, HEADS, 16]),
                                             ALU.mult)
                    if first_x:
                        chained(last)
                        last = dve.tensor_tensor(o_sb[:, 0:DM], o_sb[:, 0:DM], wide[:, 3, :], ALU.add)
                    last.then_inc(sem("o_ready"), 1)
                else:
                    dve.tensor_copy(o_sb.rearrange("p (b c) -> p b c", b=2), ps[:, 0:2, :]).then_inc(sem("o_ready"), 1)
                output_tail(name, d)

            def softmax_attention(name):
                d = SATTN[name]
                a = kv_users.index(name)
                k_base = counted(kv_users, name, 4)
                ln(name)
                if name == "L0_attn":
                    dve.wait_ge(sem("sigma_exp"), 1)
                    chained(dve.tensor_scalar(sig[:, 1:2], sig[:, 0:1], 1.0, None, ALU.add))
                    chained(dve.reciprocal(sig[:, 2:3], sig[:, 1:2]))
                    dve.tensor_scalar(sig[:, 3:4], sig[:, 2:3], -(d ** -0.5), None, ALU.mult
                                      ).then_inc(sem("sigma_scale"), 1)
                for b in range(4):
                    dve.wait_ge(sem("kT_in_psum"), k_base + b + 1)
                    dve.tensor_copy(a_kT[0:d, b * 512:(b + 1) * 512], ps[0:d, (0, 1, 6, 7)[b], :]
                                    ).then_inc(sem("kT_ready"), 1)

                def by_head(ap):
                    return ap.rearrange("p (h k) -> p h k", h=4)

                for b in range(4):
                    dve.wait_ge(sem("scores_in_psum"), 4 * a + b + 1)
                    s = by_head(ps[:, 4 + b, :])
                    p_b = by_head(a_p[:, b * 512:(b + 1) * 512])
                    m_b = mx16[:, 4 * b:4 * b + 4]
                    if name != "L0_attn":
                        chained(dve.tensor_tensor(p_b, s, causal[:, :].unsqueeze(1).broadcast_to([P, 4, P]), ALU.add))
                        s = p_b
                    chained(dve.tensor_reduce(m_b, s, AX.X, ALU.max))
                    dve.tensor_tensor(p_b, s, m_b.unsqueeze(2).broadcast_to([P, 4, P]), ALU.subtract
                                      ).then_inc(sem("shifted_ready"), 1)
                for b in range(4):
                    dve.wait_ge(sem("p_ready"), 4 * a + b + 1)
                    chained(dve.tensor_reduce(den16[:, 4 * b:4 * b + 4], by_head(a_p[:, b * 512:(b + 1) * 512]),
                                              AX.X, ALU.add))
                chained(dve.reciprocal(rden, den16))
                dve.wait_ge(sem("o_in_psum"), tails.index(name) + 1)
                width = HEADS * d
                for c in range(ceil_div(width, 512)):
                    w_c = min(512, width)
                    hpc = w_c // d
                    last = dve.tensor_tensor(
                        o_sb[:, c * 512:c * 512 + w_c].rearrange("p (h e) -> p h e", h=hpc),
                        ps[:, 4 + c, 0:w_c].rearrange("p (h e) -> p h e", h=hpc),
                        rden[:, c * hpc:(c + 1) * hpc].unsqueeze(2).broadcast_to([P, hpc, d]), ALU.mult)
                last.then_inc(sem("o_ready"), 1)
                output_tail(name, d)

            def linear_attention():
                name, d = "L3_attn", 16
                a = kv_users.index(name)
                q_base, k_base = counted(q_users, name, 4), counted(kv_users, name, 4)
                ln(name)
                for m, (s_name, base, dst, banks) in enumerate(
                        (("qT_in_psum", q_base, a_qT, (2, 3, 4, 5)), ("kT_in_psum", k_base, a_kT, (0, 1, 6, 7)))):
                    for b in range(4):
                        dve.wait_ge(sem(s_name), base + b + 1)
                        dve.tensor_scalar(dst[0:d, b * 512:(b + 1) * 512], ps[0:d, banks[b], :], 0.0, None, ALU.min
                                          ).then_inc(sem("neg_part_ready"), 1)
                for m, (ready, dst, banks) in enumerate((("qT_ready", a_qT, (2, 3, 4, 5)),
                                                         ("kT_ready", a_kT, (0, 1, 6, 7)))):
                    for b in range(4):
                        dve.wait_ge(sem("exp_part_ready"), 4 * m + b + 1)
                        part = dst[0:d, b * 512:(b + 1) * 512]
                        dve.scalar_tensor_tensor(part, ps[0:d, banks[b], :], 0.0, part, ALU.max, ALU.add
                                                 ).then_inc(sem(ready + "_linear"), 1)
                v1 = a_v[:, 0:HEADS * (d + 1)].rearrange("p (h e) -> p h e", e=d + 1)
                dve.wait_ge(sem("v_in_psum"), a + 1)
                chained(dve.memset(v1[:, :, d:d + 1], 1.0))
                dve.tensor_copy(v1[:, :, 0:d], ps[:, 2, 0:HEADS * d].rearrange("p (h e) -> p h e", e=d)
                                ).then_inc(sem("v_ready_linear"), 1)
                for b in range(4):
                    dve.wait_ge(sem("scores_in_psum"), 4 * a + b + 1)
                    dve.tensor_tensor(a_p[:, b * 512:(b + 1) * 512].rearrange("p (h k) -> p h k", h=4),
                                      ps[:, 4 + b, :].rearrange("p (h k) -> p h k", h=4),
                                      keep_T[:, :].unsqueeze(1).broadcast_to([P, 4, P]), ALU.mult
                                      ).then_inc(sem("masked_ready"), 1)
                dve.wait_ge(sem("o_in_psum"), tails.index(name) + 1)
                o1 = ps[:, 0, 0:HEADS * (d + 1)].rearrange("p (h e) -> p h e", e=d + 1)
                chained(dve.reciprocal(rden, o1[:, :, d]))
                ov = o_sb[:, 0:HEADS * d].rearrange("p (h e) -> p h e", h=HEADS)
                chained(dve.tensor_tensor(ov, o1[:, :, 0:d], rden.unsqueeze(2).broadcast_to([P, HEADS, d]), ALU.mult))
                dve.tensor_scalar(o_sb[:, 0:HEADS * d], o_sb[:, 0:HEADS * d], 1e-12, None, ALU.add
                                  ).then_inc(sem("o_ready"), 1)
                output_tail(name, d)

            def quantise_weights():
                nb = 1536 // QBLOCK
                am, s_b, inv = (l0_quant[:, i * nb:(i + 1) * nb] for i in range(3))
                for i, piece in enumerate(of_layer["L0_ffn"]):
                    piece_arrived(dve, piece)
                    w = slot(piece)[:, 0:1536]
                    wb = w.rearrange("p (n b) -> p n b", b=QBLOCK)

                    def per_block(ap):
                        return ap.unsqueeze(2).broadcast_to([P, nb, QBLOCK])

                    chained(dve.tensor_reduce(am, wb, AX.X, ALU.max, apply_absolute_value=True))
                    chained(dve.tensor_scalar(s_b, am, 1.0 / 7.0, 1e-12, ALU.mult, ALU.max))
                    chained(dve.reciprocal(inv, s_b))
                    chained(dve.tensor_tensor(wb, wb, per_block(inv), ALU.mult))
                    chained(dve.tensor_scalar(w, w, MAGIC, MAGIC, ALU.add, ALU.subtract))
                    chained(dve.tensor_scalar(w, w, 7.0, -8.0, ALU.min, ALU.max))
                    dve.tensor_tensor(wb, wb, per_block(s_b), ALU.mult).then_inc(sem("w_quantised"), 1)
                    dve.wait_ge(sem("w_quantised"), i + 1)

            def quantise_16(t, z):
                dve.tensor_reduce(amax[:, z:z + 1], t, AX.X, ALU.max, apply_absolute_value=True
                                  ).then_inc(sem("amax_ready"), 1)
                dve.wait_ge(sem("amax_all_ready"), z + 1)
                s, inv = qs[:, z:z + 1], qinv[:, z:z + 1]
                chained(dve.tensor_scalar(s, amax_all[:, z:z + 1], 1.0 / 32767.0, 1e-12, ALU.mult, ALU.max))
                chained(dve.reciprocal(inv, s))
                chained(dve.tensor_scalar(t, t, inv, MAGIC, ALU.mult, ALU.add))
                chained(dve.tensor_scalar(t, t, MAGIC, 32767.0, ALU.subtract, ALU.min))
                return dve.tensor_scalar(t, t, -32768.0, s, ALU.max, ALU.mult)

            def l0_ffn():
                if not x_layers:
                    quantise_weights()
                chained(normalise("L0_ffn", x[:, :]))
                quantise_16(xn[:, :], 0).then_inc(sem("xn_ready"), 1)
                for i in range(4):
                    dve.wait_ge(sem("wT_in_psum"), i + 1)
                    m, k = i // 2, i % 2
                    b0 = 2 * i % 8
                    dve.tensor_copy(l0_wT(m)[:, k, 0:512], ps[:, b0, :])
                    dve.tensor_copy(l0_wT(m)[:, k, 512:768], ps[:, b0 + 1, 0:256]).then_inc(sem("wT_copied"), 1)
                dve.wait_ge(sem("wT_in_psum"), 5)
                dve.tensor_copy(work[:, 3072:4608].rearrange("p (b c) -> p b c", b=3), ps[:, 0:3, :]
                                ).then_inc(sem("wT_copied"), 1)
                transposed("L0_ffn")
                for m, t in enumerate((l0_gate, l0_up)):
                    dve.wait_ge(sem("gate_up_in_psum"), m + 1)
                    chained(dve.tensor_copy(t[:, 0:512], ps[:, 2 + 2 * m, :]))
                    chained(dve.tensor_copy(t[:, 512:768], ps[:, 3 + 2 * m, 0:256]))
                    if m == 0:
                        quantise_16(t, 1).then_inc(sem("l0_gate_ready"), 1)
                    else:
                        chained(quantise_16(t, 2))
                sg = l0_tmp[:, 0:768]
                s2 = l0_tmp[:, 768:1536]
                dve.wait_ge(sem("l0_exp_ready"), 1)
                chained(dve.tensor_scalar(sg, sg, 1.0, None, ALU.add))
                chained(dve.reciprocal(s2, sg))
                chained(dve.tensor_scalar(s2, s2, 65536.0, MAGIC, ALU.mult, ALU.add))
                chained(dve.tensor_scalar(s2, s2, MAGIC, 65535.0, ALU.subtract, ALU.min))
                chained(dve.tensor_scalar(s2, s2, 0.0, 1.0 / 65536.0, ALU.max, ALU.mult))
                chained(dve.tensor_tensor(l0_gate, l0_gate, s2, ALU.mult))
                chained(quantise_16(l0_gate, 3))
                chained(dve.tensor_tensor(l0_h, l0_gate, l0_up, ALU.mult))
                quantise_16(l0_h, 4).then_inc(sem("l0_h_ready"), 1)
                dve.wait_ge(sem("l0_hT_in_psum"), 1)
                dve.tensor_copy(l0_hT[:, 0:512], ps[:, 6, :])
                dve.tensor_copy(l0_hT[:, 512:768], ps[:, 7, 0:256]).then_inc(sem("l0_hT_ready"), 1)
                add_y("l0_ffn_y", 1)

            def l1_ffn():
                ln("L1_ffn")

                def scaled(dst, banks, s_name):
                    s = cols[:, COL_AT[s_name]:COL_AT[s_name] + FT].rearrange("p (b f) -> p b f", b=2)
                    for b in range(2):
                        last = dve.tensor_tensor(dst[:, b * 512:(b + 1) * 512].rearrange("p (f t) -> p f t", f=4),
                                                 ps[:, banks[b], :].rearrange("p (f t) -> p f t", f=4),
                                                 s[:, b, :].unsqueeze(2).broadcast_to([P, 4, P]), ALU.mult)
                    return last

                dve.wait_ge(sem("consts_loaded"), 16 * 10)
                dve.wait_ge(sem("swiglu_in_psum"), 1)
                scaled(f_b, (2, 3), "w1_s").then_inc(sem("w1_scaled"), 1)
                dve.wait_ge(sem("swiglu_in_psum"), 2)
                chained(scaled(f_a, (4, 5), "w2_s"))
                chained(dve.tensor_tensor(f_a, f_a, f_b, ALU.mult))
                dve.wait_ge(sem("silu_exp"), 1)
                chained(dve.tensor_scalar(f_c, f_c, 1.0, None, ALU.add))
                chained(dve.reciprocal(f_d, f_c))
                dve.tensor_tensor(f_a, f_a, f_d, ALU.mult).then_inc(sem("swiglu_ready"), 1)
                dve.wait_ge(sem("l1_ffn_y"), 1)
                chained(dve.tensor_tensor(y[:, :], ps[:, 0, 0:DM], wide[:, 0, :], ALU.mult))
                chained(dve.tensor_tensor(x[:, :], x[:, :], y[:, :], ALU.add))

            def l2_ffn():
                piece, = of_layer["L2_ffn"]
                piece_arrived(dve, piece)
                chained(dve.tensor_copy(work[:, 0:512], slot(piece)[:, 0:512].bitcast(I32)))
                dve.tensor_scalar(work[:, 0:512], work[:, 0:512], -1.0, None, ALU.add).then_inc(sem("l2f_w_ready"), 1)
                dve.wait_ge(sem("consts_loaded"), 16 * 10)
                s, inv = qscale[:, 0:1], qscale[:, 1:2]
                chained(dve.tensor_scalar(s, act_scale[:, :], 1e-5, None, ALU.max))
                chained(dve.reciprocal(inv, s))
                chained(normalise("L2_ffn", x[:, :]))
                t = xn[:, :]
                pos, neg = scratch[:, 0:DM], scratch[:, DM:2 * DM]
                big, tmp = scratch[:, 2 * DM:3 * DM], scratch[:, 3 * DM:4 * DM]
                chained(dve.tensor_scalar(t, t, inv, MAGIC, ALU.mult, ALU.add))
                chained(dve.tensor_scalar(t, t, MAGIC, 127.0, ALU.subtract, ALU.min))
                chained(dve.tensor_scalar(t, t, -127.0, s, ALU.max, ALU.mult))
                chained(dve.tensor_scalar(pos, t, 0.0, None, ALU.max))
                chained(dve.tensor_scalar(neg, t, 0.0, None, ALU.min))
                for part, over, clip, limit, value in ((pos, ALU.is_gt, ALU.min, FLT_MAX, 1e4),
                                                       (neg, ALU.is_lt, ALU.max, -FLT_MAX, -1e4)):
                    within = ALU.is_le if part is pos else ALU.is_ge
                    chained(dve.tensor_scalar(big, part, limit, value, over, ALU.mult))
                    chained(dve.tensor_scalar(tmp, part, limit, None, clip))
                    chained(dve.scalar_tensor_tensor(part, part, limit, tmp, within, ALU.mult))
                    chained(dve.tensor_tensor(part, part, big, ALU.add))
                dve.tensor_tensor(t, pos, neg, ALU.add).then_inc(sem("xn_ready"), 1)
                transposed("L2_ffn")
                add_y("l2_ffn_y", 1)

            def l3_xattn():
                if gate_rider is None:
                    with dve.Fori(0, GROUPS * ITERS) as u:
                        gate_chunk(u)
                dve.wait_ge(sem("gate_sums"), (1 + GROUPS * ITERS) * GATE_STEPS)
                chained(dve.tensor_reduce(gate[:, :], gate_part[:, :, :], AX.X, ALU.add))
                ln("L3_xattn")
                for e in range(EXPERTS):
                    dve.wait_ge(sem("expert_down"), e + 1)
                    last = dve.scalar_tensor_tensor(x[:, :], ps[:, 4 + e % 2, 0:DM], gate[:, e:e + 1], x[:, :],
                                                    ALU.mult, ALU.add)
                    last.then_inc(sem("expert_added"), 1)
                    dve.wait_ge(sem("expert_added"), e + 1)

            def l3_ffn():
                ln("L3_ffn")
                dve.wait_ge(sem("logits_in_psum"), 1)
                chained(dve.tensor_copy(logits, ps[:, 1, 0:EXPERTS]))
                chained(dve.max(top8, logits))
                chained(dve.max_index(top_i[:, :], top8, logits))
                chained(dve.tensor_copy(top_if[:, :], top_i[:, :]))
                dve.tensor_tensor(top_w[:, 0:1], top8[:, 1:2], top8[:, 0:1], ALU.subtract).then_inc(sem("top_diff"), 1)
                dve.wait_ge(sem("top_exp"), 1)
                chained(dve.tensor_scalar(top_w[:, 2:3], top_w[:, 1:2], 1.0, None, ALU.add))
                chained(dve.reciprocal(top_w[:, 2:3], top_w[:, 2:3]))
                chained(dve.tensor_tensor(top_w[:, 3:4], top_w[:, 1:2], top_w[:, 2:3], ALU.mult))
                chained(dve.memset(combine[:, EXPERTS:EXPERTS + 1], 1.0))
                chained(dve.tensor_scalar(pick, iota8[:, :], top_if[:, 1:2], top_w[:, 3:4], ALU.is_equal, ALU.mult))
                chained(dve.tensor_scalar(combine[:, 0:EXPERTS], iota8[:, :], top_if[:, 0:1], top_w[:, 2:3],
                                          ALU.is_equal, ALU.mult))
                dve.tensor_tensor(combine[:, 0:EXPERTS], combine[:, 0:EXPERTS], pick, ALU.add
                                  ).then_inc(sem("combine_ready"), 1)
                dve.wait_ge(sem("combine_T_psum"), 1)
                dve.tensor_copy(combine_T[:, :], ps[0:EXPERTS + 1, 1, 0:P]).then_inc(sem("combine_T_ready"), 1)
                dve.wait_ge(sem("moe_bias"), 1)
                chained(dve.tensor_tensor(x[:, :], x[:, :], ps[:, 1, 0:DM], ALU.add))
                for e in range(EXPERTS + 1):
                    dve.wait_ge(sem("moe_down"), e + 1)
                    dve.scalar_tensor_tensor(x[:, :], ps[:, 6 + e % 2, 0:DM], combine[:, e:e + 1], x[:, :],
                                             ALU.mult, ALU.add).then_inc(sem("moe_added"), 1)
                    dve.wait_ge(sem("moe_added"), e + 1)

            dve.wait_ge(sem("x_loaded"), 16)
            dve.wait_ge(sem("pool_consts"), 7)
            dve.wait_ge(sem("consts_loaded"), 16 * 10)
            if has_gate:
                dve.sem_inc(sem("gate_sums"), GATE_STEPS)
            for name in layers:
                if name in XATTN:
                    cross_attention(name)
                elif name in SATTN:
                    softmax_attention(name)
                else:
                    {"L0_ffn": l0_ffn, "L1_ffn": l1_ffn, "L2_ffn": l2_ffn, "L3_xattn": l3_xattn,
                     "L3_attn": linear_attention, "L3_ffn": l3_ffn}[name]()
            dve.drain().then_inc(sem("x_final"), 1)


def lay_out(a):
    a = {k: np.asarray(v) for k, v in a.items()}

    def tiles(w):
        k = w.shape[0] // P
        return np.ascontiguousarray(w.reshape(k, P, -1).transpose(1, 0, 2).reshape(P, -1))

    def per_head_T(w, d):
        return np.ascontiguousarray(w.reshape(CD, HEADS, d).transpose(2, 1, 0).reshape(d, HEADS * CD))

    def out_in(w):
        return np.ascontiguousarray(w.reshape(-1, P, w.shape[1]).transpose(1, 0, 2).reshape(P, -1))

    ctx = a["ctx_512"][0]
    d = {
        "x": a["x"][0],
        "ctxT": ctx.T,
        "ctx_rows": ctx.reshape(KT, P, CD).transpose(1, 0, 2),
        "tokT": a["itok_BxS2xS_0_7"][0].T,
        "L0x_q": tiles(a["L0_xattn_Wq"]), "L0x_v": a["L0_xattn_Wv"], "L0x_o": tiles(a["L0_xattn_Wo"]),
        "L0x_kT": per_head_T(a["L0_xattn_Wk"], 16), "bkT": a["L0_xattn_bk"].reshape(HEADS, 16).T,
        "L0a_w": np.concatenate([
            tiles(np.concatenate([a["L0_attn_Wqt"], a["L0_attn_Wqs"]], 1)),
            tiles(np.concatenate([a["L0_attn_Wkt"], a["L0_attn_Wks"]], 1)),
            tiles(a["L0_attn_Wv"]), tiles(a["L0_attn_Wout"])], 1),
        "L0f_gate": out_in(a["L0_ffn_w_gate"]), "L0f_up": out_in(a["L0_ffn_w_up"]),
        "L0f_down": out_in(a["L0_ffn_w_down"]),
        "L1x_q": tiles(a["L1_xattn_Wq"]), "L1x_kT": per_head_T(a["L1_xattn_Wk"], 64),
        "L1x_v": a["L1_xattn_Wv"], "L1x_o": tiles(a["L1_xattn_Wo"]),
        "L1a_w": np.concatenate([tiles(a[f"L1_attn_{n}_proj_weight"].T) for n in "qkvo"], 1),
        "L1f_w1": tiles(a["L1_ffn_w1_w"].T), "L1f_w2": tiles(a["L1_ffn_w2_w"].T), "L1f_w3": tiles(a["L1_ffn_w3_w"].T),
        "L2x_q": tiles(a["L2_xattn_Wq"].T), "L2x_o": tiles(a["L2_xattn_Wo"].T),
        "L2x_kT": per_head_T(a["L2_xattn_Wkv"][:DM].T, 16), "L2x_v": a["L2_xattn_Wkv"][DM:].T,
        "L2f_w": tiles(a["L2_ffn_ternary_weight"].T),
        "L3a_w": np.concatenate([tiles(a[f"L3_attn_W{n}"].T) for n in "qkvo"], 1),
        "w3_s": a["L1_ffn_w3_s"], "gamma": a["L2_attn_gamma"], "beta": a["L2_attn_beta"],
        "bv": a["L0_xattn_bv"],
        "w_sigma": a["L0_attn_w_sigma"].reshape(1), "act_scale": a["L2_ffn_act_scale"].reshape(1),
        "b2": np.concatenate([a["L3_ffn_b2"], a["L3_ffn_bs2"][None]], 0),
        "rows": np.concatenate([a["L0_xattn_bq"], a["L0_xattn_bo"], a["L0_attn_bout"],
                                a["L1_xattn_bo"], a["L2_ffn_bias"], a["L3_ffn_gate_b"]])[None],
        "cols": np.concatenate([
            *[a[f"L1_ffn_{n}"].reshape(FT, P).T for n in ("w1_s", "w2_s", "h1_s", "h2_s")],
            a["L3_ffn_b1"].reshape(EXPERTS * FT, P).T, a["L3_ffn_bs1"].reshape(FT, P).T,
            tiles(a["L3_ffn_gate_w"])], 1),
    }
    for m in ("h1", "h2"):
        w = a[f"L1_ffn_{m}_w"].T
        for i in range(4):
            d[f"L1f_{m}_{i}"] = tiles(w[:, i * 256:(i + 1) * 256])
    for n in "qkv":
        d[f"L2a_{n}"] = tiles(a[f"L2_attn_W{n}"].transpose(1, 0, 2).reshape(DM, -1))
    d["L2a_o"] = tiles(a["L2_attn_Wo"])
    for e in range(EXPERTS):
        d[f"L3x_in{e}"] = tiles(a["L3_xattn_proj_in"][e].T)
        d[f"L3x_out{e}"] = tiles(a["L3_xattn_proj_out"][e].T)
        d[f"L3f_w1_{e}"], d[f"L3f_w2_{e}"] = tiles(a["L3_ffn_w1"][e]), tiles(a["L3_ffn_w2"][e])
    d[f"L3f_w1_{EXPERTS}"], d[f"L3f_w2_{EXPERTS}"] = tiles(a["L3_ffn_ws1"]), tiles(a["L3_ffn_ws2"])
    return {k: np.ascontiguousarray(v) for k, v in d.items()}


def kernel(**inputs):
    import concourse.bacc as bacc
    from concourse.bass_utils import run_bass_kernel_spmd

    arrays = {f"in_{k}": v for k, v in lay_out(inputs).items()}
    nc = bacc.Bacc("TRN2", target_bir_lowering=False, num_devices=1)
    dram = {k[3:]: nc.dram_tensor(k, v.shape, mybir.dt.from_np(v.dtype), kind="ExternalInput").ap()
            for k, v in arrays.items()}
    out = nc.dram_tensor("out", (P, DM), F32, kind="ExternalOutput").ap()
    build_program(nc, dram, out)
    result = run_bass_kernel_spmd(nc, [arrays], core_ids=[0])
    return result.results[0]["out"].reshape(1, P, DM)
```

```python
from contextlib import ExitStack

import numpy as np

import concourse.bass as bass
from concourse import mybir

ALU = mybir.AluOpType
ACT = mybir.ActivationFunctionType
AX = mybir.AxisListType
F32 = mybir.dt.float32
F16 = mybir.dt.float16
BF16 = mybir.dt.bfloat16
I32 = mybir.dt.int32
U32 = mybir.dt.uint32
RMAX = bass.bass_isa.ReduceOp.max

P = 128
DM = 256
KD = DM // P
HEADS = 16
KEYS = 12544
CD = 128
KT = KEYS // P
GROUPS = 4
HPG = HEADS // GROUPS
GW = HPG * P
ITERS = 7
TPI = KT // ITERS
KPI = KEYS // ITERS
MCHUNK = 448
MCPI = KPI // MCHUNK
MUPI = MCPI * HPG
UW = CD + 1
STEPS = {16: [1] * TPI, 64: [2, 2, 2, 1, 2, 2, 2, 1]}
P_SLOTS = {16: 8, 64: 4}
CREDIT = 8
STACKS = HEADS // 2
STACK_W = 3 * 32
STACK_ROWS = STACK_W + HPG
BIAS_UNIT = 64.0
BUILDS = [(c, s) for c in range(MCPI) for s in range(2)]
BUILD_AFTER = {0: (1, 1), 2: (2, 0), 3: (2, 1), 5: (3, 0), 6: (3, 1)}
VALUES_AFTER = {1: 1, 4: 2}
NO_UNIT_AFTER = 2
GHALF = MCHUNK // 2
VW = 17
V_CHUNKS = [(0, 4), (4, 9), (9, 14)]
EXPERTS = 8
GATE_STEPS = 2 * EXPERTS
HID = 1024
FT = HID // P
L0_HID = 768
XHID = 512
QBLOCK = 32
MAGIC = 12582912.0
MASKED = -1e30
FLT_MAX = 3.4028234663852886e38
PIECE = 2048
RING_A = 6
RING_B = 12
FREE_FROM = 24

XATTN = {"L0_xattn": 16, "L1_xattn": 64, "L2_xattn": 16}
SATTN = {"L0_attn": 16, "L1_attn": 16, "L2_attn": 64}
LAYERS = ["L0_xattn", "L0_attn", "L0_ffn", "L1_xattn", "L1_attn", "L1_ffn",
          "L2_xattn", "L2_attn", "L2_ffn", "L3_xattn", "L3_attn", "L3_ffn"]

PIECES = [
    ("L0_xattn", [("L0x_q", 0, P, 512), ("L0x_v", 512, P, 256), ("L0x_o", 768, P, 512),
                  ("L0x_k", 1280, P, 256)]),
    ("L0_xattn", [("L0x_kT", 0, 16, 2048)]),
    ("L0_attn", [("L0a_w", 0, P, 2048)]),
    ("L0_ffn", [("L0f_gate", 0, P, 1536)]),
    ("L0_ffn", [("L0f_up", 0, P, 1536)]),
    ("L0_ffn", [("L0f_down", 0, P, 1536)]),
    ("L1_xattn", [("L1x_q", 0, P, 2048)]),
    ("L1_xattn", [("L1x_kT", 0, 64, 2048)]),
    ("L1_xattn", [("L1x_v", 0, P, 1024)]),
    ("L1_xattn", [("L1x_o", 0, P, 2048)]),
    ("L1_attn", [("L1a_w", 0, P, 2048)]),
    ("L1_ffn", [("L1f_w1", 0, P, 2048)]),
    ("L1_ffn", [("L1f_w2", 0, P, 2048)]),
    *[("L1_ffn", [(f"L1f_h1_{i}", 0, P, 2048)]) for i in range(4)],
    *[("L1_ffn", [(f"L1f_h2_{i}", 0, P, 2048)]) for i in range(4)],
    ("L1_ffn", [("L1f_w3", 0, P, 2048)]),
    ("L2_xattn", [("L2x_q", 0, P, 512), ("L2x_v", 512, P, 256), ("L2x_o", 768, P, 512),
                  ("L2x_k", 1280, P, 256)]),
    ("L2_xattn", [("L2x_kT", 0, 16, 2048)]),
    *[("L2_attn", [(f"L2a_{n}", 0, P, 2048)]) for n in "qkvo"],
    ("L2_ffn", [("L2f_w", 0, P, 512)]),
    *[("L3_xattn", [(f"L3x_in{e}", 0, P, 1024), (f"L3x_out{e}", 1024, P, 1024)]) for e in range(EXPERTS)],
    ("L3_attn", [("L3a_w", 0, P, 2048)]),
    *[("L3_ffn", [(f"L3f_w{w}_{e}", 0, P, 2048)]) for e in range(EXPERTS + 1) for w in (1, 2)],
]

ROWS = {"bq": 256, "L0x_bo": 256, "bout": 256, "L1x_bo": 256, "L2f_bias": 256, "gate_b": 8}
ROW_AT = {n: sum(list(ROWS.values())[:i]) for i, n in enumerate(ROWS)}
COLS = {"w1_s": FT, "w2_s": FT, "h1_s": FT, "h2_s": FT, "b1": FT * (EXPERTS + 1), "w_gate": KD * EXPERTS, "head_half": 2}
COL_AT = {n: sum(list(COLS.values())[:i]) for i, n in enumerate(COLS)}
N_ROW, N_COL = sum(ROWS.values()), sum(COLS.values())
WIDE = ["w3_s", "gamma", "beta", "bv"]


def ceil_div(a, b):
    return -(-a // b)


def build_program(nc, dram, out, layers=LAYERS):
    ctx = ExitStack()
    with ctx:
        def sb(name, shape, dt=F32):
            return ctx.enter_context(nc.sbuf_tensor(name, shape, dt))

        sems = {}

        def sem(name):
            if name not in sems:
                sems[name] = ctx.enter_context(nc.semaphore(name))
            return sems[name]

        ctx_mem = sb("ctx_mem", [P, 2 * KEYS // 2 + KT * UW])
        ctxT_hi = ctx_mem[:, 0:KEYS // 2].bitcast(F16)
        ctxT_lo = ctx_mem[:, KEYS // 2:KEYS].bitcast(F16)
        ctx_flat = ctx_mem[:, KEYS:]
        ctx_rows = ctx_mem[:, KEYS:].rearrange("p (t c) -> p t c", c=UW)
        ring_a = sb("weight_ring", [P, RING_A, PIECE])
        work = sb("work", [P, 9216])
        gate_ctx = sb("gate_ctx", [P, 2, GHALF])
        gate_tok = sb("gate_tok", [P, 2, GHALF], I32)
        gate_part = sb("gate_part", [P, EXPERTS, 2 * GROUPS * ITERS])
        gate = sb("gate", [P, EXPERTS])
        wv_hi = sb("wv_hi", [P, DM], F16)
        wv_lo = sb("wv_lo", [P, DM], F16)
        x = sb("x", [P, DM])
        xn = sb("xn", [P, DM])
        y = sb("y", [P, DM])
        xnT = sb("xnT", [P, KD, P])
        ident = sb("ident", [P, P])
        causal = sb("causal", [P, P])
        keep_T = sb("keep_T", [P, P])
        ones_row = sb("ones_row", [1, P])
        ones_hpg = sb("ones_hpg", [HPG, P], BF16)
        iota8 = sb("iota8", [P, EXPERTS])
        minus_half = sb("minus_half", [P, 1])
        rows = sb("rows", [1, N_ROW])
        cols = sb("cols", [P, N_COL])
        wide = sb("wide", [P, len(WIDE), DM])
        b2 = sb("b2", [EXPERTS + 1, DM])
        bkT = sb("bkT", [16, HEADS])
        w_sigma = sb("w_sigma", [P, 1])
        act_scale = sb("act_scale", [P, 1])
        tiny = sb("tiny", [P, 160])
        stats, mv = tiny[:, 0:6], tiny[:, 6:8]
        veps, rstd = tiny[:, 8:9], tiny[:, 9:10]
        mx_group, neg_max = tiny[:, 10:14], tiny[:, 14:18]
        rden = tiny[:, 18:34]
        mx16, den16 = tiny[:, 34:50], tiny[:, 50:66]
        sig = tiny[:, 66:70]
        amax, qs, qinv = tiny[:, 70:75], tiny[:, 75:80], tiny[:, 80:85]
        amax_all = tiny[:, 85:90]
        top8 = tiny[:, 90:98]
        top_w = tiny[:, 98:102]
        combine = tiny[:, 102:102 + EXPERTS + 1]
        qscale = tiny[:, 112:114]
        key_bias_score = tiny[:, 116:132]
        logits = tiny[:, 132:140]
        pick = tiny[:, 140:148]
        top_i = sb("top_i", [P, 8], U32)
        top_if = sb("top_if", [P, 8])
        mx_part = sb("mx_part", [P, HPG, MCPI * ITERS])
        bias_rows = sb("bias_rows", [HPG, HPG, P], BF16)
        l0_quant = gate_part[:, :, :].rearrange("p e c -> p (e c)")[:, 0:3 * 1536 // QBLOCK]
        combine_T = work[0:EXPERTS + 1, 8192:8192 + P]
        ps = ctx.enter_context(nc.psum_tensor("ps", [P, 8, 512], F32))

        probs = work[:, 0:4096]
        u_norm = work[:, 4096:6144]
        x_qT = work[:, 4096:6144]
        q_hi = work[:, 6144:7168].bitcast(F16)
        q_lo = work[:, 7168:8192].bitcast(F16)
        u_T = work[:, 0:2048]
        gate_junk = work[:, 8192:8192 + 2 * GHALF].rearrange("p (s c) -> p s c", s=2)
        v_ring = work[:, 8192:8192 + TPI * HPG * VW].rearrange("p (t h c) -> p t h c", t=TPI, h=HPG)
        k_stack = ctx_flat[:, 0:KPI].bitcast(F16).rearrange("p (s k) -> p s k", s=2)
        q_stack = ctx_flat[:, KPI:KPI + 1024].bitcast(F16)
        wk_size = STACKS * STACK_W // 2
        wk_hi, wk_lo = (ctx_flat[:, KPI + 1024 + m * wk_size:KPI + 1024 + (m + 1) * wk_size].bitcast(F16)
                        for m in range(2))
        u_raw = work[:, 4096:4608].rearrange("p (g q) -> p g q", g=GROUPS)
        a_qT, a_kT = work[:, 0:2048], work[:, 2048:4096]
        a_v = work[:, 4096:5120]
        a_p, a_pT = work[:, 5120:7168], work[:, 7168:9216]
        o_sb = work[:, 2048:3072]
        o_T = work[:, 3072:4096]
        stage = work[:, 0:2 * KPI].rearrange("p (s c) -> p s c", s=2)

        def l0_wT(m):
            return work[:, m * 1536:(m + 1) * 1536].rearrange("p (k n) -> p k n", k=KD)

        l0_down = work[:, 3072:4608].rearrange("p (k n) -> p k n", k=6)
        l0_gate, l0_up = work[:, 4608:5376], work[:, 5376:6144]
        l0_h = work[:, 6144:6912]
        l0_hT = work[:, 6912:7680]
        l0_tmp = work[:, 7680:9216]
        f_a, f_b, f_c = work[:, 0:1024], work[:, 1024:2048], work[:, 2048:3072]
        f_d = work[:, 3072:4096]
        l2f_w = work[:, 0:512].rearrange("p (k n) -> p k n", k=KD)
        e_relu = work[:, 0:1024].rearrange("p (s n) -> p s n", s=2)
        m_h = work[:, 0:2048].rearrange("p (s n) -> p s n", s=2)
        scratch = work[:, 8192:9216]

        def key_weights(piece):
            w = slot(piece)[:, 1280:1536].rearrange("p (s c) -> p s c", c=32)
            return w.unsqueeze(2).broadcast_to([P, STACKS, 3, 32])

        def q_part(row, b, half):
            return q_stack[row:STACK_W, b * 1024:(b + 1) * 1024].rearrange(
                "p (s h q) -> p s h q", h=2, q=P)[:, :, half, :]

        def head_scale(row, half):
            at = COL_AT["head_half"] + half
            return cols[row:STACK_W, at:at + 1]

        block = ctx.enter_context(nc.Block())

        x_layers = [n for n in layers if n in XATTN]
        v_layers = [n for n in x_layers if XATTN[n] == 16]
        u_layers = [n for n in x_layers if XATTN[n] == 64]
        tails = [n for n in layers if n in XATTN or n in SATTN or n == "L3_attn"]
        ln_at = {}
        for n in layers:
            ln_at[n] = len(ln_at)
            if n == "L2_attn":
                ln_at["L2_attn/post"] = len(ln_at)
        q_users = [n for n in layers if n in XATTN or n in SATTN or n == "L3_attn"]
        kv_users = [n for n in layers if n in SATTN or n == "L3_attn"]
        pieces = [p for p in PIECES if p[0] in layers]
        of_layer = {n: [i for i, p in enumerate(pieces) if p[0] == n] for n in layers}
        free_from = min([i for i, p in enumerate(pieces) if PIECES.index(p) >= FREE_FROM], default=len(pieces))
        has_gate = "L3_xattn" in layers
        gate_rider = "L1_xattn" if "L1_xattn" in layers else None

        slot_of, last_in, before = [], {}, []
        for i in range(len(pieces)):
            if i < free_from:
                s = i % RING_A
            else:
                k = i - free_from
                order = [(free_from + j) % RING_A for j in range(RING_A)] + [RING_A + j for j in range(RING_B)]
                s = order[k % len(order)]
            slot_of.append(s)
            before.append(last_in.get(s))
            last_in[s] = i
        arrivals, slot_count = [], {}
        for i, (_, parts) in enumerate(pieces):
            slot_count[slot_of[i]] = slot_count.get(slot_of[i], 0) + 16 * len(parts)
            arrivals.append(slot_count[slot_of[i]])

        def slot(i):
            s = slot_of[i]
            if s < RING_A:
                return ring_a[:, s, :]
            return ctx_mem[:, (s - RING_A) * PIECE:(s - RING_A + 1) * PIECE]

        def piece_arrived(eng, i):
            eng.wait_ge(sem(f"piece_in_slot{slot_of[i]}"), arrivals[i])

        def last_use(i):
            layer = pieces[i][0]
            k = i - of_layer[layer][0]
            if layer in tails:
                return sem("y_in_psum"), tails.index(layer) + 1
            if layer == "L1_ffn" and k < 2:
                return sem("swiglu_in_psum"), k + 1
            if layer == "L1_ffn" and k < 10:
                return sem("hidden_in_psum"), (k - 2) // 2 + 1
            if layer == "L3_xattn":
                return sem("expert_down"), k + 1
            if layer == "L3_ffn":
                return (sem("moe_down"), k // 2 + 1) if k % 2 else (sem("moe_up"), k + 2)
            return {"L0_ffn": sem("l0_ffn_y"), "L1_ffn": sem("l1_ffn_y"), "L2_ffn": sem("l2_ffn_y")}[layer], 1

        def v_count(name, g, i):
            return ((v_layers.index(name) * GROUPS + g) * ITERS + i) * len(V_CHUNKS)

        def step_base(name):
            return sum(GROUPS * ITERS * len(STEPS[XATTN[m]]) for m in x_layers[:x_layers.index(name)])

        def k_count(name, g, i):
            return ((v_layers.index(name) * GROUPS + g) * ITERS + i) * len(BUILDS)

        def steps_since(j, slots, total):
            return slots if j >= slots else total - (total - 1 - j) // slots * slots

        def counted(names, layer, per=1):
            return names.index(layer) * per

        @block.sync
        def _(sp):
            def load_piece(i):
                if before[i] is not None:
                    sp.wait_ge(*last_use(before[i]))
                if slot_of[i] >= RING_A and x_layers:
                    sp.wait_ge(sem("u_done"), GROUPS * len(x_layers))
                for name, at, r, c in pieces[i][1]:
                    dst = slot(i)[0:r, at:at + c]
                    if name == "L2f_w":
                        dst = dst.bitcast(I32)
                    sp.dma_start(dst, dram[name]).then_inc(sem(f"piece_in_slot{slot_of[i]}"), 16)

            sp.dma_start(x[:, :], dram["x"]).then_inc(sem("x_loaded"), 16)
            consts = [(rows[:, :], "rows"), (cols[:, :], "cols"), (b2[:, :], "b2"), (bkT[:, :], "bkT")]
            for dst, name in consts:
                sp.dma_start(dst, dram[name]).then_inc(sem("consts_loaded"), 16)
            for i, name in enumerate(WIDE):
                sp.dma_start(wide[:, i, :], dram[name].partition_broadcast(P)).then_inc(sem("consts_loaded"), 16)
            for dst, name in ((w_sigma, "w_sigma"), (act_scale, "act_scale")):
                sp.dma_start(dst[:, :], dram[name].partition_broadcast(P)).then_inc(sem("consts_loaded"), 16)
            first = min(2, len(pieces))
            for i in range(first):
                load_piece(i)
            if x_layers:
                for c in range(ITERS):
                    if c >= 2:
                        sp.wait_ge(sem("ctx_low_made"), c - 1)
                    sp.dma_start(stage[:, c % 2, :], dram["ctxT"][:, c * KPI:(c + 1) * KPI]).then_inc(
                        sem(f"ctxT_staged{c % 2}"), 16)
            done = min(RING_A, len(pieces))
            for i in range(first, done):
                load_piece(i)
            if u_layers:
                before_u = x_layers.index(u_layers[0])
                if before_u:
                    sp.wait_ge(sem("u_done"), before_u * GROUPS)
                for c in range(ITERS):
                    sp.dma_start(ctx_rows[:, c * TPI:(c + 1) * TPI, 0:CD], dram["ctx_rows"][:, c * TPI:(c + 1) * TPI, :]
                                 ).then_inc(sem("ctx_rows_loaded"), 16)

            def stream_gate():
                with sp.Fori(0, GROUPS * ITERS) as u:
                    for s in range(2):
                        sp.wait_ge(sem("gate_sums"), u * GATE_STEPS + (s + 1) * EXPERTS)
                        for dst, name in ((gate_ctx, "ctxT"), (gate_tok, "tokT")):
                            sp.dma_start(dst[:, s, :], dram[name][:, bass.ds(u * MCHUNK + s * GHALF, GHALF)]
                                         ).then_inc(sem(f"gate_in_slot{s}"), 16)

            stop = min(of_layer[gate_rider][-1] + 3, len(pieces)) if gate_rider else done
            for i in range(done, stop):
                load_piece(i)
            if has_gate:
                stream_gate()
            for i in range(max(done, stop), len(pieces)):
                load_piece(i)
            sp.wait_ge(sem("x_final"), 1)
            sp.dma_start(out, x[:, :]).then_inc(sem("stored"), 16)
            sp.wait_ge(sem("stored"), 16)

        @block.gpsimd
        def _(pool):
            made = [0]

            def chained(ins):
                made[0] += 1
                ins.then_inc(sem("pool_step"), 1)
                pool.wait_ge(sem("pool_step"), made[0])

            chained(pool.memset(ident[:, :], 0.0))
            chained(pool.memset(causal[:, :], 0.0))
            chained(pool.memset(keep_T[:, :], 1.0))
            pool.memset(minus_half[:, :], -0.5).then_inc(sem("pool_consts"), 1)
            pool.memset(ones_row[:, :], 1.0).then_inc(sem("pool_consts"), 1)
            pool.memset(ones_hpg[:, :], 1.0).then_inc(sem("pool_consts"), 1)
            pool.iota(iota8[:, :], [[1, EXPERTS]], base=0, channel_multiplier=0,
                      allow_small_or_imprecise_dtypes=True).then_inc(sem("pool_consts"), 1)
            pool.affine_select(out=ident[:, :], in_=ident[:, :], compare_op=ALU.not_equal, fill=1.0, base=0,
                               pattern=[[-1, P]], channel_multiplier=1).then_inc(sem("pool_consts"), 1)
            pool.affine_select(out=causal[:, :], in_=causal[:, :], compare_op=ALU.is_ge, fill=MASKED, base=0,
                               pattern=[[-1, P]], channel_multiplier=1).then_inc(sem("pool_consts"), 1)
            pool.affine_select(out=keep_T[:, :], in_=keep_T[:, :], compare_op=ALU.is_ge, fill=0.0, base=0,
                               pattern=[[1, P]], channel_multiplier=-1).then_inc(sem("pool_consts"), 1)

            def layernorm(name):
                pool.wait_ge(sem("var_ready"), ln_at[name] + 1)
                eps = 1e-3 if name == "L2_attn/post" else 1e-5
                chained(pool.tensor_scalar(veps, mv[:, 1:2], eps, None, ALU.add))
                pool.tensor_tensor(rstd, veps, minus_half[:, :], ALU.pow).then_inc(sem("rstd_ready"), 1)

            pool.wait_ge(sem("pool_consts"), 7)
            for name in layers:
                layernorm(name)
                if name == "L2_attn":
                    layernorm("L2_attn/post")
                if name == "L0_ffn":
                    for z in range(5):
                        pool.wait_ge(sem("amax_ready"), z + 1)
                        pool.partition_all_reduce(amax_all[:, z:z + 1], amax[:, z:z + 1], P, RMAX
                                                  ).then_inc(sem("amax_all_ready"), 1)

        @block.tensor
        def _(pe):
            def transpose_xn(name):
                pe.wait_ge(sem("xn_ready"), layers.index(name) + 1)
                for k in range(KD):
                    last = pe.transpose(ps[:, 0, k * P:(k + 1) * P], xn[:, k * P:(k + 1) * P], ident[:, :])
                last.then_inc(sem("xnT_in_psum"), 1)
                pe.wait_ge(sem("xnT_ready"), layers.index(name) + 1)

            def heads_T(w, d, banks, done, bias=None):
                for h in range(HEADS):
                    dst = ps[0:d, banks[h // 4], (h % 4) * P:(h % 4 + 1) * P]
                    for k in range(KD):
                        last = pe.matmul(dst, w[:, k, h * d:(h + 1) * d], xnT[:, k, :], start=(k == 0),
                                         stop=(k == KD - 1 and bias is None))
                    if bias is not None:
                        last = pe.matmul(dst, bias[:, h * d:(h + 1) * d], ones_row[:, :], start=False, stop=True)
                    if h % 4 == 3:
                        last.then_inc(sem(done), 1)
                return last

            def output_tail(name, d, w_o, bias):
                t = tails.index(name)
                nk = HEADS * d // P
                pe.wait_ge(sem("o_ready"), t + 1)
                for k in range(nk):
                    last = pe.transpose(ps[:, 6 + k // 4, (k % 4) * P:(k % 4 + 1) * P],
                                        o_sb[:, k * P:(k + 1) * P], ident[:, :])
                last.then_inc(sem("oT_in_psum"), 1)
                pe.wait_ge(sem("oT_ready"), t + 1)
                if bias is not None:
                    pe.matmul(ps[:, 0, 0:DM], ones_row[:, :], bias, start=True, stop=False)
                for k in range(nk):
                    last = pe.matmul(ps[:, 0, 0:DM], o_T[:, k * P:(k + 1) * P], w_o[:, k, :],
                                     start=(k == 0 and bias is None), stop=(k == nk - 1))
                last.then_inc(sem("y_in_psum"), 1)

            def row(name):
                return rows[:, ROW_AT[name]:ROW_AT[name] + ROWS[name]]

            def cross_attention(name):
                d = XATTN[name]
                n = x_layers.index(name)
                q_base = counted(q_users, name, 4)
                pcs = of_layer[name]
                if len(pcs) == 2:
                    q_piece, k_piece = pcs
                    w = slot(q_piece)
                    w_q = w[:, 0:512].rearrange("p (k n) -> p k n", k=KD)
                    w_v, w_o = w[:, 512:768], w[:, 768:1280].rearrange("p (k n) -> p k n", k=2)
                else:
                    q_piece, k_piece, v_piece, o_piece = pcs
                    w_q = slot(q_piece).rearrange("p (k n) -> p k n", k=KD)
                    w_v, w_o = slot(v_piece)[:, 0:1024], slot(o_piece).rearrange("p (k n) -> p k n", k=8)
                first_x = name == "L0_xattn"
                transpose_xn(name)
                piece_arrived(pe, q_piece)
                last = heads_T(w_q, d, (2, 3, 4, 5), "qT_in_psum", row("bq") if first_x else None)
                piece_arrived(pe, k_piece)
                w_kT = slot(k_piece)[0:d, :]
                for h in range(HEADS):
                    if h % 4 == 0:
                        pe.wait_ge(sem("qT_ready"), q_base + h // 4 + 1)
                    last = pe.matmul(ps[:, (0, 1, 6, 7)[h // 4], (h % 4) * P:(h % 4 + 1) * P],
                                     w_kT[:, h * P:(h + 1) * P], x_qT[0:d, h * P:(h + 1) * P], start=True, stop=True)
                    if h % 4 == 3:
                        last.then_inc(sem("absorbed_in_psum"), 1)
                if first_x:
                    for h in range(HEADS):
                        last = pe.matmul(ps[:, 2, h:h + 1], x_qT[0:d, h * P:(h + 1) * P], bkT[:, h:h + 1],
                                         start=True, stop=True)
                    last.then_inc(sem("key_bias_in_psum"), 1)
                if d == 16:
                    for s in range(STACKS):
                        for r in range(3):
                            dst = ps[32 * r:32 * r + 32, 4 + s // 4, (s % 4) * P:(s % 4 + 1) * P]
                            for k in range(KD):
                                last = pe.matmul(dst, w_q[:, k, s * 32:(s + 1) * 32], xnT[:, k, :], start=(k == 0),
                                                 stop=(k == KD - 1 and not first_x))
                            if first_x:
                                last = pe.matmul(dst, row("bq")[:, s * 32:(s + 1) * 32], ones_row[:, :],
                                                 start=False, stop=True)
                    last.then_inc(sem("q_stack_in_psum"), 1)
                else:
                    pe.wait_ge(sem("q_low_ready"), 4 * (u_layers.index(name) + 1))
                pe.wait_ge(sem("q_high_ready"), 4 * (n + 1))

                def max_unit(g, i, u, count):
                    c, hh = u // HPG, u % HPG
                    pe.wait_ge(sem("max_slots_free"), count + u + 1)
                    pe.matmul(ps[:, u % 2, 0:MCHUNK], q_hi[:, bass.ds(g * GW + hh * P, P)],
                              ctxT_hi[:, bass.ds(i * KPI + c * MCHUNK, MCHUNK)], start=True, stop=True
                              ).then_inc(sem("max_scores_ready"), 1)

                def bias_transpose(g):
                    pe.wait_ge(sem("neg_max_ready"), n * GROUPS + g + 1)
                    if d == 16:
                        last = pe.matmul(ps[STACK_W:STACK_ROWS, 0, 0:P], neg_max, ident[:, :], start=True, stop=True)
                    else:
                        last = pe.transpose(ps[0:HPG, 0, 0:P], neg_max, ident[:, :])
                    last.then_inc(sem("neg_max_T"), 1)

                def scores(g, i, j, count):
                    pe.wait_ge(sem("step_exp_done"), count + j + 1 - 2 + CREDIT)
                    for t in range(steps[j]):
                        dst = ps[:, 2 + 2 * (j % 2) + t, :]
                        key = i * KPI + (tile_of[j] + t) * P
                        hi, lo = ctxT_hi[:, bass.ds(key, P)], ctxT_lo[:, bass.ds(key, P)]
                        qh, ql = q_hi[:, bass.ds(g * GW, GW)], q_lo[:, bass.ds(g * GW, GW)]
                        pe.matmul(dst, hi, qh, start=True, stop=False)
                        pe.matmul(dst, hi, ql, start=False, stop=False)
                        pe.matmul(dst, lo, qh, start=False, stop=False)
                        last = pe.matmul(dst, ones_hpg[:, :], bias_rows[:, :, :].rearrange("p a b -> p (a b)"),
                                         start=False, stop=True)
                    last.then_inc(sem("step_scores_ready"), 1)

                def sum_up(i, j, count):
                    pe.wait_ge(sem("step_exp_done"), count + j + 1 + CREDIT)
                    for t in range(steps[j]):
                        for hh in range(HPG):
                            at = (j % P_SLOTS[d]) * 2 * GW + t * GW + hh * P
                            last = pe.matmul(ps[:, 6 + hh // 2, (hh % 2) * UW:(hh % 2 + 1) * UW],
                                             probs[:, at:at + P],
                                             ctx_flat[:, bass.ds((i * TPI + tile_of[j] + t) * UW, UW)],
                                             start=False, stop=False, skip_group_check=True)
                    last.then_inc(sem("step_summed"), 1)

                def build_keys(g, i, c, s, kcount):
                    pe.wait_ge(sem("keys_ready"), kcount + BUILDS.index((c, s)) + 1)
                    dst = ps[0:STACK_W, 4 + s, 0:MCHUNK]
                    at = bass.ds(g * 2 * STACK_W + s * STACK_W, STACK_W)
                    keys = bass.ds(i * KPI + c * MCHUNK, MCHUNK)
                    pe.matmul(dst, wk_hi[:, at], ctxT_hi[:, keys], start=True, stop=False)
                    pe.matmul(dst, wk_lo[:, at], ctxT_hi[:, keys], start=False, stop=False)
                    pe.matmul(dst, wk_hi[:, at], ctxT_lo[:, keys], start=False, stop=True
                              ).then_inc(sem("keys_in_psum"), 1)

                def stacked_scores(g, t, count, kcount):
                    pe.wait_ge(sem("step_exp_done"), count + t + 1 - 2 + CREDIT)
                    chunk = ((t + 1) * P - 1) // MCHUNK
                    pe.wait_ge(sem("keys_ready"), kcount + BUILDS.index((chunk, 1)) + 1 + 2)
                    for s in range(2):
                        last = pe.matmul(ps[:, 2 + t % 2, s * 2 * P:(s + 1) * 2 * P],
                                         k_stack[0:STACK_ROWS, s, t * P:(t + 1) * P],
                                         q_stack[0:STACK_ROWS, bass.ds(g * GW + s * 2 * P, 2 * P)],
                                         start=True, stop=True)
                    last.then_inc(sem("step_scores_ready"), 1)

                def project_values(g, i, c, vcount):
                    pe.wait_ge(sem("values_ready"), vcount + c + 1)
                    a, b = V_CHUNKS[c]
                    for t in range(a, b):
                        dst = ps[:, 7, (t - a) * 64:(t - a + 1) * 64]
                        key = (i * TPI + t) * P
                        hi, lo = ctxT_hi[:, bass.ds(key, P)], ctxT_lo[:, bass.ds(key, P)]
                        cols_g = bass.ds(g * HPG * 16, HPG * 16)
                        pe.matmul(dst, hi, wv_hi[:, cols_g], start=True, stop=False)
                        pe.matmul(dst, hi, wv_lo[:, cols_g], start=False, stop=False)
                        last = pe.matmul(dst, lo, wv_hi[:, cols_g], start=False, stop=True)
                    last.then_inc(sem("values_in_psum"), 1)

                def sum_values(t, count, vcount):
                    pe.wait_ge(sem("step_exp_done"), count + t + 1 + CREDIT)
                    for c, (a, b) in enumerate(V_CHUNKS):
                        if a == t:
                            pe.wait_ge(sem("values_ready"), vcount + c + 2)
                    for hh in range(HPG):
                        at = (t % P_SLOTS[d]) * GW + hh * P
                        last = pe.matmul(ps[32 * hh:32 * hh + VW, 6, 0:P], v_ring[:, t, hh, :], probs[:, at:at + P],
                                         start=False, stop=False, skip_group_check=True)
                    last.then_inc(sem("step_summed"), 1)

                steps = STEPS[d]
                tile_of = [sum(steps[:j]) for j in range(len(steps))]

                def max_loop():
                    with pe.Fori(0, ITERS) as i:
                        if n == 0:
                            pe.wait_ge(sem("ctx_low_made"), i + 1)
                        for u in range(MUPI):
                            max_unit(0, i, u, i * MUPI + n * GROUPS * ITERS * MUPI)

                def keys_loop(g, max_group):
                    with pe.Fori(0, ITERS) as i:
                        count = (g * ITERS + i) * len(steps) + step_base(name)
                        pe.wait_ge(sem("bias_rows_ready"), n * GROUPS + g + 1)
                        pe.wait_ge(sem("u_cleared"), n * GROUPS + g + 1)
                        units = [0]

                        def max_units(k):
                            if max_group is None:
                                return
                            mcount = (max_group * ITERS + i) * MUPI + n * GROUPS * ITERS * MUPI
                            for _ in range(k):
                                max_unit(max_group, i, units[0], mcount)
                                units[0] += 1

                        if d == 64:
                            for j in range(len(steps)):
                                scores(g, i, j, count)
                                if j >= 1:
                                    sum_up(i, j - 1, count)
                                max_units(2)
                            sum_up(i, len(steps) - 1, count)
                            return
                        vcount, kcount = v_count(name, g, i), k_count(name, g, i)
                        build_keys(g, i, 0, 0, kcount)
                        build_keys(g, i, 0, 1, kcount)
                        max_units(2)
                        project_values(g, i, 0, vcount)
                        build_keys(g, i, 1, 0, kcount)
                        for t in range(TPI):
                            stacked_scores(g, t, count, kcount)
                            if t >= 2:
                                sum_values(t - 2, count, vcount)
                            if t in BUILD_AFTER:
                                build_keys(g, i, *BUILD_AFTER[t], kcount)
                            if t in VALUES_AFTER:
                                project_values(g, i, VALUES_AFTER[t], vcount)
                            if t != NO_UNIT_AFTER:
                                max_units(1)
                        sum_values(TPI - 2, count, vcount)
                        max_units(1)
                        sum_values(TPI - 1, count, vcount)

                max_loop()
                if d == 64:
                    pe.wait_ge(sem("ctx_rows_loaded"), 16 * ITERS)
                pe.wait_ge(sem("ones_ready"), n + 1)
                if d == 16:
                    pe.wait_ge(sem("wv_high_ready"), v_layers.index(name) + 1)
                    pe.wait_ge(sem("wv_low_ready"), v_layers.index(name) + 1)
                    pe.wait_ge(sem("wk_ready"), v_layers.index(name) + 1)
                    pe.wait_ge(sem("q_stack_ready"), v_layers.index(name) + 1)
                with pe.Fori(0, GROUPS - 1) as g:
                    bias_transpose(g)
                    keys_loop(g, g + 1)
                bias_transpose(GROUPS - 1)
                keys_loop(GROUPS - 1, None)

                if d == 16:
                    for g in range(GROUPS):
                        pe.wait_ge(sem("u_done"), n * GROUPS + g + 1)
                        last = pe.transpose(ps[:, 0, g * P:(g + 1) * P], u_raw[:, g, :], ident[:, :])
                    last.then_inc(sem("o_in_psum"), 1)
                else:
                    for b in range(4):
                        pe.wait_ge(sem("u_done"), n * GROUPS + b + 1)
                        for hh in range(4):
                            h = 4 * b + hh
                            last = pe.transpose(ps[:, 2 + b, hh * P:(hh + 1) * P], u_norm[:, h * P:(h + 1) * P],
                                                ident[:, :])
                        last.then_inc(sem("uT_in_psum"), 1)
                    piece_arrived(pe, v_piece)
                    for h in range(HEADS):
                        if h % 4 == 0:
                            pe.wait_ge(sem("uT_ready"), 4 * u_layers.index(name) + h // 4 + 1)
                        at = h * d
                        last = pe.matmul(ps[:, at // 512, at % 512:at % 512 + d], u_T[:, h * P:(h + 1) * P],
                                         w_v[:, at:at + d], start=True, stop=True)
                    last.then_inc(sem("o_in_psum"), 1)
                    piece_arrived(pe, o_piece)
                bias = {"L0_xattn": "L0x_bo", "L1_xattn": "L1x_bo"}.get(name)
                output_tail(name, d, w_o, row(bias) if bias else None)

            def self_attention(name):
                d = SATTN[name] if name in SATTN else 16
                q_base = counted(q_users, name, 4)
                k_base = counted(kv_users, name, 4)
                a = kv_users.index(name)
                pcs = of_layer[name]
                width = HEADS * d
                if len(pcs) == 1:
                    w = slot(pcs[0]).rearrange("p (m k n) -> p m k n", m=4, k=KD)
                    w_q, w_k, w_v, w_o = (w[:, m] for m in range(4))
                    p_q = p_k = p_v = p_o = pcs[0]
                else:
                    w_q, w_k, w_v = (slot(p).rearrange("p (k n) -> p k n", k=KD) for p in pcs[:3])
                    w_o = slot(pcs[3]).rearrange("p (k n) -> p k n", k=8)
                    p_q, p_k, p_v, p_o = pcs
                transpose_xn(name)
                piece_arrived(pe, p_q)
                heads_T(w_q, d, (2, 3, 4, 5), "qT_in_psum")
                piece_arrived(pe, p_k)
                heads_T(w_k, d, (0, 1, 6, 7), "kT_in_psum")
                piece_arrived(pe, p_v)
                linear = name == "L3_attn"
                if linear:
                    pe.wait_ge(sem("qT_ready_linear"), 4)
                else:
                    pe.wait_ge(sem("qT_ready"), q_base + 4)
                for c in range(ceil_div(width, 512)):
                    w_c = min(512, width)
                    for k in range(KD):
                        last = pe.matmul(ps[:, 2 + c, 0:w_c], xnT[:, k, :], w_v[:, k, c * 512:c * 512 + w_c],
                                         start=(k == 0), stop=(k == KD - 1))
                last.then_inc(sem("v_in_psum"), 1)
                if linear:
                    pe.wait_ge(sem("kT_ready_linear"), 4)
                else:
                    pe.wait_ge(sem("kT_ready"), k_base + 4)
                for h in range(HEADS):
                    qh, kh = a_qT[0:d, h * P:(h + 1) * P], a_kT[0:d, h * P:(h + 1) * P]
                    dst = ps[:, 4 + h // 4, (h % 4) * P:(h % 4 + 1) * P]
                    last = pe.matmul(dst, kh if linear else qh, qh if linear else kh, start=True, stop=True)
                    if h % 4 == 3:
                        last.then_inc(sem("scores_in_psum"), 1)
                if linear:
                    pe.wait_ge(sem("v_ready_linear"), 1)
                    pe.wait_ge(sem("masked_ready"), 4)
                    for h in range(HEADS):
                        last = pe.matmul(ps[:, 0, h * (d + 1):(h + 1) * (d + 1)], a_p[:, h * P:(h + 1) * P],
                                         a_v[:, h * (d + 1):(h + 1) * (d + 1)], start=True, stop=True)
                    last.then_inc(sem("o_in_psum"), 1)
                else:
                    pe.wait_ge(sem("v_ready"), a + 1)
                    for b in range(4):
                        pe.wait_ge(sem("p_ready"), 4 * a + b + 1)
                        for hh in range(4):
                            h = 4 * b + hh
                            last = pe.transpose(ps[:, b, hh * P:(hh + 1) * P], a_p[:, h * P:(h + 1) * P], ident[:, :])
                        last.then_inc(sem("pT_in_psum"), 1)
                    for h in range(HEADS):
                        if h % 4 == 0:
                            pe.wait_ge(sem("pT_ready"), 4 * a + h // 4 + 1)
                        at = h * d
                        last = pe.matmul(ps[:, 4 + at // 512, at % 512:at % 512 + d], a_pT[:, h * P:(h + 1) * P],
                                         a_v[:, at:at + d], start=True, stop=True)
                    last.then_inc(sem("o_in_psum"), 1)
                piece_arrived(pe, p_o)
                output_tail(name, d, w_o, row("bout") if name == "L0_attn" else None)

            def l0_ffn():
                g_piece, u_piece, d_piece = of_layer["L0_ffn"]
                if ln_at["L0_ffn"]:
                    pe.wait_ge(sem("x_updated"), ln_at["L0_ffn"])
                for m in range(2):
                    pe.wait_ge(sem("w_quantised"), m + 1)
                    wq = slot((g_piece, u_piece)[m])[:, 0:1536].rearrange("p (o i) -> p o i", o=6)
                    for k in range(KD):
                        for o in range(6):
                            at = o * P
                            last = pe.transpose(ps[:, 2 * (2 * m + k) % 8 + at // 512, at % 512:at % 512 + P],
                                                wq[:, o, k * P:(k + 1) * P], ident[:, :])
                        last.then_inc(sem("wT_in_psum"), 1)
                pe.wait_ge(sem("w_quantised"), 3)
                pe.wait_ge(sem("wT_copied"), 2)
                wq = slot(d_piece)[:, 0:1536].rearrange("p (o i) -> p o i", o=2)
                for k in range(6):
                    for o in range(2):
                        at = k * DM + o * P
                        last = pe.transpose(ps[:, at // 512, at % 512:at % 512 + P],
                                            wq[:, o, k * P:(k + 1) * P], ident[:, :])
                last.then_inc(sem("wT_in_psum"), 1)
                pe.wait_ge(sem("wT_copied"), 5)
                transpose_xn("L0_ffn")
                for m in range(2):
                    for at, c in ((0, 512), (512, 256)):
                        for k in range(KD):
                            last = pe.matmul(ps[:, 2 + 2 * m + at // 512, 0:c], xnT[:, k, :],
                                             l0_wT(m)[:, k, at:at + c], start=(k == 0), stop=(k == KD - 1))
                    last.then_inc(sem("gate_up_in_psum"), 1)
                pe.wait_ge(sem("l0_h_ready"), 1)
                for k in range(6):
                    last = pe.transpose(ps[:, 6 + k // 4, (k % 4) * P:(k % 4 + 1) * P], l0_h[:, k * P:(k + 1) * P],
                                        ident[:, :])
                last.then_inc(sem("l0_hT_in_psum"), 1)
                pe.wait_ge(sem("l0_hT_ready"), 1)
                for k in range(6):
                    last = pe.matmul(ps[:, 0, 0:DM], l0_hT[:, k * P:(k + 1) * P], l0_down[:, k, :], start=(k == 0),
                                     stop=(k == 5))
                last.then_inc(sem("l0_ffn_y"), 1)

            def l1_ffn():
                pcs = of_layer["L1_ffn"]
                transpose_xn("L1_ffn")
                for m in range(2):
                    piece_arrived(pe, pcs[m])
                    w = slot(pcs[m]).rearrange("p (k n) -> p k n", k=KD)
                    for f in range(FT):
                        for k in range(KD):
                            last = pe.matmul(ps[:, 2 + 2 * m + f // 4, (f % 4) * P:(f % 4 + 1) * P],
                                             w[:, k, f * P:(f + 1) * P], xnT[:, k, :], start=(k == 0), stop=(k == KD - 1))
                    last.then_inc(sem("swiglu_in_psum"), 1)
                pe.wait_ge(sem("swiglu_ready"), 1)
                src = f_a
                for m, (banks, dst) in enumerate((((6, 7), f_b), ((2, 3), f_a))):
                    if m:
                        pe.wait_ge(sem("gelu_ready"), FT)
                    for f in range(FT):
                        piece = pcs[2 + 4 * m + f // 2]
                        if f % 2 == 0:
                            piece_arrived(pe, piece)
                        w = slot(piece).rearrange("p (k n) -> p k n", k=FT)
                        for k in range(FT):
                            last = pe.matmul(ps[:, banks[f // 4], (f % 4) * P:(f % 4 + 1) * P],
                                             w[:, k, (f % 2) * P:(f % 2 + 1) * P], src[:, k * P:(k + 1) * P],
                                             start=(k == 0), stop=(k == FT - 1))
                        if f % 4 == 3:
                            last.then_inc(sem("hidden_in_psum"), 1)
                    src = dst
                pe.wait_ge(sem("gelu_ready"), 2 * FT)
                piece_arrived(pe, pcs[10])
                w = slot(pcs[10]).rearrange("p (k n) -> p k n", k=FT)
                for k in range(FT):
                    last = pe.matmul(ps[:, 0, 0:DM], f_a[:, k * P:(k + 1) * P], w[:, k, :], start=(k == 0),
                                     stop=(k == FT - 1))
                last.then_inc(sem("l1_ffn_y"), 1)

            def l2_ffn():
                transpose_xn("L2_ffn")
                pe.wait_ge(sem("l2f_w_ready"), 1)
                pe.matmul(ps[:, 0, 0:DM], ones_row[:, :], row("L2f_bias"), start=True, stop=False)
                for k in range(KD):
                    last = pe.matmul(ps[:, 0, 0:DM], xnT[:, k, :], l2f_w[:, k, :], start=False, stop=(k == KD - 1))
                last.then_inc(sem("l2_ffn_y"), 1)

            def l3_xattn():
                pcs = of_layer["L3_xattn"]
                transpose_xn("L3_xattn")
                nh = XHID // P

                def up(e):
                    piece_arrived(pe, pcs[e])
                    w = slot(pcs[e])[:, 0:1024].rearrange("p (k n) -> p k n", k=KD)
                    if e >= 2:
                        pe.wait_ge(sem("relu_ready"), e - 1)
                    for f in range(nh):
                        for k in range(KD):
                            last = pe.matmul(ps[:, 2 + e % 2, f * P:(f + 1) * P], w[:, k, f * P:(f + 1) * P],
                                             xnT[:, k, :], start=(k == 0), stop=(k == KD - 1))
                    last.then_inc(sem("expert_up"), 1)

                def down(e):
                    w = slot(pcs[e])[:, 1024:2048].rearrange("p (k n) -> p k n", k=nh)
                    pe.wait_ge(sem("relu_ready"), e + 1)
                    if e >= 2:
                        pe.wait_ge(sem("expert_added"), e - 1)
                    for k in range(nh):
                        last = pe.matmul(ps[:, 4 + e % 2, 0:DM], e_relu[:, e % 2, k * P:(k + 1) * P], w[:, k, :],
                                         start=(k == 0), stop=(k == nh - 1))
                    last.then_inc(sem("expert_down"), 1)

                for e in range(EXPERTS + 1):
                    if e < EXPERTS:
                        up(e)
                    if e >= 1:
                        down(e - 1)

            def l3_ffn():
                pcs = of_layer["L3_ffn"]
                transpose_xn("L3_ffn")
                w_gate = cols[:, COL_AT["w_gate"]:COL_AT["w_gate"] + KD * EXPERTS].rearrange("p (k n) -> p k n", k=KD)
                pe.matmul(ps[:, 1, 0:EXPERTS], ones_row[:, :], row("gate_b"), start=True, stop=False)
                for k in range(KD):
                    last = pe.matmul(ps[:, 1, 0:EXPERTS], xnT[:, k, :], w_gate[:, k, :], start=False, stop=(k == KD - 1))
                last.then_inc(sem("logits_in_psum"), 1)

                def up(e):
                    piece_arrived(pe, pcs[2 * e])
                    w = slot(pcs[2 * e]).rearrange("p (k n) -> p k n", k=KD)
                    for f in range(FT):
                        if e >= 2 and f % 4 == 0:
                            pe.wait_ge(sem("moe_gelu_ready"), FT * (e - 2) + f + 4)
                        for k in range(KD):
                            last = pe.matmul(ps[:, 2 + 2 * (e % 2) + f // 4, (f % 4) * P:(f % 4 + 1) * P],
                                             w[:, k, f * P:(f + 1) * P], xnT[:, k, :], start=(k == 0), stop=(k == KD - 1))
                        if f % 4 == 3:
                            last.then_inc(sem("moe_up"), 1)

                def down(e):
                    piece_arrived(pe, pcs[2 * e + 1])
                    w = slot(pcs[2 * e + 1]).rearrange("p (k n) -> p k n", k=FT)
                    if e >= 2:
                        pe.wait_ge(sem("moe_added"), e - 1)
                    for k in range(FT):
                        pe.wait_ge(sem("moe_gelu_ready"), FT * e + k + 1)
                        last = pe.matmul(ps[:, 6 + e % 2, 0:DM], m_h[:, e % 2, k * P:(k + 1) * P], w[:, k, :],
                                         start=(k == 0), stop=(k == FT - 1))
                    last.then_inc(sem("moe_down"), 1)

                for e in range(EXPERTS + 2):
                    if e < EXPERTS + 1:
                        up(e)
                    if e == 1:
                        pe.wait_ge(sem("combine_ready"), 1)
                        pe.transpose(ps[0:EXPERTS + 1, 1, 0:P], combine, ident[:, :]).then_inc(sem("combine_T_psum"), 1)
                        pe.wait_ge(sem("combine_T_ready"), 1)
                        pe.matmul(ps[:, 1, 0:DM], combine_T[:, :], b2[:, :], start=True, stop=True
                                  ).then_inc(sem("moe_bias"), 1)
                    if e >= 1:
                        down(e - 1)

            pe.wait_ge(sem("consts_loaded"), 16 * 10)
            pe.wait_ge(sem("pool_consts"), 7)
            if x_layers:
                pe.sem_inc(sem("step_summed"), CREDIT)
            for name in layers:
                if name in XATTN:
                    cross_attention(name)
                elif name in SATTN or name == "L3_attn":
                    self_attention(name)
                else:
                    {"L0_ffn": l0_ffn, "L1_ffn": l1_ffn, "L2_ffn": l2_ffn, "L3_xattn": l3_xattn,
                     "L3_ffn": l3_ffn}[name]()

        @block.scalar
        def _(act):
            def heads_T_out(name, d, scale_of):
                q_base = counted(q_users, name, 4)
                dst = x_qT if name in XATTN else a_qT
                for b in range(4):
                    act.wait_ge(sem("qT_in_psum"), q_base + b + 1)
                    act.activation(dst[0:d, b * 512:(b + 1) * 512], ps[0:d, 2 + b, :], ACT.Identity, scale=scale_of(b)
                                   ).then_inc(sem("qT_ready"), 1)

            def cross_attention(name):
                d = XATTN[name]
                n = x_layers.index(name)
                heads_T_out(name, d, lambda b: d ** -0.5)
                for b in range(4):
                    act.wait_ge(sem("absorbed_in_psum"), 4 * n + b + 1)
                    act.activation(q_hi[:, b * 512:(b + 1) * 512], ps[:, (0, 1, 6, 7)[b], :], ACT.Copy
                                   ).then_inc(sem("q_high_ready"), 1)
                if d == 16:
                    piece = of_layer[name][0]
                    piece_arrived(act, piece)
                    act.activation(wv_hi[:, :], slot(piece)[:, 512:768], ACT.Copy).then_inc(sem("wv_high_ready"), 1)
                    act.activation(wk_hi.rearrange("p (s r c) -> p s r c", r=3, c=32), key_weights(piece), ACT.Copy
                                   ).then_inc(sem("wk_high_ready"), 1)
                    act.wait_ge(sem("consts_loaded"), 16 * 10)
                    act.wait_ge(sem("q_stack_in_psum"), v_layers.index(name) + 1)
                    for b in range(2):
                        for half in range(2):
                            act.activation(q_part(0, b, half), ps[0:STACK_W, 4 + b, :].rearrange(
                                "p (s q) -> p s q", s=4), ACT.Identity, scale=head_scale(0, half)
                                ).then_inc(sem("q_stack_high"), 1)
                if n == 0:
                    act.sem_inc(sem("step_exp_done"), CREDIT)
                    for c in range(ITERS):
                        act.wait_ge(sem(f"ctxT_staged{c % 2}"), 16 * (c // 2 + 1))
                        act.activation(ctxT_hi[:, c * KPI:(c + 1) * KPI], stage[:, c % 2, :], ACT.Copy
                                       ).then_inc(sem("ctx_high_made"), 1)

                steps = STEPS[d]

                def exp_step(j, count):
                    act.wait_ge(sem("step_scores_ready"), count + j + 1)
                    back = steps_since(j, P_SLOTS[d], len(steps))
                    act.wait_ge(sem("step_summed"), count + j + 1 - back + CREDIT)
                    if d == 16:
                        at = j % P_SLOTS[d] * GW
                        act.activation(probs[:, at:at + GW], ps[:, 2 + j % 2, :], ACT.Exp
                                       ).then_inc(sem("step_exp_done"), 1)
                    else:
                        at, k, b = j % P_SLOTS[d] * 2 * GW, steps[j], 2 + 2 * (j % 2)
                        act.activation(probs[:, at:at + k * GW].rearrange("p (t c) -> p t c", t=k), ps[:, b:b + k, :],
                                       ACT.Exp).then_inc(sem("step_exp_done"), 1)

                def high_keys(c, s, kcount):
                    act.wait_ge(sem("keys_in_psum"), kcount + BUILDS.index((c, s)) + 1)
                    act.activation(k_stack[0:STACK_W, s, c * MCHUNK:(c + 1) * MCHUNK],
                                   ps[0:STACK_W, 4 + s, 0:MCHUNK], ACT.Copy).then_inc(sem("keys_high_made"), 1)

                def exp_loop(g):
                    with act.Fori(0, ITERS) as i:
                        count = (g * ITERS + i) * len(steps) + step_base(name)
                        if d == 16:
                            kcount = k_count(name, g, i)
                            high_keys(0, 0, kcount)
                            high_keys(0, 1, kcount)
                            high_keys(1, 0, kcount)
                        for j in range(len(steps)):
                            exp_step(j, count)
                            if d == 16 and j in BUILD_AFTER:
                                high_keys(*BUILD_AFTER[j], kcount)

                with act.Fori(0, GROUPS) as g:
                    exp_loop(g)
                for b in range(4 if d == 64 else 0):
                    act.wait_ge(sem("uT_in_psum"), 4 * u_layers.index(name) + b + 1)
                    act.activation(u_T[:, b * 512:(b + 1) * 512], ps[:, 2 + b, :], ACT.Copy
                                   ).then_inc(sem("uT_ready"), 1)

            def self_attention(name):
                d = SATTN[name] if name in SATTN else 16
                a = kv_users.index(name)
                if name == "L3_attn":
                    q_base = counted(q_users, name, 4)
                    k_base = counted(kv_users, name, 4)
                    for m, dst in enumerate((a_qT, a_kT)):
                        for b in range(4):
                            act.wait_ge(sem("neg_part_ready"), 4 * m + b + 1)
                            part = dst[0:d, b * 512:(b + 1) * 512]
                            act.activation(part, part, ACT.Exp).then_inc(sem("exp_part_ready"), 1)
                    return
                if name == "L0_attn":
                    act.wait_ge(sem("consts_loaded"), 16 * 10)
                    act.activation(sig[:, 0:1], w_sigma[:, :], ACT.Exp, scale=-1.0).then_inc(sem("sigma_exp"), 1)
                    act.wait_ge(sem("sigma_scale"), 1)
                heads_T_out(name, d, lambda b: sig[0:d, 3:4] if (name == "L0_attn" and b == 0) else d ** -0.5)
                act.wait_ge(sem("v_in_psum"), a + 1)
                width = HEADS * d
                if width <= 512:
                    act.activation(a_v[:, 0:width], ps[:, 2, 0:width], ACT.Copy).then_inc(sem("v_ready"), 1)
                else:
                    act.activation(a_v[:, 0:width].rearrange("p (b c) -> p b c", b=2), ps[:, 2:4, :], ACT.Copy
                                   ).then_inc(sem("v_ready"), 1)
                for b in range(4):
                    act.wait_ge(sem("shifted_ready"), 4 * a + b + 1)
                    part = a_p[:, b * 512:(b + 1) * 512]
                    act.activation(part, part, ACT.Exp).then_inc(sem("p_ready"), 1)
                for b in range(4):
                    act.wait_ge(sem("pT_in_psum"), 4 * a + b + 1)
                    act.activation(a_pT[:, b * 512:(b + 1) * 512], ps[:, b, :], ACT.Copy).then_inc(sem("pT_ready"), 1)

            def l0_ffn():
                act.wait_ge(sem("l0_gate_ready"), 1)
                act.activation(l0_tmp[:, 0:768], l0_gate, ACT.Exp, scale=-1.0).then_inc(sem("l0_exp_ready"), 1)

            def l1_ffn():
                s = cols[:, COL_AT["w1_s"]:COL_AT["w1_s"] + FT]
                act.wait_ge(sem("w1_scaled"), 1)
                act.activation(f_c, f_b, ACT.Exp, scale=-1.0).then_inc(sem("silu_exp"), 1)
                for m, (banks, dst, sc) in enumerate((((6, 7), f_b, "h1_s"), ((2, 3), f_a, "h2_s"))):
                    for f in range(FT):
                        if f % 4 == 0:
                            act.wait_ge(sem("hidden_in_psum"), 2 * m + f // 4 + 1)
                        act.activation(dst[:, f * P:(f + 1) * P], ps[:, banks[f // 4], (f % 4) * P:(f % 4 + 1) * P],
                                       ACT.Gelu, scale=cols[:, COL_AT[sc] + f:COL_AT[sc] + f + 1]
                                       ).then_inc(sem("gelu_ready"), 1)

            def l3_xattn():
                for e in range(EXPERTS):
                    act.wait_ge(sem("expert_up"), e + 1)
                    if e >= 2:
                        act.wait_ge(sem("expert_down"), e - 1)
                    act.activation(e_relu[:, e % 2, :], ps[:, 2 + e % 2, :], ACT.Relu).then_inc(sem("relu_ready"), 1)

            def l3_ffn():
                act.wait_ge(sem("top_diff"), 1)
                act.activation(top_w[:, 1:2], top_w[:, 0:1], ACT.Exp).then_inc(sem("top_exp"), 1)
                for e in range(EXPERTS + 1):
                    if e >= 2:
                        act.wait_ge(sem("moe_down"), e - 1)
                    for f in range(FT):
                        if f % 4 == 0:
                            act.wait_ge(sem("moe_up"), 2 * e + f // 4 + 1)
                        at = COL_AT["b1"] + e * FT + f
                        act.activation(m_h[:, e % 2, f * P:(f + 1) * P],
                                       ps[:, 2 + 2 * (e % 2) + f // 4, (f % 4) * P:(f % 4 + 1) * P], ACT.Gelu,
                                       bias=cols[:, at:at + 1]).then_inc(sem("moe_gelu_ready"), 1)

            for name in layers:
                if name in XATTN:
                    cross_attention(name)
                elif name in SATTN or name == "L3_attn":
                    self_attention(name)
                elif name != "L2_ffn":
                    {"L0_ffn": l0_ffn, "L1_ffn": l1_ffn, "L3_xattn": l3_xattn, "L3_ffn": l3_ffn}[name]()

        @block.vector
        def _(dve):
            steps = [0]
            updates = [0]

            def chained(ins):
                steps[0] += 1
                ins.then_inc(sem("dve_step"), 1)
                dve.wait_ge(sem("dve_step"), steps[0])

            def normalise(name, src):
                chained(dve.bn_stats(stats, src))
                dve.bn_aggr(mv, stats).then_inc(sem("var_ready"), 1)
                dve.wait_ge(sem("rstd_ready"), ln_at[name] + 1)
                dve.wait_ge(sem("var_ready"), ln_at[name] + 1)
                return dve.tensor_scalar(xn[:, :], src, mv[:, 0:1], rstd, ALU.subtract, ALU.mult)

            def transposed(name):
                dve.wait_ge(sem("xnT_in_psum"), layers.index(name) + 1)
                dve.tensor_copy(xnT[:, :, :],
                                ps[:, 0, 0:DM].rearrange("p (k n) -> p k n", k=KD)).then_inc(sem("xnT_ready"), 1)

            def ln(name):
                normalise(name, x[:, :]).then_inc(sem("xn_ready"), 1)
                transposed(name)

            def add_y(name_sem, value):
                dve.wait_ge(sem(name_sem), value)
                updates[0] += 1
                dve.tensor_tensor(x[:, :], x[:, :], ps[:, 0, 0:DM], ALU.add).then_inc(sem("x_updated"), 1)
                dve.wait_ge(sem("x_updated"), updates[0])

            def output_tail(name, d):
                t = tails.index(name)
                width = HEADS * d
                dve.wait_ge(sem("oT_in_psum"), t + 1)
                if width <= 512:
                    dve.tensor_copy(o_T[:, 0:width], ps[:, 6, 0:width]).then_inc(sem("oT_ready"), 1)
                else:
                    dve.tensor_copy(o_T.rearrange("p (b c) -> p b c", b=2), ps[:, 6:8, :]).then_inc(sem("oT_ready"), 1)
                if name == "L2_attn":
                    dve.wait_ge(sem("y_in_psum"), t + 1)
                    chained(dve.tensor_tensor(y[:, :], xn[:, :], ps[:, 0, 0:DM], ALU.add))
                    chained(normalise("L2_attn/post", y[:, :]))
                    chained(dve.tensor_tensor(y[:, :], xn[:, :], wide[:, 1, :], ALU.mult))
                    chained(dve.tensor_tensor(y[:, :], y[:, :], wide[:, 2, :], ALU.add))
                    chained(dve.tensor_tensor(x[:, :], x[:, :], y[:, :], ALU.add))
                else:
                    add_y("y_in_psum", t + 1)

            def gate_chunk(u):
                for s in range(2):
                    dve.wait_ge(sem(f"gate_in_slot{s}"), u * 32 + 32)
                    for e in range(EXPERTS):
                        k = s * EXPERTS + e
                        dve.wait_ge(sem("gate_sums"), u * GATE_STEPS + GATE_STEPS + k - 1)
                        dve.scalar_tensor_tensor(gate_junk[:, k % 2, :], gate_tok[:, s, :], float(e),
                                                 gate_ctx[:, s, :], ALU.is_equal, ALU.mult,
                                                 accum_out=gate_part[:, e, bass.ds(u * 2 + s, 1)]
                                                 ).then_inc(sem("gate_sums"), 1)

            def cross_attention(name):
                d = XATTN[name]
                n = x_layers.index(name)
                ln(name)
                for b in range(4 if d == 64 else 0):
                    dve.wait_ge(sem("q_high_ready"), 4 * n + b + 1)
                    part = slice(b * 512, (b + 1) * 512)
                    dve.tensor_tensor(q_lo[:, part], ps[:, (0, 1, 6, 7)[b], :], q_hi[:, part], ALU.subtract
                                      ).then_inc(sem("q_low_ready"), 1)
                first_x = name == "L0_xattn"
                if first_x:
                    dve.wait_ge(sem("key_bias_in_psum"), 1)
                    chained(dve.tensor_copy(key_bias_score, ps[:, 2, 0:HEADS]))
                if d == 16:
                    piece = of_layer[name][0]
                    dve.wait_ge(sem("wv_high_ready"), v_layers.index(name) + 1)
                    dve.tensor_tensor(wv_lo[:, :], slot(piece)[:, 512:768], wv_hi[:, :], ALU.subtract
                                      ).then_inc(sem("wv_low_ready"), 1)
                    dve.wait_ge(sem("wk_high_ready"), v_layers.index(name) + 1)
                    dve.tensor_tensor(wk_lo.rearrange("p (s r c) -> p s r c", r=3, c=32), key_weights(piece),
                                      wk_hi.rearrange("p (s r c) -> p s r c", r=3, c=32), ALU.subtract
                                      ).then_inc(sem("wk_ready"), 1)
                    dve.wait_ge(sem("q_stack_high"), 4 * (v_layers.index(name) + 1))
                    for b in range(2):
                        for half in range(2):
                            low = q_part(64, b, half)
                            last = dve.scalar_tensor_tensor(low, ps[64:STACK_W, 4 + b, :].rearrange(
                                "p (s q) -> p s q", s=4), head_scale(64, half), low, ALU.mult, ALU.subtract)
                    last.then_inc(sem("q_stack_ready"), 1)
                    dve.memset(k_stack[STACK_W:STACK_ROWS, :, :], BIAS_UNIT)
                    dve.memset(v_ring[:, :, :, VW - 1:VW], 1.0).then_inc(sem("ones_ready"), 1)
                    if name == v_layers[0]:
                        dve.sem_inc(sem("values_ready"), 1)
                        dve.sem_inc(sem("keys_ready"), 2)
                else:
                    dve.memset(ctx_rows[:, :, CD:UW], 1.0).then_inc(sem("ones_ready"), 1)
                if n == 0:
                    dve.sem_inc(sem("max_slots_free"), 2)
                    for c in range(ITERS):
                        dve.wait_ge(sem("ctx_high_made"), c + 1)
                        part = slice(c * KPI, (c + 1) * KPI)
                        dve.tensor_tensor(ctxT_lo[:, part], stage[:, c % 2, :], ctxT_hi[:, part], ALU.subtract
                                          ).then_inc(sem("ctx_low_made"), 1)

                def copy_values(c, vcount):
                    a, b = V_CHUNKS[c]
                    dve.wait_ge(sem("values_in_psum"), vcount + c + 1)
                    dve.tensor_copy(v_ring[:, a:b, :, 0:16].rearrange("p t h c -> p (t h) c"),
                                    ps[:, 7, 0:(b - a) * 64].rearrange("p (t c) -> p t c", c=16)
                                    ).then_inc(sem("values_ready"), 1)

                def low_keys(c, s, kcount):
                    dve.wait_ge(sem("keys_high_made"), kcount + BUILDS.index((c, s)) + 1)
                    part = k_stack[32:64, s, c * MCHUNK:(c + 1) * MCHUNK]
                    dve.tensor_tensor(part, ps[32:64, 4 + s, 0:MCHUNK], part, ALU.subtract
                                      ).then_inc(sem("keys_ready"), 1)

                def maximum(g, i, u):
                    c, hh = u // HPG, u % HPG
                    dve.wait_ge(sem("max_scores_ready"), (g * ITERS + i) * MUPI + n * GROUPS * ITERS * MUPI + u + 1)
                    dve.tensor_reduce(mx_part[:, hh, bass.ds(i * MCPI + c, 1)], ps[:, u % 2, 0:MCHUNK],
                                      AX.X, ALU.max).then_inc(sem("max_slots_free"), 1)

                def max_loop(g):
                    with dve.Fori(0, ITERS) as i:
                        for u in range(MUPI):
                            maximum(g, i, u)
                        if name == gate_rider and has_gate:
                            gate_chunk(g * ITERS + i)

                def stacks_loop(g, max_group):
                    with dve.Fori(0, ITERS) as i:
                        vcount, kcount = v_count(name, g, i), k_count(name, g, i)
                        units = [0]

                        def maxima(k):
                            for _ in range(k if max_group is not None else 0):
                                maximum(max_group, i, units[0])
                                units[0] += 1

                        low_keys(0, 0, kcount)
                        low_keys(0, 1, kcount)
                        maxima(2)
                        copy_values(0, vcount)
                        low_keys(1, 0, kcount)
                        for t in range(TPI):
                            if t != NO_UNIT_AFTER:
                                maxima(1)
                            if t in BUILD_AFTER:
                                low_keys(*BUILD_AFTER[t], kcount)
                            if t in VALUES_AFTER:
                                copy_values(VALUES_AFTER[t], vcount)
                        maxima(1)

                def keys_loop(g, max_group):
                    if d == 16:
                        stacks_loop(g, max_group)
                    elif max_group is not None:
                        max_loop(max_group)

                def start_group(g):
                    dve.wait_ge(sem("max_slots_free"), (n * GROUPS + g + 1) * ITERS * MUPI + 2)
                    dve.tensor_reduce(mx_group, mx_part[:, :, :], AX.X, ALU.max).then_inc(sem("group_max"), 1)
                    dve.wait_ge(sem("group_max"), n * GROUPS + g + 1)
                    if first_x:
                        kb = key_bias_score[:, bass.ds(g * HPG, HPG)]
                        dve.tensor_tensor(mx_group, mx_group, kb, ALU.add).then_inc(sem("with_key_bias"), 1)
                        dve.wait_ge(sem("with_key_bias"), g + 1)
                        dve.tensor_tensor(neg_max, kb, mx_group, ALU.subtract).then_inc(sem("neg_max_ready"), 1)
                    else:
                        dve.tensor_scalar(neg_max, mx_group, -1.0, None, ALU.mult).then_inc(sem("neg_max_ready"), 1)
                    dve.memset(ps[:, 6, 0:P] if d == 16 else ps[:, 6:8, 0:2 * UW], 0.0).then_inc(sem("u_cleared"), 1)
                    dve.wait_ge(sem("neg_max_T"), n * GROUPS + g + 1)
                    at = STACK_W if d == 16 else 0
                    rows_T = ps[at:at + HPG, 0, 0:P].unsqueeze(1).broadcast_to([HPG, HPG, P])
                    own = ident[at:at + HPG, at:at + HPG].unsqueeze(2).broadcast_to([HPG, HPG, P])
                    if d == 16:
                        dst = q_stack[at:at + HPG, bass.ds(g * GW, GW)].rearrange("p (h q) -> p h q", h=HPG)
                        last = dve.scalar_tensor_tensor(dst, rows_T, 1 / BIAS_UNIT, own, ALU.mult, ALU.mult)
                    else:
                        last = dve.tensor_tensor(bias_rows[:, :, :], rows_T, own, ALU.mult)
                    last.then_inc(sem("bias_rows_ready"), 1)

                def end_group(g):
                    dve.wait_ge(sem("step_summed"), step_base(name) + (g + 1) * ITERS * len(STEPS[d]) + CREDIT)
                    if d == 16:
                        dve.tensor_copy(u_raw[:, bass.ds(g, 1), :].rearrange("p g q -> p (g q)"), ps[:, 6, 0:P]
                                        ).then_inc(sem("u_done"), 1)
                        return
                    den = ps[:, 6:8, 0:2 * UW].rearrange("p b (h c) -> p b h c", c=UW)[:, :, :, CD]
                    dve.reciprocal(rden[:, 0:HPG].rearrange("p (b h) -> p b h", b=2), den).then_inc(sem("rden_ready"), 1)
                    dve.wait_ge(sem("rden_ready"), u_layers.index(name) * GROUPS + g + 1)
                    for hh in range(HPG):
                        last = dve.tensor_scalar(u_norm[:, bass.ds(g * GW + hh * P, P)],
                                                 ps[:, 6 + hh // 2, (hh % 2) * UW:(hh % 2) * UW + CD],
                                                 rden[:, hh:hh + 1], None, ALU.mult)
                    last.then_inc(sem("u_done"), 1)

                max_loop(0)
                if n == 0 and "L0_ffn" in layers:
                    quantise_weights()
                with dve.Fori(0, GROUPS - 1) as g:
                    start_group(g)
                    keys_loop(g, g + 1)
                    end_group(g)
                start_group(GROUPS - 1)
                keys_loop(GROUPS - 1, None)
                end_group(GROUPS - 1)
                dve.wait_ge(sem("o_in_psum"), tails.index(name) + 1)
                if d == 16:
                    sums = ps[:, 0, :].rearrange("p (h c) -> p h c", c=32)
                    ov = o_sb[:, 0:DM].rearrange("p (h c) -> p h c", c=16)
                    chained(dve.reciprocal(rden, sums[:, :, VW - 1]))
                    last = dve.tensor_tensor(ov, sums[:, :, 0:16], rden.unsqueeze(2).broadcast_to([P, HEADS, 16]),
                                             ALU.mult)
                    if first_x:
                        chained(last)
                        last = dve.tensor_tensor(o_sb[:, 0:DM], o_sb[:, 0:DM], wide[:, 3, :], ALU.add)
                    last.then_inc(sem("o_ready"), 1)
                else:
                    dve.tensor_copy(o_sb.rearrange("p (b c) -> p b c", b=2), ps[:, 0:2, :]).then_inc(sem("o_ready"), 1)
                output_tail(name, d)

            def softmax_attention(name):
                d = SATTN[name]
                a = kv_users.index(name)
                k_base = counted(kv_users, name, 4)
                ln(name)
                if name == "L0_attn":
                    dve.wait_ge(sem("sigma_exp"), 1)
                    chained(dve.tensor_scalar(sig[:, 1:2], sig[:, 0:1], 1.0, None, ALU.add))
                    chained(dve.reciprocal(sig[:, 2:3], sig[:, 1:2]))
                    dve.tensor_scalar(sig[:, 3:4], sig[:, 2:3], -(d ** -0.5), None, ALU.mult
                                      ).then_inc(sem("sigma_scale"), 1)
                for b in range(4):
                    dve.wait_ge(sem("kT_in_psum"), k_base + b + 1)
                    dve.tensor_copy(a_kT[0:d, b * 512:(b + 1) * 512], ps[0:d, (0, 1, 6, 7)[b], :]
                                    ).then_inc(sem("kT_ready"), 1)

                def by_head(ap):
                    return ap.rearrange("p (h k) -> p h k", h=4)

                for b in range(4):
                    dve.wait_ge(sem("scores_in_psum"), 4 * a + b + 1)
                    s = by_head(ps[:, 4 + b, :])
                    p_b = by_head(a_p[:, b * 512:(b + 1) * 512])
                    m_b = mx16[:, 4 * b:4 * b + 4]
                    if name != "L0_attn":
                        chained(dve.tensor_tensor(p_b, s, causal[:, :].unsqueeze(1).broadcast_to([P, 4, P]), ALU.add))
                        s = p_b
                    chained(dve.tensor_reduce(m_b, s, AX.X, ALU.max))
                    dve.tensor_tensor(p_b, s, m_b.unsqueeze(2).broadcast_to([P, 4, P]), ALU.subtract
                                      ).then_inc(sem("shifted_ready"), 1)
                for b in range(4):
                    dve.wait_ge(sem("p_ready"), 4 * a + b + 1)
                    chained(dve.tensor_reduce(den16[:, 4 * b:4 * b + 4], by_head(a_p[:, b * 512:(b + 1) * 512]),
                                              AX.X, ALU.add))
                chained(dve.reciprocal(rden, den16))
                dve.wait_ge(sem("o_in_psum"), tails.index(name) + 1)
                width = HEADS * d
                for c in range(ceil_div(width, 512)):
                    w_c = min(512, width)
                    hpc = w_c // d
                    last = dve.tensor_tensor(
                        o_sb[:, c * 512:c * 512 + w_c].rearrange("p (h e) -> p h e", h=hpc),
                        ps[:, 4 + c, 0:w_c].rearrange("p (h e) -> p h e", h=hpc),
                        rden[:, c * hpc:(c + 1) * hpc].unsqueeze(2).broadcast_to([P, hpc, d]), ALU.mult)
                last.then_inc(sem("o_ready"), 1)
                output_tail(name, d)

            def linear_attention():
                name, d = "L3_attn", 16
                a = kv_users.index(name)
                q_base, k_base = counted(q_users, name, 4), counted(kv_users, name, 4)
                ln(name)
                for m, (s_name, base, dst, banks) in enumerate(
                        (("qT_in_psum", q_base, a_qT, (2, 3, 4, 5)), ("kT_in_psum", k_base, a_kT, (0, 1, 6, 7)))):
                    for b in range(4):
                        dve.wait_ge(sem(s_name), base + b + 1)
                        dve.tensor_scalar(dst[0:d, b * 512:(b + 1) * 512], ps[0:d, banks[b], :], 0.0, None, ALU.min
                                          ).then_inc(sem("neg_part_ready"), 1)
                for m, (ready, dst, banks) in enumerate((("qT_ready", a_qT, (2, 3, 4, 5)),
                                                         ("kT_ready", a_kT, (0, 1, 6, 7)))):
                    for b in range(4):
                        dve.wait_ge(sem("exp_part_ready"), 4 * m + b + 1)
                        part = dst[0:d, b * 512:(b + 1) * 512]
                        dve.scalar_tensor_tensor(part, ps[0:d, banks[b], :], 0.0, part, ALU.max, ALU.add
                                                 ).then_inc(sem(ready + "_linear"), 1)
                v1 = a_v[:, 0:HEADS * (d + 1)].rearrange("p (h e) -> p h e", e=d + 1)
                dve.wait_ge(sem("v_in_psum"), a + 1)
                chained(dve.memset(v1[:, :, d:d + 1], 1.0))
                dve.tensor_copy(v1[:, :, 0:d], ps[:, 2, 0:HEADS * d].rearrange("p (h e) -> p h e", e=d)
                                ).then_inc(sem("v_ready_linear"), 1)
                for b in range(4):
                    dve.wait_ge(sem("scores_in_psum"), 4 * a + b + 1)
                    dve.tensor_tensor(a_p[:, b * 512:(b + 1) * 512].rearrange("p (h k) -> p h k", h=4),
                                      ps[:, 4 + b, :].rearrange("p (h k) -> p h k", h=4),
                                      keep_T[:, :].unsqueeze(1).broadcast_to([P, 4, P]), ALU.mult
                                      ).then_inc(sem("masked_ready"), 1)
                dve.wait_ge(sem("o_in_psum"), tails.index(name) + 1)
                o1 = ps[:, 0, 0:HEADS * (d + 1)].rearrange("p (h e) -> p h e", e=d + 1)
                chained(dve.reciprocal(rden, o1[:, :, d]))
                ov = o_sb[:, 0:HEADS * d].rearrange("p (h e) -> p h e", h=HEADS)
                chained(dve.tensor_tensor(ov, o1[:, :, 0:d], rden.unsqueeze(2).broadcast_to([P, HEADS, d]), ALU.mult))
                dve.tensor_scalar(o_sb[:, 0:HEADS * d], o_sb[:, 0:HEADS * d], 1e-12, None, ALU.add
                                  ).then_inc(sem("o_ready"), 1)
                output_tail(name, d)

            def quantise_weights():
                nb = 1536 // QBLOCK
                am, s_b, inv = (l0_quant[:, i * nb:(i + 1) * nb] for i in range(3))
                for i, piece in enumerate(of_layer["L0_ffn"]):
                    piece_arrived(dve, piece)
                    w = slot(piece)[:, 0:1536]
                    wb = w.rearrange("p (n b) -> p n b", b=QBLOCK)

                    def per_block(ap):
                        return ap.unsqueeze(2).broadcast_to([P, nb, QBLOCK])

                    chained(dve.tensor_reduce(am, wb, AX.X, ALU.max, apply_absolute_value=True))
                    chained(dve.tensor_scalar(s_b, am, 1.0 / 7.0, 1e-12, ALU.mult, ALU.max))
                    chained(dve.reciprocal(inv, s_b))
                    chained(dve.tensor_tensor(wb, wb, per_block(inv), ALU.mult))
                    chained(dve.tensor_scalar(w, w, MAGIC, MAGIC, ALU.add, ALU.subtract))
                    chained(dve.tensor_scalar(w, w, 7.0, -8.0, ALU.min, ALU.max))
                    dve.tensor_tensor(wb, wb, per_block(s_b), ALU.mult).then_inc(sem("w_quantised"), 1)
                    dve.wait_ge(sem("w_quantised"), i + 1)

            def quantise_16(t, z):
                dve.tensor_reduce(amax[:, z:z + 1], t, AX.X, ALU.max, apply_absolute_value=True
                                  ).then_inc(sem("amax_ready"), 1)
                dve.wait_ge(sem("amax_all_ready"), z + 1)
                s, inv = qs[:, z:z + 1], qinv[:, z:z + 1]
                chained(dve.tensor_scalar(s, amax_all[:, z:z + 1], 1.0 / 32767.0, 1e-12, ALU.mult, ALU.max))
                chained(dve.reciprocal(inv, s))
                chained(dve.tensor_scalar(t, t, inv, MAGIC, ALU.mult, ALU.add))
                chained(dve.tensor_scalar(t, t, MAGIC, 32767.0, ALU.subtract, ALU.min))
                return dve.tensor_scalar(t, t, -32768.0, s, ALU.max, ALU.mult)

            def l0_ffn():
                if not x_layers:
                    quantise_weights()
                chained(normalise("L0_ffn", x[:, :]))
                quantise_16(xn[:, :], 0).then_inc(sem("xn_ready"), 1)
                for i in range(4):
                    dve.wait_ge(sem("wT_in_psum"), i + 1)
                    m, k = i // 2, i % 2
                    b0 = 2 * i % 8
                    dve.tensor_copy(l0_wT(m)[:, k, 0:512], ps[:, b0, :])
                    dve.tensor_copy(l0_wT(m)[:, k, 512:768], ps[:, b0 + 1, 0:256]).then_inc(sem("wT_copied"), 1)
                dve.wait_ge(sem("wT_in_psum"), 5)
                dve.tensor_copy(work[:, 3072:4608].rearrange("p (b c) -> p b c", b=3), ps[:, 0:3, :]
                                ).then_inc(sem("wT_copied"), 1)
                transposed("L0_ffn")
                for m, t in enumerate((l0_gate, l0_up)):
                    dve.wait_ge(sem("gate_up_in_psum"), m + 1)
                    chained(dve.tensor_copy(t[:, 0:512], ps[:, 2 + 2 * m, :]))
                    chained(dve.tensor_copy(t[:, 512:768], ps[:, 3 + 2 * m, 0:256]))
                    if m == 0:
                        quantise_16(t, 1).then_inc(sem("l0_gate_ready"), 1)
                    else:
                        chained(quantise_16(t, 2))
                sg = l0_tmp[:, 0:768]
                s2 = l0_tmp[:, 768:1536]
                dve.wait_ge(sem("l0_exp_ready"), 1)
                chained(dve.tensor_scalar(sg, sg, 1.0, None, ALU.add))
                chained(dve.reciprocal(s2, sg))
                chained(dve.tensor_scalar(s2, s2, 65536.0, MAGIC, ALU.mult, ALU.add))
                chained(dve.tensor_scalar(s2, s2, MAGIC, 65535.0, ALU.subtract, ALU.min))
                chained(dve.tensor_scalar(s2, s2, 0.0, 1.0 / 65536.0, ALU.max, ALU.mult))
                chained(dve.tensor_tensor(l0_gate, l0_gate, s2, ALU.mult))
                chained(quantise_16(l0_gate, 3))
                chained(dve.tensor_tensor(l0_h, l0_gate, l0_up, ALU.mult))
                quantise_16(l0_h, 4).then_inc(sem("l0_h_ready"), 1)
                dve.wait_ge(sem("l0_hT_in_psum"), 1)
                dve.tensor_copy(l0_hT[:, 0:512], ps[:, 6, :])
                dve.tensor_copy(l0_hT[:, 512:768], ps[:, 7, 0:256]).then_inc(sem("l0_hT_ready"), 1)
                add_y("l0_ffn_y", 1)

            def l1_ffn():
                ln("L1_ffn")

                def scaled(dst, banks, s_name):
                    s = cols[:, COL_AT[s_name]:COL_AT[s_name] + FT].rearrange("p (b f) -> p b f", b=2)
                    for b in range(2):
                        last = dve.tensor_tensor(dst[:, b * 512:(b + 1) * 512].rearrange("p (f t) -> p f t", f=4),
                                                 ps[:, banks[b], :].rearrange("p (f t) -> p f t", f=4),
                                                 s[:, b, :].unsqueeze(2).broadcast_to([P, 4, P]), ALU.mult)
                    return last

                dve.wait_ge(sem("consts_loaded"), 16 * 10)
                dve.wait_ge(sem("swiglu_in_psum"), 1)
                scaled(f_b, (2, 3), "w1_s").then_inc(sem("w1_scaled"), 1)
                dve.wait_ge(sem("swiglu_in_psum"), 2)
                chained(scaled(f_a, (4, 5), "w2_s"))
                chained(dve.tensor_tensor(f_a, f_a, f_b, ALU.mult))
                dve.wait_ge(sem("silu_exp"), 1)
                chained(dve.tensor_scalar(f_c, f_c, 1.0, None, ALU.add))
                chained(dve.reciprocal(f_d, f_c))
                dve.tensor_tensor(f_a, f_a, f_d, ALU.mult).then_inc(sem("swiglu_ready"), 1)
                dve.wait_ge(sem("l1_ffn_y"), 1)
                chained(dve.tensor_tensor(y[:, :], ps[:, 0, 0:DM], wide[:, 0, :], ALU.mult))
                chained(dve.tensor_tensor(x[:, :], x[:, :], y[:, :], ALU.add))

            def l2_ffn():
                piece, = of_layer["L2_ffn"]
                piece_arrived(dve, piece)
                chained(dve.tensor_copy(work[:, 0:512], slot(piece)[:, 0:512].bitcast(I32)))
                dve.tensor_scalar(work[:, 0:512], work[:, 0:512], -1.0, None, ALU.add).then_inc(sem("l2f_w_ready"), 1)
                dve.wait_ge(sem("consts_loaded"), 16 * 10)
                s, inv = qscale[:, 0:1], qscale[:, 1:2]
                chained(dve.tensor_scalar(s, act_scale[:, :], 1e-5, None, ALU.max))
                chained(dve.reciprocal(inv, s))
                chained(normalise("L2_ffn", x[:, :]))
                t = xn[:, :]
                pos, neg = scratch[:, 0:DM], scratch[:, DM:2 * DM]
                big, tmp = scratch[:, 2 * DM:3 * DM], scratch[:, 3 * DM:4 * DM]
                chained(dve.tensor_scalar(t, t, inv, MAGIC, ALU.mult, ALU.add))
                chained(dve.tensor_scalar(t, t, MAGIC, 127.0, ALU.subtract, ALU.min))
                chained(dve.tensor_scalar(t, t, -127.0, s, ALU.max, ALU.mult))
                chained(dve.tensor_scalar(pos, t, 0.0, None, ALU.max))
                chained(dve.tensor_scalar(neg, t, 0.0, None, ALU.min))
                for part, over, clip, limit, value in ((pos, ALU.is_gt, ALU.min, FLT_MAX, 1e4),
                                                       (neg, ALU.is_lt, ALU.max, -FLT_MAX, -1e4)):
                    within = ALU.is_le if part is pos else ALU.is_ge
                    chained(dve.tensor_scalar(big, part, limit, value, over, ALU.mult))
                    chained(dve.tensor_scalar(tmp, part, limit, None, clip))
                    chained(dve.scalar_tensor_tensor(part, part, limit, tmp, within, ALU.mult))
                    chained(dve.tensor_tensor(part, part, big, ALU.add))
                dve.tensor_tensor(t, pos, neg, ALU.add).then_inc(sem("xn_ready"), 1)
                transposed("L2_ffn")
                add_y("l2_ffn_y", 1)

            def l3_xattn():
                if gate_rider is None:
                    with dve.Fori(0, GROUPS * ITERS) as u:
                        gate_chunk(u)
                dve.wait_ge(sem("gate_sums"), (1 + GROUPS * ITERS) * GATE_STEPS)
                chained(dve.tensor_reduce(gate[:, :], gate_part[:, :, :], AX.X, ALU.add))
                ln("L3_xattn")
                for e in range(EXPERTS):
                    dve.wait_ge(sem("expert_down"), e + 1)
                    last = dve.scalar_tensor_tensor(x[:, :], ps[:, 4 + e % 2, 0:DM], gate[:, e:e + 1], x[:, :],
                                                    ALU.mult, ALU.add)
                    last.then_inc(sem("expert_added"), 1)
                    dve.wait_ge(sem("expert_added"), e + 1)

            def l3_ffn():
                ln("L3_ffn")
                dve.wait_ge(sem("logits_in_psum"), 1)
                chained(dve.tensor_copy(logits, ps[:, 1, 0:EXPERTS]))
                chained(dve.max(top8, logits))
                chained(dve.max_index(top_i[:, :], top8, logits))
                chained(dve.tensor_copy(top_if[:, :], top_i[:, :]))
                dve.tensor_tensor(top_w[:, 0:1], top8[:, 1:2], top8[:, 0:1], ALU.subtract).then_inc(sem("top_diff"), 1)
                dve.wait_ge(sem("top_exp"), 1)
                chained(dve.tensor_scalar(top_w[:, 2:3], top_w[:, 1:2], 1.0, None, ALU.add))
                chained(dve.reciprocal(top_w[:, 2:3], top_w[:, 2:3]))
                chained(dve.tensor_tensor(top_w[:, 3:4], top_w[:, 1:2], top_w[:, 2:3], ALU.mult))
                chained(dve.memset(combine[:, EXPERTS:EXPERTS + 1], 1.0))
                chained(dve.tensor_scalar(pick, iota8[:, :], top_if[:, 1:2], top_w[:, 3:4], ALU.is_equal, ALU.mult))
                chained(dve.tensor_scalar(combine[:, 0:EXPERTS], iota8[:, :], top_if[:, 0:1], top_w[:, 2:3],
                                          ALU.is_equal, ALU.mult))
                dve.tensor_tensor(combine[:, 0:EXPERTS], combine[:, 0:EXPERTS], pick, ALU.add
                                  ).then_inc(sem("combine_ready"), 1)
                dve.wait_ge(sem("combine_T_psum"), 1)
                dve.tensor_copy(combine_T[:, :], ps[0:EXPERTS + 1, 1, 0:P]).then_inc(sem("combine_T_ready"), 1)
                dve.wait_ge(sem("moe_bias"), 1)
                chained(dve.tensor_tensor(x[:, :], x[:, :], ps[:, 1, 0:DM], ALU.add))
                for e in range(EXPERTS + 1):
                    dve.wait_ge(sem("moe_down"), e + 1)
                    dve.scalar_tensor_tensor(x[:, :], ps[:, 6 + e % 2, 0:DM], combine[:, e:e + 1], x[:, :],
                                             ALU.mult, ALU.add).then_inc(sem("moe_added"), 1)
                    dve.wait_ge(sem("moe_added"), e + 1)

            dve.wait_ge(sem("x_loaded"), 16)
            dve.wait_ge(sem("pool_consts"), 7)
            dve.wait_ge(sem("consts_loaded"), 16 * 10)
            if has_gate:
                dve.sem_inc(sem("gate_sums"), GATE_STEPS)
            for name in layers:
                if name in XATTN:
                    cross_attention(name)
                elif name in SATTN:
                    softmax_attention(name)
                else:
                    {"L0_ffn": l0_ffn, "L1_ffn": l1_ffn, "L2_ffn": l2_ffn, "L3_xattn": l3_xattn,
                     "L3_attn": linear_attention, "L3_ffn": l3_ffn}[name]()
            dve.drain().then_inc(sem("x_final"), 1)


def lay_out(a):
    a = {k: np.asarray(v) for k, v in a.items()}

    def tiles(w):
        k = w.shape[0] // P
        return np.ascontiguousarray(w.reshape(k, P, -1).transpose(1, 0, 2).reshape(P, -1))

    def per_head_T(w, d):
        return np.ascontiguousarray(w.reshape(CD, HEADS, d).transpose(2, 1, 0).reshape(d, HEADS * CD))

    def out_in(w):
        return np.ascontiguousarray(w.reshape(-1, P, w.shape[1]).transpose(1, 0, 2).reshape(P, -1))

    ctx = a["ctx_512"][0]
    row_head = (np.arange(P)[:, None] // 16) % 2
    head_half = np.where(row_head == np.arange(2)[None], 0.25, 0.0).astype(np.float32)
    d = {
        "x": a["x"][0],
        "ctxT": ctx.T,
        "ctx_rows": ctx.reshape(KT, P, CD).transpose(1, 0, 2),
        "tokT": a["itok_BxS2xS_0_7"][0].T,
        "L0x_q": tiles(a["L0_xattn_Wq"]), "L0x_v": a["L0_xattn_Wv"], "L0x_o": tiles(a["L0_xattn_Wo"]),
        "L0x_k": a["L0_xattn_Wk"], "L2x_k": a["L2_xattn_Wkv"][:DM].T,
        "L0x_kT": per_head_T(a["L0_xattn_Wk"], 16), "bkT": a["L0_xattn_bk"].reshape(HEADS, 16).T,
        "L0a_w": np.concatenate([
            tiles(np.concatenate([a["L0_attn_Wqt"], a["L0_attn_Wqs"]], 1)),
            tiles(np.concatenate([a["L0_attn_Wkt"], a["L0_attn_Wks"]], 1)),
            tiles(a["L0_attn_Wv"]), tiles(a["L0_attn_Wout"])], 1),
        "L0f_gate": out_in(a["L0_ffn_w_gate"]), "L0f_up": out_in(a["L0_ffn_w_up"]),
        "L0f_down": out_in(a["L0_ffn_w_down"]),
        "L1x_q": tiles(a["L1_xattn_Wq"]), "L1x_kT": per_head_T(a["L1_xattn_Wk"], 64),
        "L1x_v": a["L1_xattn_Wv"], "L1x_o": tiles(a["L1_xattn_Wo"]),
        "L1a_w": np.concatenate([tiles(a[f"L1_attn_{n}_proj_weight"].T) for n in "qkvo"], 1),
        "L1f_w1": tiles(a["L1_ffn_w1_w"].T), "L1f_w2": tiles(a["L1_ffn_w2_w"].T), "L1f_w3": tiles(a["L1_ffn_w3_w"].T),
        "L2x_q": tiles(a["L2_xattn_Wq"].T), "L2x_o": tiles(a["L2_xattn_Wo"].T),
        "L2x_kT": per_head_T(a["L2_xattn_Wkv"][:DM].T, 16), "L2x_v": a["L2_xattn_Wkv"][DM:].T,
        "L2f_w": tiles(a["L2_ffn_ternary_weight"].T),
        "L3a_w": np.concatenate([tiles(a[f"L3_attn_W{n}"].T) for n in "qkvo"], 1),
        "w3_s": a["L1_ffn_w3_s"], "gamma": a["L2_attn_gamma"], "beta": a["L2_attn_beta"],
        "bv": a["L0_xattn_bv"],
        "w_sigma": a["L0_attn_w_sigma"].reshape(1), "act_scale": a["L2_ffn_act_scale"].reshape(1),
        "b2": np.concatenate([a["L3_ffn_b2"], a["L3_ffn_bs2"][None]], 0),
        "rows": np.concatenate([a["L0_xattn_bq"], a["L0_xattn_bo"], a["L0_attn_bout"],
                                a["L1_xattn_bo"], a["L2_ffn_bias"], a["L3_ffn_gate_b"]])[None],
        "cols": np.concatenate([
            *[a[f"L1_ffn_{n}"].reshape(FT, P).T for n in ("w1_s", "w2_s", "h1_s", "h2_s")],
            a["L3_ffn_b1"].reshape(EXPERTS * FT, P).T, a["L3_ffn_bs1"].reshape(FT, P).T,
            tiles(a["L3_ffn_gate_w"]), head_half], 1),
    }
    for m in ("h1", "h2"):
        w = a[f"L1_ffn_{m}_w"].T
        for i in range(4):
            d[f"L1f_{m}_{i}"] = tiles(w[:, i * 256:(i + 1) * 256])
    for n in "qkv":
        d[f"L2a_{n}"] = tiles(a[f"L2_attn_W{n}"].transpose(1, 0, 2).reshape(DM, -1))
    d["L2a_o"] = tiles(a["L2_attn_Wo"])
    for e in range(EXPERTS):
        d[f"L3x_in{e}"] = tiles(a["L3_xattn_proj_in"][e].T)
        d[f"L3x_out{e}"] = tiles(a["L3_xattn_proj_out"][e].T)
        d[f"L3f_w1_{e}"], d[f"L3f_w2_{e}"] = tiles(a["L3_ffn_w1"][e]), tiles(a["L3_ffn_w2"][e])
    d[f"L3f_w1_{EXPERTS}"], d[f"L3f_w2_{EXPERTS}"] = tiles(a["L3_ffn_ws1"]), tiles(a["L3_ffn_ws2"])
    return {k: np.ascontiguousarray(v) for k, v in d.items()}


def kernel(**inputs):
    import concourse.bacc as bacc
    from concourse.bass_utils import run_bass_kernel_spmd

    arrays = {f"in_{k}": v for k, v in lay_out(inputs).items()}
    nc = bacc.Bacc("TRN2", target_bir_lowering=False, num_devices=1)
    dram = {k[3:]: nc.dram_tensor(k, v.shape, mybir.dt.from_np(v.dtype), kind="ExternalInput").ap()
            for k, v in arrays.items()}
    out = nc.dram_tensor("out", (P, DM), F32, kind="ExternalOutput").ap()
    build_program(nc, dram, out)
    result = run_bass_kernel_spmd(nc, [arrays], core_ids=[0])
    return result.results[0]["out"].reshape(1, P, DM)
```

```python
from contextlib import ExitStack

import numpy as np

import concourse.bass as bass
from concourse import mybir

ALU = mybir.AluOpType
ACT = mybir.ActivationFunctionType
AX = mybir.AxisListType
F32 = mybir.dt.float32
F16 = mybir.dt.float16
BF16 = mybir.dt.bfloat16
I32 = mybir.dt.int32
U32 = mybir.dt.uint32
RMAX = bass.bass_isa.ReduceOp.max


def ceil_div(a, b):
    return -(-a // b)


P = 128
DM = 256
KD = DM // P
HEADS = 16
KEYS = 12544
CD = 128
KT = KEYS // P
GROUPS = 4
HPG = HEADS // GROUPS
GW = HPG * P
ITERS = 7
TPI = KT // ITERS
KPI = KEYS // ITERS
MCHUNK = 448
MCPI = KPI // MCHUNK
MUPI = MCPI * HPG
DIRECT, DIRECT_BANKS = (3, 6), (6, 4)
FOLDED, FOLDED_BANKS = (0, 1, 2, 4, 5, 7), (0, 2)
NF = len(FOLDED)
UW = CD + 1
RW = 2 * CD + 1
PROB_SHIFT = float(np.log(256.0))
S_BANKS = {16: 2, 64: 4}
P_SLOTS = {16: 8, 64: 4}
SUM_LAG = 2
TWO_UNITS_AFTER = 6
CREDIT = 8
STACKS = HEADS // 2
STACK_W = 3 * 32
STACK_ROWS = STACK_W + HPG
BIAS_UNIT = 64.0
BUILDS = [(c, s) for c in range(MCPI) for s in range(2)]
BUILD_AFTER = {0: (1, 1), 2: (2, 0), 3: (2, 1), 5: (3, 0), 6: (3, 1)}
VALUES_AFTER = {1: 1, 4: 2}
NO_UNIT_AFTER = 2
GHALF = MCHUNK // 2
VW = 17
V_CHUNKS = [(0, 4), (4, 9), (9, 14)]
EXPERTS = 8
GATE_STEPS = 2 * EXPERTS
HID = 1024
FT = HID // P
L0_HID = 768
XHID = 512
QBLOCK = 32
QSLICE = ceil_div(1536 // QBLOCK, ITERS)
QSTEPS = 7
MAGIC = 12582912.0
MASKED = -1e30
FLT_MAX = 3.4028234663852886e38
PIECE = 2048
RING_A = 6
RING_B = 12
FREE_FROM = 24

XATTN = {"L0_xattn": 16, "L1_xattn": 64, "L2_xattn": 16}
SATTN = {"L0_attn": 16, "L1_attn": 16, "L2_attn": 64}
LAYERS = ["L0_xattn", "L0_attn", "L0_ffn", "L1_xattn", "L1_attn", "L1_ffn",
          "L2_xattn", "L2_attn", "L2_ffn", "L3_xattn", "L3_attn", "L3_ffn"]

PIECES = [
    ("L0_xattn", [("L0x_q", 0, P, 512), ("L0x_v", 512, P, 256), ("L0x_o", 768, P, 512),
                  ("L0x_k", 1280, P, 256)]),
    ("L0_xattn", [("L0x_kT", 0, 32, 1024)]),
    ("L0_attn", [("L0a_w", 0, P, 2048)]),
    ("L0_ffn", [("L0f_gate", 0, P, 1536)]),
    ("L0_ffn", [("L0f_up", 0, P, 1536)]),
    ("L0_ffn", [("L0f_down", 0, P, 1536)]),
    ("L1_xattn", [("L1x_q", 0, P, 2048)]),
    ("L1_xattn", [("L1x_kT", 0, P, 1024)]),
    ("L1_xattn", [("L1x_v", 0, P, 1024)]),
    ("L1_xattn", [("L1x_o", 0, P, 2048)]),
    ("L1_attn", [("L1a_w", 0, P, 2048)]),
    ("L1_ffn", [("L1f_w1", 0, P, 2048)]),
    ("L1_ffn", [("L1f_w2", 0, P, 2048)]),
    *[("L1_ffn", [(f"L1f_h1_{i}", 0, P, 2048)]) for i in range(4)],
    *[("L1_ffn", [(f"L1f_h2_{i}", 0, P, 2048)]) for i in range(4)],
    ("L1_ffn", [("L1f_w3", 0, P, 2048)]),
    ("L2_xattn", [("L2x_q", 0, P, 512), ("L2x_v", 512, P, 256), ("L2x_o", 768, P, 512),
                  ("L2x_k", 1280, P, 256)]),
    ("L2_xattn", [("L2x_kT", 0, 32, 1024)]),
    *[("L2_attn", [(f"L2a_{n}", 0, P, 2048)]) for n in "qkvo"],
    ("L2_ffn", [("L2f_w", 0, P, 512)]),
    *[("L3_xattn", [(f"L3x_in{e}", 0, P, 1024), (f"L3x_out{e}", 1024, P, 1024)]) for e in range(EXPERTS)],
    ("L3_attn", [("L3a_w", 0, P, 2048)]),
    *[("L3_ffn", [(f"L3f_w{w}_{e}", 0, P, 2048)]) for e in range(EXPERTS + 1) for w in (1, 2)],
]

ROWS = {"bq": 256, "L0x_bo": 256, "bout": 256, "L1x_bo": 256, "L2f_bias": 256, "gate_b": 8}
ROW_AT = {n: sum(list(ROWS.values())[:i]) for i, n in enumerate(ROWS)}
COLS = {"w1_s": FT, "w2_s": FT, "h1_s": FT, "h2_s": FT, "b1": FT * (EXPERTS + 1), "w_gate": KD * EXPERTS, "head_half": 2}
COL_AT = {n: sum(list(COLS.values())[:i]) for i, n in enumerate(COLS)}
N_ROW, N_COL = sum(ROWS.values()), sum(COLS.values())
WIDE = ["w3_s", "gamma", "beta", "bv"]


def build_program(nc, dram, out, layers=LAYERS):
    ctx = ExitStack()
    with ctx:
        def sb(name, shape, dt=F32):
            return ctx.enter_context(nc.sbuf_tensor(name, shape, dt))

        sems = {}

        def sem(name):
            if name not in sems:
                sems[name] = ctx.enter_context(nc.semaphore(name))
            return sems[name]

        ctx_mem = sb("ctx_mem", [P, 2 * KEYS // 2 + KT * RW // 2])
        ctxT_hi = ctx_mem[:, 0:KEYS // 2].bitcast(F16)
        ctxT_lo = ctx_mem[:, KEYS // 2:KEYS].bitcast(F16)
        ctx_flat = ctx_mem[:, KEYS:]
        rows_flat = ctx_mem[:, KEYS:KEYS + KT * RW // 2].bitcast(F16)
        ctx_rows = rows_flat.rearrange("p (t c) -> p t c", c=RW)
        ring_a = sb("weight_ring", [P, RING_A, PIECE])
        work = sb("work", [P, 9216])
        gate_ctx = sb("gate_ctx", [P, 2, GHALF])
        gate_tok = sb("gate_tok", [P, 2, GHALF], I32)
        gate_part = sb("gate_part", [P, EXPERTS, 2 * GROUPS * ITERS])
        gate = sb("gate", [P, EXPERTS])
        wv_hi = sb("wv_hi", [P, DM], F16)
        wv_lo = sb("wv_lo", [P, DM], F16)
        x = sb("x", [P, DM])
        xn = sb("xn", [P, DM])
        y = sb("y", [P, DM])
        xnT = sb("xnT", [P, KD, P])
        ident = sb("ident", [P, P])
        causal = sb("causal", [P, P])
        keep_T = sb("keep_T", [P, P])
        ones_row = sb("ones_row", [1, P])
        bias_unit = sb("bias_unit", [HPG, P], F16)
        iota8 = sb("iota8", [P, EXPERTS])
        minus_half = sb("minus_half", [P, 1])
        rows = sb("rows", [1, N_ROW])
        cols = sb("cols", [P, N_COL])
        wide = sb("wide", [P, len(WIDE), DM])
        b2 = sb("b2", [EXPERTS + 1, DM])
        bkT = sb("bkT", [32, HEADS // 2])
        w_sigma = sb("w_sigma", [P, 1])
        act_scale = sb("act_scale", [P, 1])
        tiny = sb("tiny", [P, 160])
        stats, mv = tiny[:, 0:6], tiny[:, 6:8]
        veps, rstd = tiny[:, 8:9], tiny[:, 9:10]
        mx_group, neg_max = tiny[:, 10:14], tiny[:, 14:18]
        rden = tiny[:, 18:34]
        mx16, den16 = tiny[:, 34:50], tiny[:, 50:66]
        sig = tiny[:, 66:69]
        sig_half = tiny[:, 148:150]
        table_cell = tiny[:, 150:153]
        amax, qs, qinv = tiny[:, 70:75], tiny[:, 75:80], tiny[:, 80:85]
        amax_all = tiny[:, 85:90]
        top8 = tiny[:, 90:98]
        top_w = tiny[:, 98:102]
        combine = tiny[:, 102:102 + EXPERTS + 1]
        qscale = tiny[:, 112:114]
        key_bias_score = tiny[:, 116:132]
        logits = tiny[:, 132:140]
        pick = tiny[:, 140:148]
        top_i = sb("top_i", [P, 8], U32)
        top_if = sb("top_if", [P, 8])
        mx_part = sb("mx_part", [P, HPG, MCPI * ITERS])
        bias_rows = sb("bias_rows", [HPG, HPG, P], F16)
        quant_scales = gate_part[:, :, :].rearrange("p e c -> p (e c)")[:, 0:9 * QSLICE].rearrange(
            "p (v m n) -> p v m n", v=3, m=3)
        combine_T = work[0:EXPERTS + 1, 8192:8192 + P]
        ps = ctx.enter_context(nc.psum_tensor("ps", [P, 8, 512], F32))

        probs = work[:, 0:4096]
        p_wide = work[:, 0:2048].rearrange("p (s c) -> p s c", s=4)
        p_hi = work[:, 2048:3072].bitcast(F16)
        p_lo = work[:, 3072:4096].bitcast(F16)
        run_max = work[:, 4096:4992].bitcast(BF16).rearrange("p (h k) -> p h k", h=HPG)
        copied = work[:, 4992:5888].bitcast(BF16).rearrange("p (s h k) -> p s h k", s=2, h=2)
        u_norm = work[:, 4096:6144]
        x_qT = work[:, 4096:6144]
        q_hi = work[:, 6144:7168].bitcast(F16)
        q_lo = work[:, 7168:8192].bitcast(F16)
        u_T = work[:, 0:2048]
        gate_junk = work[:, 8192:8192 + 2 * GHALF].rearrange("p (s c) -> p s c", s=2)
        v_ring = work[:, 8192:8192 + TPI * HPG * VW].rearrange("p (t h c) -> p t h c", t=TPI, h=HPG)
        k_stack = ctx_flat[:, 0:KPI].bitcast(F16).rearrange("p (s k) -> p s k", s=2)
        q_stack = ctx_flat[:, KPI:KPI + 1024].bitcast(F16)
        wk_size = STACKS * STACK_W // 2
        wk_hi, wk_lo = (ctx_flat[:, KPI + 1024 + m * wk_size:KPI + 1024 + (m + 1) * wk_size].bitcast(F16)
                        for m in range(2))
        kT_at = KPI + 1024 + 2 * wk_size
        kT_16 = ctx_flat[0:32, kT_at:kT_at + STACKS * P // 2].bitcast(F16)
        wq_at = kT_at + STACKS * P // 2 + STACKS // 2
        w_q3 = ctx_flat[:, wq_at:wq_at + KD * STACKS * STACK_W]
        bq_3 = ctx_flat[0:1, wq_at + KD * STACKS * STACK_W:wq_at + (KD + 1) * STACKS * STACK_W]
        bk_16 = ctx_flat[0:32, kT_at + STACKS * P // 2:kT_at + STACKS * P // 2 + STACKS // 2].bitcast(F16)
        u_raw = work[:, 4096:4608].rearrange("p (g q) -> p g q", g=GROUPS)
        a_qT, a_kT = work[:, 0:2048], work[:, 2048:4096]
        a_v = work[:, 4096:5120]
        linear_q = work[:, 512:768]
        a_p, a_pT = work[:, 5120:7168], work[:, 7168:9216]
        o_sb = work[:, 2048:3072]
        o_T = work[:, 3072:4096]
        stage = work[:, 0:2 * KPI].rearrange("p (s c) -> p s c", s=2)

        def l0_wT(m):
            return work[:, m * 1536:(m + 1) * 1536].rearrange("p (k n) -> p k n", k=KD)

        l0_down = work[:, 3072:4608].rearrange("p (k n) -> p k n", k=6)
        l0_gate, l0_up = work[:, 4608:5376], work[:, 5376:6144]
        l0_h = work[:, 6144:6912]
        l0_hT = work[:, 6912:7680]
        l0_tmp = work[:, 7680:9216]
        f_a, f_b, f_c = work[:, 0:1024], work[:, 1024:2048], work[:, 2048:3072]
        f_d = work[:, 3072:4096]
        l2f_w = work[:, 0:512].rearrange("p (k n) -> p k n", k=KD)
        e_relu = work[:, 0:1024].rearrange("p (s n) -> p s n", s=2)
        m_h = work[:, 0:2048].rearrange("p (s n) -> p s n", s=2)
        scratch = work[:, 8192:9216]

        def stage_rows(c):
            return stage[:, c % 2, :].rearrange("p (t c) -> p t c", c=CD)

        def key_weights(piece):
            w = slot(piece)[:, 1280:1536].rearrange("p (s c) -> p s c", c=32)
            return w.unsqueeze(2).broadcast_to([P, STACKS, 3, 32])

        def q_part(row, b, half):
            return q_stack[row:STACK_W, b * 1024:(b + 1) * 1024].rearrange(
                "p (s h q) -> p s h q", h=2, q=P)[:, :, half, :]

        half_scale = cols[:, COL_AT["head_half"]:COL_AT["head_half"] + 2]

        def head_scale(row, half):
            at = COL_AT["head_half"] + half
            return cols[row:STACK_W, at:at + 1]

        block = ctx.enter_context(nc.Block())

        x_layers = [n for n in layers if n in XATTN]
        v_layers = [n for n in x_layers if XATTN[n] == 16]
        u_layers = [n for n in x_layers if XATTN[n] == 64]
        n_before_u = layers.index(u_layers[0]) if u_layers else 0
        tails = [n for n in layers if n in XATTN or n in SATTN or n == "L3_attn"]
        ln_at = {}
        for n in layers:
            ln_at[n] = len(ln_at)
            if n == "L2_attn":
                ln_at["L2_attn/post"] = len(ln_at)
        q_users = [n for n in layers if XATTN.get(n) == 64 or n in SATTN or n == "L3_attn"]
        kv_users = [n for n in layers if n in SATTN or n == "L3_attn"]
        pieces = [p for p in PIECES if p[0] in layers]
        of_layer = {n: [i for i, p in enumerate(pieces) if p[0] == n] for n in layers}
        free_from = min([i for i, p in enumerate(pieces) if PIECES.index(p) >= FREE_FROM], default=len(pieces))
        has_gate = "L3_xattn" in layers
        gate_rider = "L1_xattn" if "L1_xattn" in layers else None

        slot_of, last_in, before = [], {}, []
        for i in range(len(pieces)):
            if i < free_from:
                s = i % RING_A
            else:
                k = i - free_from
                order = [(free_from + j) % RING_A for j in range(RING_A)] + [RING_A + j for j in range(RING_B)]
                s = order[k % len(order)]
            slot_of.append(s)
            before.append(last_in.get(s))
            last_in[s] = i
        arrivals, slot_count = [], {}
        for i, (_, parts) in enumerate(pieces):
            slot_count[slot_of[i]] = slot_count.get(slot_of[i], 0) + 16 * len(parts)
            arrivals.append(slot_count[slot_of[i]])

        def slot(i):
            s = slot_of[i]
            if s < RING_A:
                return ring_a[:, s, :]
            return ctx_mem[:, (s - RING_A) * PIECE:(s - RING_A + 1) * PIECE]

        def piece_arrived(eng, i):
            eng.wait_ge(sem(f"piece_in_slot{slot_of[i]}"), arrivals[i])

        def last_use(i):
            layer = pieces[i][0]
            k = i - of_layer[layer][0]
            if layer in tails:
                return sem("y_in_psum"), tails.index(layer) + 1
            if layer == "L1_ffn" and k < 2:
                return sem("swiglu_in_psum"), k + 1
            if layer == "L1_ffn" and k < 10:
                return sem("hidden_in_psum"), (k - 2) // 2 + 1
            if layer == "L3_xattn":
                return sem("expert_down"), k + 1
            if layer == "L3_ffn":
                return (sem("moe_down"), k // 2 + 1) if k % 2 else (sem("moe_up"), k + 2)
            return {"L0_ffn": sem("l0_ffn_y"), "L1_ffn": sem("l1_ffn_y"), "L2_ffn": sem("l2_ffn_y")}[layer], 1

        def v_count(name, g, i):
            return ((v_layers.index(name) * GROUPS + g) * ITERS + i) * len(V_CHUNKS)

        def step_base(name):
            return x_layers.index(name) * GROUPS * KT

        def k_count(name, g, i):
            return ((v_layers.index(name) * GROUPS + g) * ITERS + i) * len(BUILDS)

        def steps_since(t, slots):
            return slots if t >= slots else TPI - (TPI - 1 - t) // slots * slots

        def width_banks(name):
            return ceil_div(HEADS * {**XATTN, **SATTN}.get(name, 16), 512)

        def counted(names, layer):
            return sum(width_banks(m) for m in names[:names.index(layer)])

        def head_at(d, place):
            if d == 64:
                return place % 8 * 2 + place // 8
            return place % 4 // 2 * 8 + place // 4 * 2 + place % 2

        def head_rows(t, d, h, halves):
            if d == 64:
                return t[h % 2 * d:(h % 2 + 1) * d, h // 2 * P:(h // 2 + 1) * P]
            row, col = h % 8 // 2 * 32, (h // 8 * 2 + h % 2 if halves else h // 8) * P
            return t[row:row + 32, col:col + P]

        @block.sync
        def _(sp):
            def load_piece(i):
                if before[i] is not None:
                    sp.wait_ge(*last_use(before[i]))
                if slot_of[i] >= RING_A and x_layers:
                    sp.wait_ge(sem("u_done"), GROUPS * len(x_layers))
                for name, at, r, c in pieces[i][1]:
                    dst = slot(i)[0:r, at:at + c]
                    if name == "L2f_w":
                        dst = dst.bitcast(I32)
                    sp.dma_start(dst, dram[name]).then_inc(sem(f"piece_in_slot{slot_of[i]}"), 16)

            sp.dma_start(x[:, :], dram["x"]).then_inc(sem("x_loaded"), 16)
            consts = [(rows[:, :], "rows"), (cols[:, :], "cols"), (b2[:, :], "b2"), (bkT[:, :], "bkT")]
            for dst, name in consts:
                sp.dma_start(dst, dram[name]).then_inc(sem("consts_loaded"), 16)
            for i, name in enumerate(WIDE):
                sp.dma_start(wide[:, i, :], dram[name].partition_broadcast(P)).then_inc(sem("consts_loaded"), 16)
            for dst, name in ((w_sigma, "w_sigma"), (act_scale, "act_scale")):
                sp.dma_start(dst[:, :], dram[name].partition_broadcast(P)).then_inc(sem("consts_loaded"), 16)
            first = min(2, len(pieces))
            for i in range(first):
                load_piece(i)
            if x_layers:
                for c in range(ITERS):
                    if c >= 2:
                        sp.wait_ge(sem("ctx_low_made"), c - 1)
                    sp.dma_start(stage[:, c % 2, :], dram["ctxT"][:, c * KPI:(c + 1) * KPI]).then_inc(
                        sem(f"ctxT_staged{c % 2}"), 16)
            done = min(RING_A, len(pieces))
            for i in range(first, done):
                load_piece(i)
            def stream_gate():
                with sp.Fori(0, GROUPS * ITERS) as u:
                    for s in range(2):
                        sp.wait_ge(sem("gate_sums"), u * GATE_STEPS + (s + 1) * EXPERTS)
                        for dst, name in ((gate_ctx, "ctxT"), (gate_tok, "tokT")):
                            sp.dma_start(dst[:, s, :], dram[name][:, bass.ds(u * MCHUNK + s * GHALF, GHALF)]
                                         ).then_inc(sem(f"gate_in_slot{s}"), 16)

            stop = min(of_layer[gate_rider][-1] + 3, len(pieces)) if gate_rider else done
            for i in range(done, stop):
                load_piece(i)
            if u_layers:
                if n_before_u:
                    sp.wait_ge(sem("l0_ffn_y"), 1)
                sp.wait_ge(sem("ctx_low_made"), ITERS)
                for c in range(ITERS):
                    if c >= 2:
                        sp.wait_ge(sem("rows_low_made"), c - 1)
                    sp.dma_start(stage_rows(c), dram["ctx_rows"][:, c * TPI:(c + 1) * TPI, :]
                                 ).then_inc(sem(f"rows_staged{c % 2}"), 16)
            if has_gate:
                stream_gate()
            for i in range(max(done, stop), len(pieces)):
                load_piece(i)
            sp.wait_ge(sem("x_final"), 1)
            sp.dma_start(out, x[:, :]).then_inc(sem("stored"), 16)
            sp.wait_ge(sem("stored"), 16)

        @block.gpsimd
        def _(pool):
            made = [0]

            def chained(ins):
                made[0] += 1
                ins.then_inc(sem("pool_step"), 1)
                pool.wait_ge(sem("pool_step"), made[0])

            chained(pool.memset(ident[:, :], 0.0))
            chained(pool.memset(causal[:, :], 0.0))
            chained(pool.memset(keep_T[:, :], 1.0))
            pool.memset(minus_half[:, :], -0.5).then_inc(sem("pool_consts"), 1)
            pool.memset(ones_row[:, :], 1.0).then_inc(sem("pool_consts"), 1)
            pool.memset(bias_unit[:, :], BIAS_UNIT).then_inc(sem("pool_consts"), 1)
            pool.iota(iota8[:, :], [[1, EXPERTS]], base=0, channel_multiplier=0,
                      allow_small_or_imprecise_dtypes=True).then_inc(sem("pool_consts"), 1)
            pool.affine_select(out=ident[:, :], in_=ident[:, :], compare_op=ALU.not_equal, fill=1.0, base=0,
                               pattern=[[-1, P]], channel_multiplier=1).then_inc(sem("pool_consts"), 1)
            pool.affine_select(out=causal[:, :], in_=causal[:, :], compare_op=ALU.is_ge, fill=MASKED, base=0,
                               pattern=[[-1, P]], channel_multiplier=1).then_inc(sem("pool_consts"), 1)
            pool.affine_select(out=keep_T[:, :], in_=keep_T[:, :], compare_op=ALU.is_ge, fill=0.0, base=0,
                               pattern=[[1, P]], channel_multiplier=-1).then_inc(sem("pool_consts"), 1)

            def layernorm(name):
                pool.wait_ge(sem("var_ready"), ln_at[name] + 1)
                eps = 1e-3 if name == "L2_attn/post" else 1e-5
                chained(pool.tensor_scalar(veps, mv[:, 1:2], eps, None, ALU.add))
                pool.tensor_tensor(rstd, veps, minus_half[:, :], ALU.pow).then_inc(sem("rstd_ready"), 1)

            pool.wait_ge(sem("pool_consts"), 7)
            for name in layers:
                layernorm(name)
                if name in x_layers[:1]:
                    for c in range(ITERS):
                        pool.wait_ge(sem("ctx_high_made"), c + 1)
                        part = slice(c * KPI, (c + 1) * KPI)
                        pool.tensor_tensor(ctxT_lo[:, part], stage[:, c % 2, :], ctxT_hi[:, part], ALU.subtract
                                           ).then_inc(sem("ctx_low_made"), 1)
                if name in XATTN and XATTN[name] == 64:
                    for c in range(ITERS):
                        pool.wait_ge(sem("rows_high_made"), c + 1)
                        tiles_c = ctx_rows[:, c * TPI:(c + 1) * TPI, :]
                        pool.tensor_tensor(tiles_c[:, :, 0:CD], stage_rows(c), tiles_c[:, :, CD:2 * CD], ALU.subtract
                                           ).then_inc(sem("rows_low_made"), 1)
                if name == "L2_attn":
                    layernorm("L2_attn/post")
                if name == "L0_ffn":
                    for z in range(5):
                        pool.wait_ge(sem("amax_ready"), z + 1)
                        pool.partition_all_reduce(amax_all[:, z:z + 1], amax[:, z:z + 1], P, RMAX
                                                  ).then_inc(sem("amax_all_ready"), 1)

        @block.tensor
        def _(pe):
            def transpose_xn(name):
                pe.wait_ge(sem("xn_ready"), layers.index(name) + 1)
                for k in range(KD):
                    last = pe.transpose(ps[:, 0, k * P:(k + 1) * P], xn[:, k * P:(k + 1) * P], ident[:, :])
                last.then_inc(sem("xnT_in_psum"), 1)
                pe.wait_ge(sem("xnT_ready"), layers.index(name) + 1)

            def heads_T(w, d, bank, done):
                blocks = HEADS * d // P
                for m in range(blocks):
                    for k in range(KD):
                        last = pe.matmul(ps[:, bank + m // 4, m % 4 * P:(m % 4 + 1) * P], w[:, k, m * P:(m + 1) * P],
                                         xnT[:, k, :], start=(k == 0), stop=(k == KD - 1))
                    if m % 4 == 3 or m == blocks - 1:
                        last.then_inc(sem(done), 1)

            def output_tail(name, d, w_o, bias):
                t = tails.index(name)
                nk = HEADS * d // P
                pe.wait_ge(sem("o_ready"), t + 1)
                for k in range(nk):
                    last = pe.transpose(ps[:, 6 + k // 4, (k % 4) * P:(k % 4 + 1) * P],
                                        o_sb[:, k * P:(k + 1) * P], ident[:, :])
                last.then_inc(sem("oT_in_psum"), 1)
                pe.wait_ge(sem("oT_ready"), t + 1)
                if bias is not None:
                    pe.matmul(ps[:, 0, 0:DM], ones_row[:, :], bias, start=True, stop=False)
                for k in range(nk):
                    last = pe.matmul(ps[:, 0, 0:DM], o_T[:, k * P:(k + 1) * P], w_o[:, k, :],
                                     start=(k == 0 and bias is None), stop=(k == nk - 1))
                last.then_inc(sem("y_in_psum"), 1)

            def row(name):
                return rows[:, ROW_AT[name]:ROW_AT[name] + ROWS[name]]

            def cross_attention(name):
                d = XATTN[name]
                n = x_layers.index(name)
                q_base = counted(q_users, name) if d == 64 else None
                pcs = of_layer[name]
                if len(pcs) == 2:
                    q_piece, k_piece = pcs
                    w = slot(q_piece)
                    w_q = w[:, 0:512].rearrange("p (k n) -> p k n", k=KD)
                    w_v, w_o = w[:, 512:768], w[:, 768:1280].rearrange("p (k n) -> p k n", k=2)
                else:
                    q_piece, k_piece, v_piece, o_piece = pcs
                    w_q = slot(q_piece).rearrange("p (k n) -> p k n", k=KD)
                    w_v, w_o = slot(v_piece)[:, 0:1024], slot(o_piece).rearrange("p (k n) -> p k n", k=8)
                first_x = name == "L0_xattn"
                transpose_xn(name)
                piece_arrived(pe, q_piece)
                if d == 16:
                    v = v_layers.index(name)
                    pe.wait_ge(sem("w_q3_ready"), v + 1)
                    for s in range(STACKS):
                        dst = ps[0:STACK_W, 4 + s // 4, (s % 4) * P:(s % 4 + 1) * P]
                        for k in range(KD):
                            at = (k * STACKS + s) * STACK_W
                            last = pe.matmul(dst, w_q3[:, at:at + STACK_W], xnT[:, k, :], start=(k == 0),
                                             stop=(k == KD - 1 and not first_x))
                        if first_x:
                            last = pe.matmul(dst, bq_3[:, s * STACK_W:(s + 1) * STACK_W], ones_row[:, :],
                                             start=False, stop=True)
                        if s % 4 == 3:
                            last.then_inc(sem("q_stack_in_psum"), 1)
                    pe.wait_ge(sem("kT_rounded"), v + 1)
                    for s in range(STACKS):
                        if s % 4 == 0:
                            pe.wait_ge(sem("q_stack_high"), 4 * v + s // 2 + 2)
                        last = pe.matmul(ps[:, (0, 1, 6, 7)[s // 2], s % 2 * 2 * P:(s % 2 + 1) * 2 * P],
                                         kT_16[:, s * P:(s + 1) * P], q_stack[0:32, s * 2 * P:(s + 1) * 2 * P],
                                         start=True, stop=True)
                        if s % 2 == 1:
                            last.then_inc(sem("absorbed_in_psum"), 1)
                    if first_x:
                        for h in range(HEADS):
                            last = pe.matmul(ps[:, 2, h:h + 1], q_stack[0:32, h * P:(h + 1) * P],
                                             bk_16[:, h // 2:h // 2 + 1], start=True, stop=True)
                        last.then_inc(sem("key_bias_in_psum"), 1)
                        pe.wait_ge(sem("key_bias_read"), 1)
                    pe.wait_ge(sem("q_stack_ready"), v + 1)
                else:
                    heads_T(w_q, d, 4, "qT_in_psum")
                    piece_arrived(pe, k_piece)
                    w_kT = slot(k_piece)[:, 0:1024]
                    pe.wait_ge(sem("qT_ready"), q_base + 2)
                    for place in range(HEADS):
                        h = head_at(d, place)
                        last = pe.matmul(ps[:, (0, 1, 6, 7)[place // 4], place % 4 * P:(place % 4 + 1) * P],
                                         head_rows(w_kT, d, h, False), head_rows(x_qT, d, h, False),
                                         start=True, stop=True)
                        if place % 4 == 3:
                            last.then_inc(sem("absorbed_in_psum"), 1)
                    pe.wait_ge(sem("q_low_ready"), 4 * (u_layers.index(name) + 1))
                pe.wait_ge(sem("q_high_ready"), 4 * (n + 1))

                def max_unit(g, i, u, count):
                    c, hh = u // HPG, u % HPG
                    pe.wait_ge(sem("max_slots_free"), count + u + 1)
                    pe.matmul(ps[:, u % 2, 0:MCHUNK], q_hi[:, bass.ds(g * GW + hh * P, P)],
                              ctxT_hi[:, bass.ds(i * KPI + c * MCHUNK, MCHUNK)], start=True, stop=True
                              ).then_inc(sem("max_scores_ready"), 1)

                def bias_transpose(g):
                    pe.wait_ge(sem("neg_max_ready"), n * GROUPS + g + 1)
                    if d == 16:
                        last = pe.matmul(ps[STACK_W:STACK_ROWS, 0, 0:P], neg_max, ident[:, :], start=True, stop=True)
                    else:
                        last = pe.transpose(ps[0:HPG, 0, 0:P], neg_max, ident[:, :])
                    last.then_inc(sem("neg_max_T"), 1)

                def scores(g, i, t, count):
                    pe.wait_ge(sem("step_exp_done"), count + t + 1 - steps_since(t, S_BANKS[d]) + CREDIT)
                    dst = ps[:, 2 + t % S_BANKS[d], :]
                    key = (i * TPI + t) * P
                    hi, lo = ctxT_hi[:, bass.ds(key, P)], ctxT_lo[:, bass.ds(key, P)]
                    qh, ql = q_hi[:, bass.ds(g * GW, GW)], q_lo[:, bass.ds(g * GW, GW)]
                    pe.matmul(dst, hi, qh, start=True, stop=False)
                    pe.matmul(dst, hi, ql, start=False, stop=False)
                    pe.matmul(dst, lo, qh, start=False, stop=False)
                    pe.matmul(dst, bias_unit[:, :], bias_rows[:, :, :].rearrange("p a b -> p (a b)"),
                              start=False, stop=True).then_inc(sem("step_scores_ready"), 1)

                def sum_up(i, t, count):
                    pe.wait_ge(sem("step_low_ready"), count - step_base(name) + t + 1)
                    at_t = (i * TPI + t) * RW
                    for hh in range(HPG):
                        at = t % P_SLOTS[d] * GW + hh * P
                        bank, col = 6 + hh // 2, (hh % 2) * UW
                        for p_part, c_at, width in ((p_hi, CD, UW), (p_hi, 0, CD), (p_lo, CD, UW)):
                            last = pe.matmul(ps[:, bank, col:col + width], p_part[:, at:at + P],
                                             rows_flat[:, bass.ds(at_t + c_at, width)],
                                             start=False, stop=False, skip_group_check=True)
                    last.then_inc(sem("step_summed"), 1)

                def build_keys(g, i, c, s, kcount):
                    pe.wait_ge(sem("keys_ready"), kcount + BUILDS.index((c, s)) + 1)
                    dst = ps[0:STACK_W, 4 + s, 0:MCHUNK]
                    at = bass.ds(g * 2 * STACK_W + s * STACK_W, STACK_W)
                    keys = bass.ds(i * KPI + c * MCHUNK, MCHUNK)
                    pe.matmul(dst, wk_hi[:, at], ctxT_hi[:, keys], start=True, stop=False)
                    pe.matmul(dst, wk_lo[:, at], ctxT_hi[:, keys], start=False, stop=False)
                    pe.matmul(dst, wk_hi[:, at], ctxT_lo[:, keys], start=False, stop=True
                              ).then_inc(sem("keys_in_psum"), 1)

                def stacked_scores(g, t, count, kcount):
                    pe.wait_ge(sem("step_exp_done"), count + t + 1 - 2 + CREDIT)
                    chunk = ((t + 1) * P - 1) // MCHUNK
                    pe.wait_ge(sem("keys_ready"), kcount + BUILDS.index((chunk, 1)) + 1 + 2)
                    for s in range(2):
                        last = pe.matmul(ps[:, 2 + t % 2, s * 2 * P:(s + 1) * 2 * P],
                                         k_stack[0:STACK_ROWS, s, t * P:(t + 1) * P],
                                         q_stack[0:STACK_ROWS, bass.ds(g * GW + s * 2 * P, 2 * P)],
                                         start=True, stop=True)
                    last.then_inc(sem("step_scores_ready"), 1)

                def project_values(g, i, c, vcount):
                    pe.wait_ge(sem("values_ready"), vcount + c + 1)
                    a, b = V_CHUNKS[c]
                    for t in range(a, b):
                        dst = ps[:, 7, (t - a) * 64:(t - a + 1) * 64]
                        key = (i * TPI + t) * P
                        hi, lo = ctxT_hi[:, bass.ds(key, P)], ctxT_lo[:, bass.ds(key, P)]
                        cols_g = bass.ds(g * HPG * 16, HPG * 16)
                        pe.matmul(dst, hi, wv_hi[:, cols_g], start=True, stop=False)
                        pe.matmul(dst, hi, wv_lo[:, cols_g], start=False, stop=False)
                        last = pe.matmul(dst, lo, wv_hi[:, cols_g], start=False, stop=True)
                    last.then_inc(sem("values_in_psum"), 1)

                def sum_values(t, count, vcount):
                    pe.wait_ge(sem("step_exp_done"), count + t + 1 + CREDIT)
                    for c, (a, b) in enumerate(V_CHUNKS):
                        if a == t:
                            pe.wait_ge(sem("values_ready"), vcount + c + 2)
                    for hh in range(HPG):
                        at = (t % P_SLOTS[d]) * GW + hh * P
                        last = pe.matmul(ps[32 * hh:32 * hh + VW, 6, 0:P], v_ring[:, t, hh, :], probs[:, at:at + P],
                                         start=False, stop=False, skip_group_check=True)
                    last.then_inc(sem("step_summed"), 1)

                def max_loop():
                    with pe.Fori(0, ITERS) as i:
                        if n == 0:
                            pe.wait_ge(sem("ctx_high_made"), i + 1)
                        for k in range(MUPI // 2):
                            c, hp = k // 2, k % 2
                            if k in DIRECT:
                                j = DIRECT.index(k)
                                bank, ready = DIRECT_BANKS[j], sem("first_scores_ready")
                                pe.wait_ge(sem("first_slots_free"), (n * ITERS + i) * len(DIRECT) + j + 1)
                            else:
                                j = FOLDED.index(k)
                                bank, ready = FOLDED_BANKS[j % 2], sem("folded_scores_ready")
                                pe.wait_ge(sem("scores_copied"), (n * ITERS + i) * NF + j + 1)
                            for t in range(2):
                                last = pe.matmul(ps[:, bank + t, 0:MCHUNK],
                                                 q_hi[:, (2 * hp + t) * P:(2 * hp + t + 1) * P],
                                                 ctxT_hi[:, bass.ds(i * KPI + c * MCHUNK, MCHUNK)],
                                                 start=True, stop=True)
                            last.then_inc(ready, 1)

                def bias_ready(g):
                    pe.wait_ge(sem("bias_rows_ready"), n * GROUPS + g + 1)

                def sums_cleared(g):
                    pe.wait_ge(sem("u_cleared"), n * GROUPS + g + 1)

                def iteration(g, i, max_group):
                    count = (g * ITERS + i) * TPI + step_base(name)
                    if d == 64:
                        bias_ready(g)
                    units = [0]

                    def max_units(k):
                        if max_group is None:
                            return
                        mcount = ((max_group - 1 + n * (GROUPS - 1)) * ITERS + i) * MUPI
                        for _ in range(k):
                            max_unit(max_group, i, units[0], mcount)
                            units[0] += 1

                    if d == 64:
                        for t in range(TPI):
                            scores(g, i, t, count)
                            if t == SUM_LAG:
                                sums_cleared(g)
                            if t >= SUM_LAG:
                                sum_up(i, t - SUM_LAG, count)
                            max_units(2 if t == TWO_UNITS_AFTER else 1)
                        sum_up(i, TPI - 2, count)
                        max_units(1)
                        sum_up(i, TPI - 1, count)
                        return
                    vcount, kcount = v_count(name, g, i), k_count(name, g, i)
                    build_keys(g, i, 0, 0, kcount)
                    build_keys(g, i, 0, 1, kcount)
                    if i == 0:
                        bias_transpose(g)
                        project_values(g, i, 0, vcount)
                        bias_ready(g)
                        max_units(2)
                    else:
                        max_units(2)
                        project_values(g, i, 0, vcount)
                    build_keys(g, i, 1, 0, kcount)
                    for t in range(TPI):
                        stacked_scores(g, t, count, kcount)
                        if t == SUM_LAG:
                            sums_cleared(g)
                        if t >= SUM_LAG:
                            sum_values(t - SUM_LAG, count, vcount)
                        if t in BUILD_AFTER:
                            build_keys(g, i, *BUILD_AFTER[t], kcount)
                        if t in VALUES_AFTER:
                            project_values(g, i, VALUES_AFTER[t], vcount)
                        if t != NO_UNIT_AFTER:
                            max_units(1)
                    sum_values(TPI - 2, count, vcount)
                    max_units(1)
                    sum_values(TPI - 1, count, vcount)

                def keys_loop(g, max_group):
                    if d == 16:
                        for i in range(ITERS):
                            iteration(g, i, max_group)
                    else:
                        bias_transpose(g)
                        with pe.Fori(0, ITERS) as i:
                            iteration(g, i, max_group)

                max_loop()
                pe.wait_ge(sem("first_slots_free"), (n + 1) * ITERS * len(DIRECT) + 2)
                pe.wait_ge(sem("scores_copied"), (n + 1) * ITERS * NF + 2)
                if n == 0:
                    pe.wait_ge(sem("ctx_low_made"), ITERS)
                if d == 64:
                    pe.wait_ge(sem("rows_low_made"), ITERS)
                pe.wait_ge(sem("ones_ready"), n + 1)
                if d == 16:
                    pe.wait_ge(sem("wv_high_ready"), v_layers.index(name) + 1)
                    pe.wait_ge(sem("wv_low_ready"), v_layers.index(name) + 1)
                    pe.wait_ge(sem("wk_ready"), v_layers.index(name) + 1)
                    pe.wait_ge(sem("q_stack_ready"), v_layers.index(name) + 1)
                with pe.Fori(0, GROUPS - 1) as g:
                    keys_loop(g, g + 1)
                keys_loop(GROUPS - 1, None)

                if d == 16:
                    for g in range(GROUPS):
                        pe.wait_ge(sem("u_done"), n * GROUPS + g + 1)
                        last = pe.transpose(ps[:, 0, g * P:(g + 1) * P], u_raw[:, g, :], ident[:, :])
                    last.then_inc(sem("o_in_psum"), 1)
                else:
                    for b in range(4):
                        pe.wait_ge(sem("u_done"), n * GROUPS + b + 1)
                        for hh in range(4):
                            h = 4 * b + hh
                            last = pe.transpose(ps[:, 2 + b, hh * P:(hh + 1) * P], u_norm[:, h * P:(h + 1) * P],
                                                ident[:, :])
                        last.then_inc(sem("uT_in_psum"), 1)
                    piece_arrived(pe, v_piece)
                    for place in range(HEADS):
                        if place % 4 == 0:
                            pe.wait_ge(sem("uT_ready"), 4 * u_layers.index(name) + place // 4 + 1)
                        at = head_at(d, place) * d
                        last = pe.matmul(ps[:, at // 512, at % 512:at % 512 + d], u_T[:, place * P:(place + 1) * P],
                                         w_v[:, at:at + d], start=True, stop=True)
                    last.then_inc(sem("o_in_psum"), 1)
                    piece_arrived(pe, o_piece)
                bias = {"L0_xattn": "L0x_bo", "L1_xattn": "L1x_bo"}.get(name)
                output_tail(name, d, w_o, row(bias) if bias else None)

            def self_attention(name):
                d = SATTN[name] if name in SATTN else 16
                q_base = counted(q_users, name)
                k_base = counted(kv_users, name)
                a = kv_users.index(name)
                pcs = of_layer[name]
                width = HEADS * d
                if len(pcs) == 1:
                    w = slot(pcs[0]).rearrange("p (m k n) -> p m k n", m=4, k=KD)
                    w_q, w_k, w_v, w_o = (w[:, m] for m in range(4))
                    p_q = p_k = p_v = p_o = pcs[0]
                else:
                    w_q, w_k, w_v = (slot(p).rearrange("p (k n) -> p k n", k=KD) for p in pcs[:3])
                    w_o = slot(pcs[3]).rearrange("p (k n) -> p k n", k=8)
                    p_q, p_k, p_v, p_o = pcs
                transpose_xn(name)
                piece_arrived(pe, p_q)
                heads_T(w_q, d, 4, "qT_in_psum")
                piece_arrived(pe, p_k)
                heads_T(w_k, d, 6, "kT_in_psum")
                piece_arrived(pe, p_v)
                linear = name == "L3_attn"
                for c in range(ceil_div(width, 512)):
                    w_c = min(512, width)
                    for k in range(KD):
                        last = pe.matmul(ps[:, 2 + c, 0:w_c], xnT[:, k, :], w_v[:, k, c * 512:c * 512 + w_c],
                                         start=(k == 0), stop=(k == KD - 1))
                last.then_inc(sem("v_in_psum"), 1)
                if linear:
                    pe.wait_ge(sem("qT_ready_linear"), 1)
                    pe.wait_ge(sem("kT_ready_linear"), 1)
                else:
                    pe.wait_ge(sem("qT_ready"), q_base + width_banks(name))
                    pe.wait_ge(sem("kT_ready"), k_base + width_banks(name))
                for place in range(HEADS):
                    h = head_at(d, place)
                    qh, kh = head_rows(a_qT, d, h, True), head_rows(a_kT, d, h, False)
                    dst = ps[:, 4 + place // 4, place % 4 * P:(place % 4 + 1) * P]
                    last = pe.matmul(dst, kh if linear else qh, qh if linear else kh, start=True, stop=True)
                    if place % 4 == 3:
                        last.then_inc(sem("scores_in_psum"), 1)
                if linear:
                    pe.wait_ge(sem("v_ready_linear"), 1)
                    for place in range(HEADS):
                        if place % 4 == 0:
                            pe.wait_ge(sem("masked_ready"), place // 4 + 1)
                        h = head_at(d, place)
                        last = pe.matmul(ps[:, 0, h * (d + 1):(h + 1) * (d + 1)], a_p[:, place * P:(place + 1) * P],
                                         a_v[:, h * (d + 1):(h + 1) * (d + 1)], start=True, stop=True)
                    last.then_inc(sem("o_in_psum"), 1)
                else:
                    pe.wait_ge(sem("v_ready"), a + 1)
                    for b in range(4):
                        pe.wait_ge(sem("p_ready"), 4 * a + b + 1)
                        for hh in range(4):
                            place = 4 * b + hh
                            last = pe.transpose(ps[:, b, hh * P:(hh + 1) * P], a_p[:, place * P:(place + 1) * P],
                                                ident[:, :])
                        last.then_inc(sem("pT_in_psum"), 1)
                    for place in range(HEADS):
                        if place % 4 == 0:
                            pe.wait_ge(sem("pT_ready"), 4 * a + place // 4 + 1)
                        at = head_at(d, place) * d
                        last = pe.matmul(ps[:, 4 + at // 512, at % 512:at % 512 + d], a_pT[:, place * P:(place + 1) * P],
                                         a_v[:, at:at + d], start=True, stop=True)
                    last.then_inc(sem("o_in_psum"), 1)
                piece_arrived(pe, p_o)
                output_tail(name, d, w_o, row("bout") if name == "L0_attn" else None)

            def l0_ffn():
                g_piece, u_piece, d_piece = of_layer["L0_ffn"]
                if ln_at["L0_ffn"]:
                    pe.wait_ge(sem("x_updated"), ln_at["L0_ffn"])
                for m in range(2):
                    pe.wait_ge(sem("quantise_steps"), 1 + ITERS * QSTEPS)
                    wq = slot((g_piece, u_piece)[m])[:, 0:1536].rearrange("p (o i) -> p o i", o=6)
                    for k in range(KD):
                        for o in range(6):
                            at = o * P
                            last = pe.transpose(ps[:, 2 * (2 * m + k) % 8 + at // 512, at % 512:at % 512 + P],
                                                wq[:, o, k * P:(k + 1) * P], ident[:, :])
                        last.then_inc(sem("wT_in_psum"), 1)
                pe.wait_ge(sem("wT_copied"), 2)
                wq = slot(d_piece)[:, 0:1536].rearrange("p (o i) -> p o i", o=2)
                for k in range(6):
                    for o in range(2):
                        at = k * DM + o * P
                        last = pe.transpose(ps[:, at // 512, at % 512:at % 512 + P],
                                            wq[:, o, k * P:(k + 1) * P], ident[:, :])
                last.then_inc(sem("wT_in_psum"), 1)
                pe.wait_ge(sem("wT_copied"), 5)
                transpose_xn("L0_ffn")
                for m in range(2):
                    for at, c in ((0, 512), (512, 256)):
                        for k in range(KD):
                            last = pe.matmul(ps[:, 2 + 2 * m + at // 512, 0:c], xnT[:, k, :],
                                             l0_wT(m)[:, k, at:at + c], start=(k == 0), stop=(k == KD - 1))
                    last.then_inc(sem("gate_up_in_psum"), 1)
                pe.wait_ge(sem("l0_h_ready"), 1)
                for k in range(6):
                    last = pe.transpose(ps[:, 6 + k // 4, (k % 4) * P:(k % 4 + 1) * P], l0_h[:, k * P:(k + 1) * P],
                                        ident[:, :])
                last.then_inc(sem("l0_hT_in_psum"), 1)
                pe.wait_ge(sem("l0_hT_ready"), 1)
                for k in range(6):
                    last = pe.matmul(ps[:, 0, 0:DM], l0_hT[:, k * P:(k + 1) * P], l0_down[:, k, :], start=(k == 0),
                                     stop=(k == 5))
                last.then_inc(sem("l0_ffn_y"), 1)

            def l1_ffn():
                pcs = of_layer["L1_ffn"]
                transpose_xn("L1_ffn")
                for m in range(2):
                    piece_arrived(pe, pcs[m])
                    w = slot(pcs[m]).rearrange("p (k n) -> p k n", k=KD)
                    for f in range(FT):
                        for k in range(KD):
                            last = pe.matmul(ps[:, 2 + 2 * m + f // 4, (f % 4) * P:(f % 4 + 1) * P],
                                             w[:, k, f * P:(f + 1) * P], xnT[:, k, :], start=(k == 0), stop=(k == KD - 1))
                    last.then_inc(sem("swiglu_in_psum"), 1)
                pe.wait_ge(sem("swiglu_ready"), 1)
                src = f_a
                for m, (banks, dst) in enumerate((((6, 7), f_b), ((2, 3), f_a))):
                    if m:
                        pe.wait_ge(sem("gelu_ready"), FT)
                    for f in range(FT):
                        piece = pcs[2 + 4 * m + f // 2]
                        if f % 2 == 0:
                            piece_arrived(pe, piece)
                        w = slot(piece).rearrange("p (k n) -> p k n", k=FT)
                        for k in range(FT):
                            last = pe.matmul(ps[:, banks[f // 4], (f % 4) * P:(f % 4 + 1) * P],
                                             w[:, k, (f % 2) * P:(f % 2 + 1) * P], src[:, k * P:(k + 1) * P],
                                             start=(k == 0), stop=(k == FT - 1))
                        if f % 4 == 3:
                            last.then_inc(sem("hidden_in_psum"), 1)
                    src = dst
                pe.wait_ge(sem("gelu_ready"), 2 * FT)
                piece_arrived(pe, pcs[10])
                w = slot(pcs[10]).rearrange("p (k n) -> p k n", k=FT)
                for k in range(FT):
                    last = pe.matmul(ps[:, 0, 0:DM], f_a[:, k * P:(k + 1) * P], w[:, k, :], start=(k == 0),
                                     stop=(k == FT - 1))
                last.then_inc(sem("l1_ffn_y"), 1)

            def l2_ffn():
                transpose_xn("L2_ffn")
                pe.wait_ge(sem("l2f_w_ready"), 1)
                pe.matmul(ps[:, 0, 0:DM], ones_row[:, :], row("L2f_bias"), start=True, stop=False)
                for k in range(KD):
                    last = pe.matmul(ps[:, 0, 0:DM], xnT[:, k, :], l2f_w[:, k, :], start=False, stop=(k == KD - 1))
                last.then_inc(sem("l2_ffn_y"), 1)

            def l3_xattn():
                pcs = of_layer["L3_xattn"]
                transpose_xn("L3_xattn")
                nh = XHID // P

                def up(e):
                    piece_arrived(pe, pcs[e])
                    w = slot(pcs[e])[:, 0:1024].rearrange("p (k n) -> p k n", k=KD)
                    if e >= 2:
                        pe.wait_ge(sem("relu_ready"), e - 1)
                    for f in range(nh):
                        for k in range(KD):
                            last = pe.matmul(ps[:, 2 + e % 2, f * P:(f + 1) * P], w[:, k, f * P:(f + 1) * P],
                                             xnT[:, k, :], start=(k == 0), stop=(k == KD - 1))
                    last.then_inc(sem("expert_up"), 1)

                def down(e):
                    w = slot(pcs[e])[:, 1024:2048].rearrange("p (k n) -> p k n", k=nh)
                    pe.wait_ge(sem("relu_ready"), e + 1)
                    if e >= 2:
                        pe.wait_ge(sem("expert_added"), e - 1)
                    for k in range(nh):
                        last = pe.matmul(ps[:, 4 + e % 2, 0:DM], e_relu[:, e % 2, k * P:(k + 1) * P], w[:, k, :],
                                         start=(k == 0), stop=(k == nh - 1))
                    last.then_inc(sem("expert_down"), 1)

                for e in range(EXPERTS + 1):
                    if e < EXPERTS:
                        up(e)
                    if e >= 1:
                        down(e - 1)

            def l3_ffn():
                pcs = of_layer["L3_ffn"]
                transpose_xn("L3_ffn")
                w_gate = cols[:, COL_AT["w_gate"]:COL_AT["w_gate"] + KD * EXPERTS].rearrange("p (k n) -> p k n", k=KD)
                pe.matmul(ps[:, 1, 0:EXPERTS], ones_row[:, :], row("gate_b"), start=True, stop=False)
                for k in range(KD):
                    last = pe.matmul(ps[:, 1, 0:EXPERTS], xnT[:, k, :], w_gate[:, k, :], start=False, stop=(k == KD - 1))
                last.then_inc(sem("logits_in_psum"), 1)

                def up(e):
                    piece_arrived(pe, pcs[2 * e])
                    w = slot(pcs[2 * e]).rearrange("p (k n) -> p k n", k=KD)
                    for f in range(FT):
                        if e >= 2 and f % 4 == 0:
                            pe.wait_ge(sem("moe_gelu_ready"), FT * (e - 2) + f + 4)
                        for k in range(KD):
                            last = pe.matmul(ps[:, 2 + 2 * (e % 2) + f // 4, (f % 4) * P:(f % 4 + 1) * P],
                                             w[:, k, f * P:(f + 1) * P], xnT[:, k, :], start=(k == 0), stop=(k == KD - 1))
                        if f % 4 == 3:
                            last.then_inc(sem("moe_up"), 1)

                def down(e):
                    piece_arrived(pe, pcs[2 * e + 1])
                    w = slot(pcs[2 * e + 1]).rearrange("p (k n) -> p k n", k=FT)
                    if e >= 2:
                        pe.wait_ge(sem("moe_added"), e - 1)
                    for k in range(FT):
                        pe.wait_ge(sem("moe_gelu_ready"), FT * e + k + 1)
                        last = pe.matmul(ps[:, 6 + e % 2, 0:DM], m_h[:, e % 2, k * P:(k + 1) * P], w[:, k, :],
                                         start=(k == 0), stop=(k == FT - 1))
                    last.then_inc(sem("moe_down"), 1)

                for e in range(EXPERTS + 2):
                    if e < EXPERTS + 1:
                        up(e)
                    if e == 1:
                        pe.wait_ge(sem("combine_ready"), 1)
                        pe.transpose(ps[0:EXPERTS + 1, 1, 0:P], combine, ident[:, :]).then_inc(sem("combine_T_psum"), 1)
                        pe.wait_ge(sem("combine_T_ready"), 1)
                        pe.matmul(ps[:, 1, 0:DM], combine_T[:, :], b2[:, :], start=True, stop=True
                                  ).then_inc(sem("moe_bias"), 1)
                    if e >= 1:
                        down(e - 1)

            pe.wait_ge(sem("consts_loaded"), 16 * 10)
            pe.wait_ge(sem("pool_consts"), 7)
            if x_layers:
                pe.sem_inc(sem("step_summed"), CREDIT)
            for name in layers:
                if name in XATTN:
                    cross_attention(name)
                elif name in SATTN or name == "L3_attn":
                    self_attention(name)
                else:
                    {"L0_ffn": l0_ffn, "L1_ffn": l1_ffn, "L2_ffn": l2_ffn, "L3_xattn": l3_xattn,
                     "L3_ffn": l3_ffn}[name]()

        @block.scalar
        def _(act):
            def heads_T_out(name, d):
                q_base = counted(q_users, name)
                if d == 64:
                    dst = x_qT if name in XATTN else a_qT
                    for b in range(2):
                        act.wait_ge(sem("qT_in_psum"), q_base + b + 1)
                        act.activation(dst[:, b * 512:(b + 1) * 512], ps[:, 4 + b, :], ACT.Identity, scale=d ** -0.5
                                       ).then_inc(sem("qT_ready"), 1)
                    return
                act.wait_ge(sem("qT_in_psum"), q_base + 1)
                dst = a_qT[:, 0:512].rearrange("p (m h q) -> p m h q", m=2, h=2)
                for half in range(2):
                    if name == "L0_attn":
                        act.activation(dst[:, 0, half, :], ps[:, 4, 0:P], ACT.Identity, scale=sig_half[:, half:half + 1])
                        last = act.activation(dst[:, 1, half, :], ps[:, 4, P:2 * P], ACT.Identity,
                                              scale=half_scale[:, half:half + 1])
                    else:
                        last = act.activation(dst[:, :, half, :], ps[:, 4, 0:2 * P].rearrange("p (m q) -> p m q", m=2),
                                              ACT.Identity, scale=half_scale[:, half:half + 1])
                last.then_inc(sem("qT_ready"), 1)

            def high_rows(c):
                act.wait_ge(sem(f"rows_staged{c % 2}"), 16 * (c // 2 + 1))
                act.activation(ctx_rows[:, c * TPI:(c + 1) * TPI, CD:2 * CD], stage_rows(c), ACT.Copy
                               ).then_inc(sem("rows_high_made"), 1)

            def cross_attention(name):
                d = XATTN[name]
                n = x_layers.index(name)

                def absorbed_out():
                    for b in range(4):
                        act.wait_ge(sem("absorbed_in_psum"), 4 * n + b + 1)
                        act.activation(q_hi[:, b * 512:(b + 1) * 512], ps[:, (0, 1, 6, 7)[b], :], ACT.Copy
                                       ).then_inc(sem("q_high_ready"), 1)

                def high_context(c):
                    if n == 0:
                        act.wait_ge(sem(f"ctxT_staged{c % 2}"), 16 * (c // 2 + 1))
                        act.activation(ctxT_hi[:, c * KPI:(c + 1) * KPI], stage[:, c % 2, :], ACT.Copy
                                       ).then_inc(sem("ctx_high_made"), 1)

                act.wait_ge(sem("consts_loaded"), 16 * 10)
                act.activation(table_cell[:, n:n + 1], half_scale[:, 0:1], ACT.Exp)
                if n == 0:
                    act.sem_inc(sem("step_exp_done"), CREDIT)
                    act.sem_inc(sem("scores_copied"), 2)
                if d == 16:
                    q_piece, k_piece = of_layer[name]
                    piece_arrived(act, q_piece)
                    if name == "L0_xattn":
                        act.wait_ge(sem("consts_loaded"), 16 * 10)
                        act.activation(bq_3.rearrange("p (s r c) -> p s r c", r=3, c=32),
                                       rows[:, ROW_AT["bq"]:ROW_AT["bq"] + DM].rearrange("p (s c) -> p s c", c=32)
                                       .unsqueeze(2).broadcast_to([1, STACKS, 3, 32]), ACT.Copy)
                    act.activation(w_q3.rearrange("p (s r c) -> p s r c", r=3, c=32),
                                   slot(q_piece)[:, 0:512].rearrange("p (s c) -> p s c", c=32)
                                   .unsqueeze(2).broadcast_to([P, KD * STACKS, 3, 32]), ACT.Copy
                                   ).then_inc(sem("w_q3_ready"), 1)
                    act.activation(wv_hi[:, :], slot(q_piece)[:, 512:768], ACT.Copy).then_inc(sem("wv_high_ready"), 1)
                    act.activation(wk_hi.rearrange("p (s r c) -> p s r c", r=3, c=32), key_weights(q_piece), ACT.Copy
                                   ).then_inc(sem("wk_high_ready"), 1)
                    act.wait_ge(sem("consts_loaded"), 16 * 10)
                    piece_arrived(act, k_piece)
                    act.activation(bk_16, bkT[:, :], ACT.Copy)
                    act.activation(kT_16, slot(k_piece)[0:32, 0:STACKS * P], ACT.Copy).then_inc(sem("kT_rounded"), 1)
                    high_context(0)
                    for b in range(2):
                        act.wait_ge(sem("q_stack_in_psum"), 2 * v_layers.index(name) + b + 1)
                        for half in range(2):
                            act.activation(q_part(0, b, half), ps[0:STACK_W, 4 + b, :].rearrange(
                                "p (s q) -> p s q", s=4), ACT.Identity, scale=head_scale(0, half)
                                ).then_inc(sem("q_stack_high"), 1)
                    absorbed_out()
                else:
                    heads_T_out(name, d)
                    absorbed_out()
                    high_context(0)

                def copy_scores(i):
                    for j in range(NF):
                        count = (n * ITERS + i) * NF + j + 1
                        act.wait_ge(sem("folded_scores_ready"), count)
                        act.wait_ge(sem("copy_used"), count)
                        b = FOLDED_BANKS[j % 2]
                        act.activation(copied[:, j % 2, :, :], ps[:, b:b + 2, 0:MCHUNK], ACT.Copy
                                       ).then_inc(sem("scores_copied"), 1)

                if n == 0 or d == 64:
                    for c in range(ITERS):
                        if n == 0 and c + 1 < ITERS:
                            high_context(c + 1)
                        if n:
                            high_rows(c)
                        copy_scores(c)
                    for c in range(ITERS if d == 64 and n == 0 else 0):
                        high_rows(c)
                else:
                    with act.Fori(0, ITERS) as i:
                        copy_scores(i)
                if d == 64:
                    act.wait_ge(sem("rows_low_made"), ITERS)

                def exp_twice(t, count):
                    act.wait_ge(sem("step_scores_ready"), count + t + 1)
                    act.wait_ge(sem("step_summed"), count + t + 1 - steps_since(t, P_SLOTS[d]) + CREDIT)
                    slot_t = t % P_SLOTS[d]
                    for dst in (p_wide[:, slot_t, :], p_hi[:, slot_t * GW:(slot_t + 1) * GW]):
                        last = act.activation(dst, ps[:, 2 + t % S_BANKS[d], :], ACT.Exp)
                    last.then_inc(sem("step_exp_done"), 1)

                def exp_once(t, count):
                    act.wait_ge(sem("step_scores_ready"), count + t + 1)
                    act.wait_ge(sem("step_summed"), count + t + 1 - steps_since(t, P_SLOTS[d]) + CREDIT)
                    at = t % P_SLOTS[d] * GW
                    act.activation(probs[:, at:at + GW], ps[:, 2 + t % S_BANKS[d], :], ACT.Exp
                                   ).then_inc(sem("step_exp_done"), 1)

                def high_keys(c, s, kcount):
                    act.wait_ge(sem("keys_in_psum"), kcount + BUILDS.index((c, s)) + 1)
                    act.activation(k_stack[0:STACK_W, s, c * MCHUNK:(c + 1) * MCHUNK],
                                   ps[0:STACK_W, 4 + s, 0:MCHUNK], ACT.Copy).then_inc(sem("keys_high_made"), 1)

                def exp_loop(g):
                    with act.Fori(0, ITERS) as i:
                        count = (g * ITERS + i) * TPI + step_base(name)
                        if d == 16:
                            kcount = k_count(name, g, i)
                            high_keys(0, 0, kcount)
                            high_keys(0, 1, kcount)
                            high_keys(1, 0, kcount)
                        for t in range(TPI):
                            (exp_once if d == 16 else exp_twice)(t, count)
                            if d == 16 and t in BUILD_AFTER:
                                high_keys(*BUILD_AFTER[t], kcount)

                with act.Fori(0, GROUPS) as g:
                    exp_loop(g)
                for b in range(4 if d == 64 else 0):
                    act.wait_ge(sem("uT_in_psum"), 4 * u_layers.index(name) + b + 1)
                    act.activation(u_T[:, b * 512:(b + 1) * 512], ps[:, 2 + b, :], ACT.Copy
                                   ).then_inc(sem("uT_ready"), 1)

            def self_attention(name):
                d = SATTN[name] if name in SATTN else 16
                a = kv_users.index(name)
                if name == "L3_attn":
                    q_base = counted(q_users, name)
                    k_base = counted(kv_users, name)
                    for m, dst in enumerate((linear_q, a_kT)):
                        act.wait_ge(sem("neg_part_ready"), m + 1)
                        part = dst[:, 0:2 * P]
                        act.activation(part, part, ACT.Exp).then_inc(sem("exp_part_ready"), 1)
                    return
                if name == "L0_attn":
                    act.wait_ge(sem("consts_loaded"), 16 * 10)
                    act.activation(sig[:, 0:1], w_sigma[:, :], ACT.Exp, scale=-1.0).then_inc(sem("sigma_exp"), 1)
                    act.wait_ge(sem("sigma_scale"), 1)
                act.wait_ge(sem("consts_loaded"), 16 * 10)
                heads_T_out(name, d)
                act.wait_ge(sem("v_in_psum"), a + 1)
                width = HEADS * d
                if width <= 512:
                    act.activation(a_v[:, 0:width], ps[:, 2, 0:width], ACT.Copy).then_inc(sem("v_ready"), 1)
                else:
                    act.activation(a_v[:, 0:width].rearrange("p (b c) -> p b c", b=2), ps[:, 2:4, :], ACT.Copy
                                   ).then_inc(sem("v_ready"), 1)
                for b in range(4):
                    act.wait_ge(sem("shifted_ready"), 4 * a + b + 1)
                    part = a_p[:, b * 512:(b + 1) * 512]
                    act.activation(part, part, ACT.Exp).then_inc(sem("p_ready"), 1)
                for b in range(4):
                    act.wait_ge(sem("pT_in_psum"), 4 * a + b + 1)
                    act.activation(a_pT[:, b * 512:(b + 1) * 512], ps[:, b, :], ACT.Copy).then_inc(sem("pT_ready"), 1)

            def l0_ffn():
                for i in range(4):
                    act.wait_ge(sem("wT_in_psum"), i + 1)
                    m, k = i // 2, i % 2
                    b0 = 2 * i % 8
                    act.activation(l0_wT(m)[:, k, 0:512], ps[:, b0, :], ACT.Copy)
                    act.activation(l0_wT(m)[:, k, 512:768], ps[:, b0 + 1, 0:256], ACT.Copy
                                   ).then_inc(sem("wT_copied"), 1)
                act.wait_ge(sem("wT_in_psum"), 5)
                act.activation(work[:, 3072:4608].rearrange("p (b c) -> p b c", b=3), ps[:, 0:3, :], ACT.Copy
                               ).then_inc(sem("wT_copied"), 1)
                act.wait_ge(sem("l0_gate_ready"), 1)
                act.activation(l0_tmp[:, 0:768], l0_gate, ACT.Exp, scale=-1.0).then_inc(sem("l0_exp_ready"), 1)

            def l1_ffn():
                s = cols[:, COL_AT["w1_s"]:COL_AT["w1_s"] + FT]
                act.wait_ge(sem("w1_scaled"), 1)
                act.activation(f_c, f_b, ACT.Exp, scale=-1.0).then_inc(sem("silu_exp"), 1)
                for m, (banks, dst, sc) in enumerate((((6, 7), f_b, "h1_s"), ((2, 3), f_a, "h2_s"))):
                    for f in range(FT):
                        if f % 4 == 0:
                            act.wait_ge(sem("hidden_in_psum"), 2 * m + f // 4 + 1)
                        act.activation(dst[:, f * P:(f + 1) * P], ps[:, banks[f // 4], (f % 4) * P:(f % 4 + 1) * P],
                                       ACT.Gelu, scale=cols[:, COL_AT[sc] + f:COL_AT[sc] + f + 1]
                                       ).then_inc(sem("gelu_ready"), 1)

            def l3_xattn():
                for e in range(EXPERTS):
                    act.wait_ge(sem("expert_up"), e + 1)
                    if e >= 2:
                        act.wait_ge(sem("expert_down"), e - 1)
                    act.activation(e_relu[:, e % 2, :], ps[:, 2 + e % 2, :], ACT.Relu).then_inc(sem("relu_ready"), 1)

            def l3_ffn():
                act.wait_ge(sem("top_diff"), 1)
                act.activation(top_w[:, 1:2], top_w[:, 0:1], ACT.Exp).then_inc(sem("top_exp"), 1)
                for e in range(EXPERTS + 1):
                    if e >= 2:
                        act.wait_ge(sem("moe_down"), e - 1)
                    for f in range(FT):
                        if f % 4 == 0:
                            act.wait_ge(sem("moe_up"), 2 * e + f // 4 + 1)
                        at = COL_AT["b1"] + e * FT + f
                        act.activation(m_h[:, e % 2, f * P:(f + 1) * P],
                                       ps[:, 2 + 2 * (e % 2) + f // 4, (f % 4) * P:(f % 4 + 1) * P], ACT.Gelu,
                                       bias=cols[:, at:at + 1]).then_inc(sem("moe_gelu_ready"), 1)

            for name in layers:
                if name in XATTN:
                    cross_attention(name)
                elif name in SATTN or name == "L3_attn":
                    self_attention(name)
                elif name != "L2_ffn":
                    {"L0_ffn": l0_ffn, "L1_ffn": l1_ffn, "L3_xattn": l3_xattn, "L3_ffn": l3_ffn}[name]()

        @block.vector
        def _(dve):
            steps = [0]
            updates = [0]

            def chained(ins):
                steps[0] += 1
                ins.then_inc(sem("dve_step"), 1)
                dve.wait_ge(sem("dve_step"), steps[0])

            def normalise(name, src):
                chained(dve.bn_stats(stats, src))
                dve.bn_aggr(mv, stats).then_inc(sem("var_ready"), 1)
                dve.wait_ge(sem("rstd_ready"), ln_at[name] + 1)
                dve.wait_ge(sem("var_ready"), ln_at[name] + 1)
                return dve.tensor_scalar(xn[:, :], src, mv[:, 0:1], rstd, ALU.subtract, ALU.mult)

            def transposed(name):
                dve.wait_ge(sem("xnT_in_psum"), layers.index(name) + 1)
                dve.tensor_copy(xnT[:, :, :],
                                ps[:, 0, 0:DM].rearrange("p (k n) -> p k n", k=KD)).then_inc(sem("xnT_ready"), 1)

            def ln(name):
                normalise(name, x[:, :]).then_inc(sem("xn_ready"), 1)
                transposed(name)

            def add_y(name_sem, value):
                dve.wait_ge(sem(name_sem), value)
                updates[0] += 1
                dve.tensor_tensor(x[:, :], x[:, :], ps[:, 0, 0:DM], ALU.add).then_inc(sem("x_updated"), 1)
                dve.wait_ge(sem("x_updated"), updates[0])

            def output_tail(name, d):
                t = tails.index(name)
                width = HEADS * d
                dve.wait_ge(sem("oT_in_psum"), t + 1)
                if width <= 512:
                    dve.tensor_copy(o_T[:, 0:width], ps[:, 6, 0:width]).then_inc(sem("oT_ready"), 1)
                else:
                    dve.tensor_copy(o_T.rearrange("p (b c) -> p b c", b=2), ps[:, 6:8, :]).then_inc(sem("oT_ready"), 1)
                if name == "L2_attn":
                    dve.wait_ge(sem("y_in_psum"), t + 1)
                    chained(dve.tensor_tensor(y[:, :], xn[:, :], ps[:, 0, 0:DM], ALU.add))
                    chained(normalise("L2_attn/post", y[:, :]))
                    chained(dve.tensor_tensor(y[:, :], xn[:, :], wide[:, 1, :], ALU.mult))
                    chained(dve.tensor_tensor(y[:, :], y[:, :], wide[:, 2, :], ALU.add))
                    chained(dve.tensor_tensor(x[:, :], x[:, :], y[:, :], ALU.add))
                else:
                    add_y("y_in_psum", t + 1)

            def gate_step(u, k):
                s, e = k // EXPERTS, k % EXPERTS
                if e == 0:
                    dve.wait_ge(sem(f"gate_in_slot{s}"), u * 32 + 32)
                dve.wait_ge(sem("gate_sums"), u * GATE_STEPS + GATE_STEPS + k - 1)
                dve.scalar_tensor_tensor(gate_junk[:, k % 2, :], gate_tok[:, s, :], float(e), gate_ctx[:, s, :],
                                         ALU.is_equal, ALU.mult, accum_out=gate_part[:, e, bass.ds(u * 2 + s, 1)]
                                         ).then_inc(sem("gate_sums"), 1)

            def cross_attention(name):
                d = XATTN[name]
                n = x_layers.index(name)
                ln(name)
                for b in range(4 if d == 64 else 0):
                    dve.wait_ge(sem("q_high_ready"), 4 * n + b + 1)
                    part = slice(b * 512, (b + 1) * 512)
                    dve.tensor_tensor(q_lo[:, part], ps[:, (0, 1, 6, 7)[b], :], q_hi[:, part], ALU.subtract
                                      ).then_inc(sem("q_low_ready"), 1)
                first_x = name == "L0_xattn"

                if n == 0:
                    dve.sem_inc(sem("max_slots_free"), 2)
                    dve.sem_inc(sem("first_slots_free"), 2)
                    dve.sem_inc(sem("copy_used"), 2)
                if d == 16:
                    v = v_layers.index(name)
                    piece = of_layer[name][0]
                    dve.wait_ge(sem("wv_high_ready"), v + 1)
                    dve.tensor_tensor(wv_lo[:, :], slot(piece)[:, 512:768], wv_hi[:, :], ALU.subtract
                                      ).then_inc(sem("wv_low_ready"), 1)
                    dve.wait_ge(sem("wk_high_ready"), v + 1)
                    dve.tensor_tensor(wk_lo.rearrange("p (s r c) -> p s r c", r=3, c=32), key_weights(piece),
                                      wk_hi.rearrange("p (s r c) -> p s r c", r=3, c=32), ALU.subtract
                                      ).then_inc(sem("wk_ready"), 1)
                    dve.memset(k_stack[STACK_W:STACK_ROWS, :, :], BIAS_UNIT)
                    dve.memset(v_ring[:, :, :, VW - 1:VW], 1.0).then_inc(sem("ones_ready"), 1)
                    if v == 0:
                        dve.sem_inc(sem("values_ready"), 1)
                        dve.sem_inc(sem("keys_ready"), 2)
                    for b in range(2):
                        dve.wait_ge(sem("q_stack_high"), 4 * v + 2 * b + 2)
                        for half in range(2):
                            low = q_part(64, b, half)
                            last = dve.scalar_tensor_tensor(low, ps[64:STACK_W, 4 + b, :].rearrange(
                                "p (s q) -> p s q", s=4), head_scale(64, half), low, ALU.mult, ALU.subtract)
                    last.then_inc(sem("q_stack_ready"), 1)
                    if first_x:
                        dve.wait_ge(sem("key_bias_in_psum"), 1)
                        dve.tensor_copy(key_bias_score, ps[:, 2, 0:HEADS]).then_inc(sem("key_bias_read"), 1)
                        dve.wait_ge(sem("key_bias_read"), 1)
                else:
                    dve.memset(ctx_rows[:, :, RW - 1:RW], 1.0).then_inc(sem("ones_ready"), 1)

                def copy_values(c, vcount):
                    a, b = V_CHUNKS[c]
                    dve.wait_ge(sem("values_in_psum"), vcount + c + 1)
                    dve.tensor_copy(v_ring[:, a:b, :, 0:16].rearrange("p t h c -> p (t h) c"),
                                    ps[:, 7, 0:(b - a) * 64].rearrange("p (t c) -> p t c", c=16)
                                    ).then_inc(sem("values_ready"), 1)

                def low_keys(c, s, kcount):
                    dve.wait_ge(sem("keys_high_made"), kcount + BUILDS.index((c, s)) + 1)
                    part = k_stack[32:64, s, c * MCHUNK:(c + 1) * MCHUNK]
                    dve.tensor_tensor(part, ps[32:64, 4 + s, 0:MCHUNK], part, ALU.subtract
                                      ).then_inc(sem("keys_ready"), 1)

                def maximum(g, i, u):
                    c, hh = u // HPG, u % HPG
                    dve.wait_ge(sem("max_scores_ready"), ((g - 1 + n * (GROUPS - 1)) * ITERS + i) * MUPI + u + 1)
                    dve.tensor_reduce(mx_part[:, hh, bass.ds(i * MCPI + c, 1)], ps[:, u % 2, 0:MCHUNK],
                                      AX.X, ALU.max).then_inc(sem("max_slots_free"), 1)

                def first_maxima(i):
                    for k in range(MUPI // 2):
                        hp = k % 2
                        if k in DIRECT:
                            j = DIRECT.index(k)
                            dve.wait_ge(sem("first_scores_ready"), (n * ITERS + i) * len(DIRECT) + j + 1)
                            b = DIRECT_BANKS[j]
                            dve.tensor_reduce(mx_part[:, 2 * hp:2 * hp + 2, bass.ds(i, 1)].rearrange("p h c -> p (h c)"),
                                              ps[:, b:b + 2, 0:MCHUNK], AX.X, ALU.max
                                              ).then_inc(sem("first_slots_free"), 1)
                            continue
                        j = FOLDED.index(k)
                        before_j = [m for m in range(j) if FOLDED[m] % 2 == hp]
                        back = j - (before_j[-1] if before_j else
                                    max(m for m in range(NF) if FOLDED[m] % 2 == hp) - NF)
                        count = (n * ITERS + i) * NF + j + 1
                        dve.wait_ge(sem("scores_copied"), count + 2)
                        dve.wait_ge(sem("copy_used"), count - back + 2)
                        run = run_max[:, 2 * hp:2 * hp + 2, :]
                        dve.tensor_tensor(run, run, copied[:, j % 2, :, :], ALU.max).then_inc(sem("copy_used"), 1)

                def max_loop():
                    chained(dve.memset(run_max[:, :, :], -FLT_MAX / 2))
                    chained(dve.memset(mx_part[:, :, :], -FLT_MAX / 2))
                    with dve.Fori(0, ITERS) as i:
                        first_maxima(i)
                    dve.wait_ge(sem("copy_used"), (n + 1) * ITERS * NF + 2)
                    dve.wait_ge(sem("first_slots_free"), (n + 1) * ITERS * len(DIRECT) + 2)
                    chained(dve.tensor_reduce(mx_part[:, :, ITERS], run_max[:, :, :], AX.X, ALU.max))

                def stacks_loop(g, max_group):
                    with dve.Fori(0, ITERS) as i:
                        vcount, kcount = v_count(name, g, i), k_count(name, g, i)
                        units = [0]

                        def maxima(k):
                            for _ in range(k if max_group is not None else 0):
                                maximum(max_group, i, units[0])
                                units[0] += 1

                        low_keys(0, 0, kcount)
                        low_keys(0, 1, kcount)
                        maxima(2)
                        copy_values(0, vcount)
                        low_keys(1, 0, kcount)
                        for t in range(TPI):
                            if t != NO_UNIT_AFTER:
                                maxima(1)
                            if t in BUILD_AFTER:
                                low_keys(*BUILD_AFTER[t], kcount)
                            if t in VALUES_AFTER:
                                copy_values(VALUES_AFTER[t], vcount)
                            if max_group is None and n == 0 and "L0_ffn" in layers and t < QSTEPS:
                                quantise_step(i, t)
                        maxima(1)

                def probs_loop(g, max_group):
                    with dve.Fori(0, ITERS) as i:
                        count = (g * ITERS + i) * TPI + step_base(name)
                        units = [0]

                        def maxima_and_gate(k):
                            for _ in range(k):
                                if max_group is not None:
                                    maximum(max_group, i, units[0])
                                if name == gate_rider and has_gate:
                                    gate_step(g * ITERS + i, units[0])
                                units[0] += 1

                        for t in range(TPI):
                            if t < TPI - 1:
                                maxima_and_gate(2 if t == TWO_UNITS_AFTER else 1)
                            dve.wait_ge(sem("step_exp_done"), count + t + 1 + CREDIT)
                            at = t % P_SLOTS[d] * GW
                            dve.tensor_tensor(p_lo[:, at:at + GW], p_wide[:, t % P_SLOTS[d], :], p_hi[:, at:at + GW],
                                              ALU.subtract).then_inc(sem("step_low_ready"), 1)
                        maxima_and_gate(2)

                def keys_loop(g, max_group):
                    if d == 16:
                        stacks_loop(g, max_group)
                    else:
                        probs_loop(g, max_group)

                def take_maxima(g):
                    dve.wait_ge(sem("max_slots_free"), (n * (GROUPS - 1) + g) * ITERS * MUPI + 2)
                    dve.tensor_reduce(mx_group, mx_part[:, :, :], AX.X, ALU.max).then_inc(sem("group_max"), 1)
                    dve.wait_ge(sem("group_max"), n * GROUPS + g + 1)
                    if first_x:
                        kb = key_bias_score[:, bass.ds(g * HPG, HPG)]
                        dve.tensor_tensor(mx_group, mx_group, kb, ALU.add).then_inc(sem("with_key_bias"), 1)
                        dve.wait_ge(sem("with_key_bias"), g + 1)
                        dve.tensor_tensor(neg_max, kb, mx_group, ALU.subtract).then_inc(sem("neg_max_ready"), 1)
                    else:
                        dve.tensor_scalar(neg_max, mx_group, -1.0, PROB_SHIFT if d == 64 else 0.0, ALU.mult, ALU.add
                                          ).then_inc(sem("neg_max_ready"), 1)

                def clear_sums(g):
                    dve.memset(ps[:, 6, 0:P] if d == 16 else ps[:, 6:8, 0:2 * UW], 0.0).then_inc(sem("u_cleared"), 1)

                def bias_for(g):
                    dve.wait_ge(sem("neg_max_T"), n * GROUPS + g + 1)
                    at = STACK_W if d == 16 else 0
                    rows_T = ps[at:at + HPG, 0, 0:P].unsqueeze(1).broadcast_to([HPG, HPG, P])
                    own = ident[at:at + HPG, at:at + HPG].unsqueeze(2).broadcast_to([HPG, HPG, P])
                    dst = bias_rows[:, :, :]
                    if d == 16:
                        dst = q_stack[at:at + HPG, bass.ds(g * GW, GW)].rearrange("p (h q) -> p h q", h=HPG)
                    last = dve.scalar_tensor_tensor(dst, rows_T, 1 / BIAS_UNIT, own, ALU.mult, ALU.mult)
                    last.then_inc(sem("bias_rows_ready"), 1)

                def end_group(g):
                    dve.wait_ge(sem("step_summed"), step_base(name) + (g + 1) * KT + CREDIT)
                    if d == 16:
                        dve.tensor_copy(u_raw[:, bass.ds(g, 1), :].rearrange("p g q -> p (g q)"), ps[:, 6, 0:P]
                                        ).then_inc(sem("u_done"), 1)
                        dve.wait_ge(sem("u_done"), n * GROUPS + g + 1)
                        return
                    den = ps[:, 6:8, 0:2 * UW].rearrange("p b (h c) -> p b h c", c=UW)[:, :, :, CD]
                    dve.reciprocal(rden[:, 0:HPG].rearrange("p (b h) -> p b h", b=2), den).then_inc(sem("rden_ready"), 1)
                    dve.wait_ge(sem("rden_ready"), u_layers.index(name) * GROUPS + g + 1)
                    for hh in range(HPG):
                        last = dve.tensor_scalar(u_norm[:, bass.ds(g * GW + hh * P, P)],
                                                 ps[:, 6 + hh // 2, (hh % 2) * UW:(hh % 2) * UW + CD],
                                                 rden[:, hh:hh + 1], None, ALU.mult)
                    last.then_inc(sem("u_done"), 1)
                    dve.wait_ge(sem("u_done"), n * GROUPS + g + 1)

                max_loop()
                take_maxima(0)
                clear_sums(0)
                bias_for(0)
                with dve.Fori(0, GROUPS - 1) as g:
                    keys_loop(g, g + 1)
                    take_maxima(g + 1)
                    if d == 64:
                        bias_for(g + 1)
                    end_group(g)
                    clear_sums(g + 1)
                    if d == 16:
                        bias_for(g + 1)
                if n == 0 and "L0_ffn" in layers:
                    prepare_quantising()
                keys_loop(GROUPS - 1, None)
                end_group(GROUPS - 1)
                dve.wait_ge(sem("o_in_psum"), tails.index(name) + 1)
                if d == 16:
                    sums = ps[:, 0, :].rearrange("p (h c) -> p h c", c=32)
                    ov = o_sb[:, 0:DM].rearrange("p (h c) -> p h c", c=16)
                    chained(dve.reciprocal(rden, sums[:, :, VW - 1]))
                    last = dve.tensor_tensor(ov, sums[:, :, 0:16], rden.unsqueeze(2).broadcast_to([P, HEADS, 16]),
                                             ALU.mult)
                    if first_x:
                        chained(last)
                        last = dve.tensor_tensor(o_sb[:, 0:DM], o_sb[:, 0:DM], wide[:, 3, :], ALU.add)
                    last.then_inc(sem("o_ready"), 1)
                else:
                    dve.tensor_copy(o_sb.rearrange("p (b c) -> p b c", b=2), ps[:, 0:2, :]).then_inc(sem("o_ready"), 1)
                output_tail(name, d)

            def softmax_attention(name):
                d = SATTN[name]
                a = kv_users.index(name)
                k_base = counted(kv_users, name)
                ln(name)
                if name == "L0_attn":
                    dve.wait_ge(sem("sigma_exp"), 1)
                    chained(dve.tensor_scalar(sig[:, 1:2], sig[:, 0:1], 1.0, None, ALU.add))
                    chained(dve.reciprocal(sig[:, 2:3], sig[:, 1:2]))
                    chained(dve.tensor_copy(sig_half, half_scale))
                    dve.tensor_scalar(sig_half[0:64, :], half_scale[0:64, :], sig[0:64, 2:3], -1.0, ALU.mult, ALU.mult
                                      ).then_inc(sem("sigma_scale"), 1)
                for b in range(width_banks(name)):
                    dve.wait_ge(sem("kT_in_psum"), k_base + b + 1)
                    w_b = min(512, HEADS * d)
                    dve.tensor_copy(a_kT[:, b * 512:b * 512 + w_b], ps[:, 6 + b, 0:w_b]).then_inc(sem("kT_ready"), 1)

                def by_head(ap):
                    return ap.rearrange("p (h k) -> p h k", h=4)

                for b in range(4):
                    dve.wait_ge(sem("scores_in_psum"), 4 * a + b + 1)
                    s = by_head(ps[:, 4 + b, :])
                    p_b = by_head(a_p[:, b * 512:(b + 1) * 512])
                    m_b = mx16[:, 4 * b:4 * b + 4]
                    if name != "L0_attn":
                        chained(dve.tensor_tensor(p_b, s, causal[:, :].unsqueeze(1).broadcast_to([P, 4, P]), ALU.add))
                        s = p_b
                    chained(dve.tensor_reduce(m_b, s, AX.X, ALU.max))
                    dve.tensor_tensor(p_b, s, m_b.unsqueeze(2).broadcast_to([P, 4, P]), ALU.subtract
                                      ).then_inc(sem("shifted_ready"), 1)
                for b in range(4):
                    dve.wait_ge(sem("p_ready"), 4 * a + b + 1)
                    chained(dve.tensor_reduce(den16[:, 4 * b:4 * b + 4], by_head(a_p[:, b * 512:(b + 1) * 512]),
                                              AX.X, ALU.add))
                chained(dve.reciprocal(rden, den16))
                dve.wait_ge(sem("o_in_psum"), tails.index(name) + 1)
                for c in range(2):
                    w_c = HEADS * d // 2
                    bank, at = (4 + c, 0) if d == 64 else (4, c * w_c)
                    if d == 64:
                        r = rden.rearrange("p (r c m) -> p r c m", r=2, c=2)[:, :, c, :].rearrange("p r m -> p m r")
                    else:
                        r = rden.rearrange("p (m c r) -> p m c r", m=4, c=2)[:, :, c, :]
                    last = dve.tensor_tensor(
                        o_sb[:, c * w_c:(c + 1) * w_c].rearrange("p (m r e) -> p m r e", m=4, r=2),
                        ps[:, bank, at:at + w_c].rearrange("p (m r e) -> p m r e", m=4, r=2),
                        r.unsqueeze(3).broadcast_to([P, 4, 2, d]), ALU.mult)
                last.then_inc(sem("o_ready"), 1)
                output_tail(name, d)

            def linear_attention():
                name, d = "L3_attn", 16
                a = kv_users.index(name)
                q_base, k_base = counted(q_users, name), counted(kv_users, name)
                ln(name)
                parts = (("qT_in_psum", q_base, linear_q, 4), ("kT_in_psum", k_base, a_kT, 6))
                for s_name, base, dst, bank in parts:
                    dve.wait_ge(sem(s_name), base + 1)
                    dve.tensor_scalar(dst[:, 0:2 * P], ps[:, bank, 0:2 * P], 0.0, None, ALU.min
                                      ).then_inc(sem("neg_part_ready"), 1)
                for m, (_, _, dst, bank) in enumerate(parts):
                    dve.wait_ge(sem("exp_part_ready"), m + 1)
                    last = dve.scalar_tensor_tensor(dst[:, 0:2 * P], ps[:, bank, 0:2 * P], 0.0, dst[:, 0:2 * P],
                                                    ALU.max, ALU.add)
                    if m:
                        last.then_inc(sem("kT_ready_linear"), 1)
                        continue
                    chained(last)
                    halves = a_qT[:, 0:512].rearrange("p (m h q) -> p m h q", m=2, h=2)
                    for half in range(2):
                        last = dve.tensor_scalar(halves[:, :, half, :], linear_q.rearrange("p (m q) -> p m q", m=2),
                                                 half_scale[:, half:half + 1], 4.0, ALU.mult, ALU.mult)
                    last.then_inc(sem("qT_ready_linear"), 1)
                v1 = a_v[:, 0:HEADS * (d + 1)].rearrange("p (h e) -> p h e", e=d + 1)
                dve.wait_ge(sem("v_in_psum"), a + 1)
                chained(dve.memset(v1[:, :, d:d + 1], 1.0))
                dve.tensor_copy(v1[:, :, 0:d], ps[:, 2, 0:HEADS * d].rearrange("p (h e) -> p h e", e=d)
                                ).then_inc(sem("v_ready_linear"), 1)
                for b in range(4):
                    dve.wait_ge(sem("scores_in_psum"), 4 * a + b + 1)
                    dve.tensor_tensor(a_p[:, b * 512:(b + 1) * 512].rearrange("p (h k) -> p h k", h=4),
                                      ps[:, 4 + b, :].rearrange("p (h k) -> p h k", h=4),
                                      keep_T[:, :].unsqueeze(1).broadcast_to([P, 4, P]), ALU.mult
                                      ).then_inc(sem("masked_ready"), 1)
                dve.wait_ge(sem("o_in_psum"), tails.index(name) + 1)
                o1 = ps[:, 0, 0:HEADS * (d + 1)].rearrange("p (h e) -> p h e", e=d + 1)
                chained(dve.reciprocal(rden, o1[:, :, d]))
                ov = o_sb[:, 0:HEADS * d].rearrange("p (h e) -> p h e", h=HEADS)
                chained(dve.tensor_tensor(ov, o1[:, :, 0:d], rden.unsqueeze(2).broadcast_to([P, HEADS, d]), ALU.mult))
                dve.tensor_scalar(o_sb[:, 0:HEADS * d], o_sb[:, 0:HEADS * d], 1e-12, None, ALU.add
                                  ).then_inc(sem("o_ready"), 1)
                output_tail(name, d)

            def quantise_step(i, k):
                s0 = slot_of[of_layer["L0_ffn"][0]]
                w = ring_a[:, s0:s0 + 3, bass.ds(i * QSLICE * QBLOCK, QSLICE * QBLOCK)]
                wb = w.rearrange("p m (n b) -> p m n b", b=QBLOCK)
                am, s_b, inv = (quant_scales[:, v] for v in range(3))

                def per_block(ap):
                    return ap.unsqueeze(3).broadcast_to([P, 3, QSLICE, QBLOCK])

                dve.wait_ge(sem("quantise_steps"), i * QSTEPS + k + 1)
                if k == 0:
                    last = dve.tensor_reduce(am, wb, AX.X, ALU.max, apply_absolute_value=True)
                elif k == 1:
                    last = dve.tensor_scalar(s_b, am, 1.0 / 7.0, 1e-12, ALU.mult, ALU.max)
                elif k == 2:
                    last = dve.reciprocal(inv, s_b)
                elif k == 3:
                    last = dve.tensor_tensor(wb, wb, per_block(inv), ALU.mult)
                elif k == 4:
                    last = dve.tensor_scalar(w, w, MAGIC, MAGIC, ALU.add, ALU.subtract)
                elif k == 5:
                    last = dve.tensor_scalar(w, w, 7.0, -8.0, ALU.min, ALU.max)
                else:
                    last = dve.tensor_tensor(wb, wb, per_block(s_b), ALU.mult)
                last.then_inc(sem("quantise_steps"), 1)

            def prepare_quantising():
                pcs = of_layer["L0_ffn"]
                s0 = slot_of[pcs[0]]
                dve.memset(ring_a[:, s0:s0 + 3, 1536:QSLICE * ITERS * QBLOCK], 0.0
                           ).then_inc(sem("quantise_steps"), 1)
                for piece in pcs:
                    piece_arrived(dve, piece)

            def quantise_16(t, z):
                dve.tensor_reduce(amax[:, z:z + 1], t, AX.X, ALU.max, apply_absolute_value=True
                                  ).then_inc(sem("amax_ready"), 1)
                dve.wait_ge(sem("amax_all_ready"), z + 1)
                s, inv = qs[:, z:z + 1], qinv[:, z:z + 1]
                chained(dve.tensor_scalar(s, amax_all[:, z:z + 1], 1.0 / 32767.0, 1e-12, ALU.mult, ALU.max))
                chained(dve.reciprocal(inv, s))
                chained(dve.tensor_scalar(t, t, inv, MAGIC, ALU.mult, ALU.add))
                chained(dve.tensor_scalar(t, t, MAGIC, 32767.0, ALU.subtract, ALU.min))
                return dve.tensor_scalar(t, t, -32768.0, s, ALU.max, ALU.mult)

            def l0_ffn():
                if not x_layers:
                    prepare_quantising()
                    for i in range(ITERS):
                        for k in range(QSTEPS):
                            quantise_step(i, k)
                chained(normalise("L0_ffn", x[:, :]))
                quantise_16(xn[:, :], 0).then_inc(sem("xn_ready"), 1)
                transposed("L0_ffn")
                for m, t in enumerate((l0_gate, l0_up)):
                    dve.wait_ge(sem("gate_up_in_psum"), m + 1)
                    chained(dve.tensor_copy(t[:, 0:512], ps[:, 2 + 2 * m, :]))
                    chained(dve.tensor_copy(t[:, 512:768], ps[:, 3 + 2 * m, 0:256]))
                    if m == 0:
                        quantise_16(t, 1).then_inc(sem("l0_gate_ready"), 1)
                    else:
                        chained(quantise_16(t, 2))
                sg = l0_tmp[:, 0:768]
                s2 = l0_tmp[:, 768:1536]
                dve.wait_ge(sem("l0_exp_ready"), 1)
                chained(dve.tensor_scalar(sg, sg, 1.0, None, ALU.add))
                chained(dve.reciprocal(s2, sg))
                chained(dve.tensor_scalar(s2, s2, 65536.0, MAGIC, ALU.mult, ALU.add))
                chained(dve.tensor_scalar(s2, s2, MAGIC, 65535.0, ALU.subtract, ALU.min))
                chained(dve.tensor_scalar(s2, s2, 0.0, 1.0 / 65536.0, ALU.max, ALU.mult))
                chained(dve.tensor_tensor(l0_gate, l0_gate, s2, ALU.mult))
                chained(quantise_16(l0_gate, 3))
                chained(dve.tensor_tensor(l0_h, l0_gate, l0_up, ALU.mult))
                quantise_16(l0_h, 4).then_inc(sem("l0_h_ready"), 1)
                dve.wait_ge(sem("l0_hT_in_psum"), 1)
                dve.tensor_copy(l0_hT[:, 0:512], ps[:, 6, :])
                dve.tensor_copy(l0_hT[:, 512:768], ps[:, 7, 0:256]).then_inc(sem("l0_hT_ready"), 1)
                add_y("l0_ffn_y", 1)

            def l1_ffn():
                ln("L1_ffn")

                def scaled(dst, banks, s_name):
                    s = cols[:, COL_AT[s_name]:COL_AT[s_name] + FT].rearrange("p (b f) -> p b f", b=2)
                    for b in range(2):
                        last = dve.tensor_tensor(dst[:, b * 512:(b + 1) * 512].rearrange("p (f t) -> p f t", f=4),
                                                 ps[:, banks[b], :].rearrange("p (f t) -> p f t", f=4),
                                                 s[:, b, :].unsqueeze(2).broadcast_to([P, 4, P]), ALU.mult)
                    return last

                dve.wait_ge(sem("consts_loaded"), 16 * 10)
                dve.wait_ge(sem("swiglu_in_psum"), 1)
                scaled(f_b, (2, 3), "w1_s").then_inc(sem("w1_scaled"), 1)
                dve.wait_ge(sem("swiglu_in_psum"), 2)
                chained(scaled(f_a, (4, 5), "w2_s"))
                chained(dve.tensor_tensor(f_a, f_a, f_b, ALU.mult))
                dve.wait_ge(sem("silu_exp"), 1)
                chained(dve.tensor_scalar(f_c, f_c, 1.0, None, ALU.add))
                chained(dve.reciprocal(f_d, f_c))
                dve.tensor_tensor(f_a, f_a, f_d, ALU.mult).then_inc(sem("swiglu_ready"), 1)
                dve.wait_ge(sem("l1_ffn_y"), 1)
                chained(dve.tensor_tensor(y[:, :], ps[:, 0, 0:DM], wide[:, 0, :], ALU.mult))
                chained(dve.tensor_tensor(x[:, :], x[:, :], y[:, :], ALU.add))

            def l2_ffn():
                piece, = of_layer["L2_ffn"]
                piece_arrived(dve, piece)
                chained(dve.tensor_copy(work[:, 0:512], slot(piece)[:, 0:512].bitcast(I32)))
                dve.tensor_scalar(work[:, 0:512], work[:, 0:512], -1.0, None, ALU.add).then_inc(sem("l2f_w_ready"), 1)
                dve.wait_ge(sem("consts_loaded"), 16 * 10)
                s, inv = qscale[:, 0:1], qscale[:, 1:2]
                chained(dve.tensor_scalar(s, act_scale[:, :], 1e-5, None, ALU.max))
                chained(dve.reciprocal(inv, s))
                chained(normalise("L2_ffn", x[:, :]))
                t = xn[:, :]
                pos, neg = scratch[:, 0:DM], scratch[:, DM:2 * DM]
                big, tmp = scratch[:, 2 * DM:3 * DM], scratch[:, 3 * DM:4 * DM]
                chained(dve.tensor_scalar(t, t, inv, MAGIC, ALU.mult, ALU.add))
                chained(dve.tensor_scalar(t, t, MAGIC, 127.0, ALU.subtract, ALU.min))
                chained(dve.tensor_scalar(t, t, -127.0, s, ALU.max, ALU.mult))
                chained(dve.tensor_scalar(pos, t, 0.0, None, ALU.max))
                chained(dve.tensor_scalar(neg, t, 0.0, None, ALU.min))
                for part, over, clip, limit, value in ((pos, ALU.is_gt, ALU.min, FLT_MAX, 1e4),
                                                       (neg, ALU.is_lt, ALU.max, -FLT_MAX, -1e4)):
                    within = ALU.is_le if part is pos else ALU.is_ge
                    chained(dve.tensor_scalar(big, part, limit, value, over, ALU.mult))
                    chained(dve.tensor_scalar(tmp, part, limit, None, clip))
                    chained(dve.scalar_tensor_tensor(part, part, limit, tmp, within, ALU.mult))
                    chained(dve.tensor_tensor(part, part, big, ALU.add))
                dve.tensor_tensor(t, pos, neg, ALU.add).then_inc(sem("xn_ready"), 1)
                transposed("L2_ffn")
                add_y("l2_ffn_y", 1)

            def l3_xattn():
                if gate_rider is None:
                    with dve.Fori(0, GROUPS * ITERS) as u:
                        for k in range(GATE_STEPS):
                            gate_step(u, k)
                dve.wait_ge(sem("gate_sums"), (1 + GROUPS * ITERS) * GATE_STEPS)
                chained(dve.tensor_reduce(gate[:, :], gate_part[:, :, :], AX.X, ALU.add))
                ln("L3_xattn")
                for e in range(EXPERTS):
                    dve.wait_ge(sem("expert_down"), e + 1)
                    last = dve.scalar_tensor_tensor(x[:, :], ps[:, 4 + e % 2, 0:DM], gate[:, e:e + 1], x[:, :],
                                                    ALU.mult, ALU.add)
                    last.then_inc(sem("expert_added"), 1)
                    dve.wait_ge(sem("expert_added"), e + 1)

            def l3_ffn():
                ln("L3_ffn")
                dve.wait_ge(sem("logits_in_psum"), 1)
                chained(dve.tensor_copy(logits, ps[:, 1, 0:EXPERTS]))
                chained(dve.max(top8, logits))
                chained(dve.max_index(top_i[:, :], top8, logits))
                chained(dve.tensor_copy(top_if[:, :], top_i[:, :]))
                dve.tensor_tensor(top_w[:, 0:1], top8[:, 1:2], top8[:, 0:1], ALU.subtract).then_inc(sem("top_diff"), 1)
                dve.wait_ge(sem("top_exp"), 1)
                chained(dve.tensor_scalar(top_w[:, 2:3], top_w[:, 1:2], 1.0, None, ALU.add))
                chained(dve.reciprocal(top_w[:, 2:3], top_w[:, 2:3]))
                chained(dve.tensor_tensor(top_w[:, 3:4], top_w[:, 1:2], top_w[:, 2:3], ALU.mult))
                chained(dve.memset(combine[:, EXPERTS:EXPERTS + 1], 1.0))
                chained(dve.tensor_scalar(pick, iota8[:, :], top_if[:, 1:2], top_w[:, 3:4], ALU.is_equal, ALU.mult))
                chained(dve.tensor_scalar(combine[:, 0:EXPERTS], iota8[:, :], top_if[:, 0:1], top_w[:, 2:3],
                                          ALU.is_equal, ALU.mult))
                dve.tensor_tensor(combine[:, 0:EXPERTS], combine[:, 0:EXPERTS], pick, ALU.add
                                  ).then_inc(sem("combine_ready"), 1)
                dve.wait_ge(sem("combine_T_psum"), 1)
                dve.tensor_copy(combine_T[:, :], ps[0:EXPERTS + 1, 1, 0:P]).then_inc(sem("combine_T_ready"), 1)
                dve.wait_ge(sem("moe_bias"), 1)
                chained(dve.tensor_tensor(x[:, :], x[:, :], ps[:, 1, 0:DM], ALU.add))
                for e in range(EXPERTS + 1):
                    dve.wait_ge(sem("moe_down"), e + 1)
                    dve.scalar_tensor_tensor(x[:, :], ps[:, 6 + e % 2, 0:DM], combine[:, e:e + 1], x[:, :],
                                             ALU.mult, ALU.add).then_inc(sem("moe_added"), 1)
                    dve.wait_ge(sem("moe_added"), e + 1)

            dve.wait_ge(sem("x_loaded"), 16)
            dve.wait_ge(sem("pool_consts"), 7)
            dve.wait_ge(sem("consts_loaded"), 16 * 10)
            if has_gate:
                dve.sem_inc(sem("gate_sums"), GATE_STEPS)
            for name in layers:
                if name in XATTN:
                    cross_attention(name)
                elif name in SATTN:
                    softmax_attention(name)
                else:
                    {"L0_ffn": l0_ffn, "L1_ffn": l1_ffn, "L2_ffn": l2_ffn, "L3_xattn": l3_xattn,
                     "L3_attn": linear_attention, "L3_ffn": l3_ffn}[name]()
            dve.drain().then_inc(sem("x_final"), 1)


def lay_out(a):
    a = {k: np.asarray(v) for k, v in a.items()}

    def tiles(w):
        k = w.shape[0] // P
        return np.ascontiguousarray(w.reshape(k, P, -1).transpose(1, 0, 2).reshape(P, -1))

    def per_pair_T(w):
        return np.ascontiguousarray(w.reshape(CD, STACKS, -1).transpose(2, 1, 0).reshape(-1, STACKS * CD))

    def out_in(w):
        return np.ascontiguousarray(w.reshape(-1, P, w.shape[1]).transpose(1, 0, 2).reshape(P, -1))

    ctx = a["ctx_512"][0]
    row_head = (np.arange(P)[:, None] // 16) % 2
    head_half = np.where(row_head == np.arange(2)[None], 0.25, 0.0).astype(np.float32)
    d = {
        "x": a["x"][0],
        "ctxT": ctx.T,
        "ctx_rows": ctx.reshape(KT, P, CD).transpose(1, 0, 2),
        "tokT": a["itok_BxS2xS_0_7"][0].T,
        "L0x_q": tiles(a["L0_xattn_Wq"]), "L0x_v": a["L0_xattn_Wv"], "L0x_o": tiles(a["L0_xattn_Wo"]),
        "L0x_k": a["L0_xattn_Wk"], "L2x_k": a["L2_xattn_Wkv"][:DM].T,
        "L0x_kT": per_pair_T(a["L0_xattn_Wk"]), "bkT": a["L0_xattn_bk"].reshape(STACKS, 32).T,
        "L0a_w": np.concatenate([
            tiles(np.concatenate([a["L0_attn_Wqt"], a["L0_attn_Wqs"]], 1)),
            tiles(np.concatenate([a["L0_attn_Wkt"], a["L0_attn_Wks"]], 1)),
            tiles(a["L0_attn_Wv"]), tiles(a["L0_attn_Wout"])], 1),
        "L0f_gate": out_in(a["L0_ffn_w_gate"]), "L0f_up": out_in(a["L0_ffn_w_up"]),
        "L0f_down": out_in(a["L0_ffn_w_down"]),
        "L1x_q": tiles(a["L1_xattn_Wq"]), "L1x_kT": per_pair_T(a["L1_xattn_Wk"]),
        "L1x_v": a["L1_xattn_Wv"], "L1x_o": tiles(a["L1_xattn_Wo"]),
        "L1a_w": np.concatenate([tiles(a[f"L1_attn_{n}_proj_weight"].T) for n in "qkvo"], 1),
        "L1f_w1": tiles(a["L1_ffn_w1_w"].T), "L1f_w2": tiles(a["L1_ffn_w2_w"].T), "L1f_w3": tiles(a["L1_ffn_w3_w"].T),
        "L2x_q": tiles(a["L2_xattn_Wq"].T), "L2x_o": tiles(a["L2_xattn_Wo"].T),
        "L2x_kT": per_pair_T(a["L2_xattn_Wkv"][:DM].T), "L2x_v": a["L2_xattn_Wkv"][DM:].T,
        "L2f_w": tiles(a["L2_ffn_ternary_weight"].T),
        "L3a_w": np.concatenate([tiles(a[f"L3_attn_W{n}"].T) for n in "qkvo"], 1),
        "w3_s": a["L1_ffn_w3_s"], "gamma": a["L2_attn_gamma"], "beta": a["L2_attn_beta"],
        "bv": a["L0_xattn_bv"],
        "w_sigma": a["L0_attn_w_sigma"].reshape(1), "act_scale": a["L2_ffn_act_scale"].reshape(1),
        "b2": np.concatenate([a["L3_ffn_b2"], a["L3_ffn_bs2"][None]], 0),
        "rows": np.concatenate([a["L0_xattn_bq"], a["L0_xattn_bo"], a["L0_attn_bout"],
                                a["L1_xattn_bo"], a["L2_ffn_bias"], a["L3_ffn_gate_b"]])[None],
        "cols": np.concatenate([
            *[a[f"L1_ffn_{n}"].reshape(FT, P).T for n in ("w1_s", "w2_s", "h1_s", "h2_s")],
            a["L3_ffn_b1"].reshape(EXPERTS * FT, P).T, a["L3_ffn_bs1"].reshape(FT, P).T,
            tiles(a["L3_ffn_gate_w"]), head_half], 1),
    }
    for m in ("h1", "h2"):
        w = a[f"L1_ffn_{m}_w"].T
        for i in range(4):
            d[f"L1f_{m}_{i}"] = tiles(w[:, i * 256:(i + 1) * 256])
    for n in "qkv":
        d[f"L2a_{n}"] = tiles(a[f"L2_attn_W{n}"].transpose(1, 0, 2).reshape(DM, -1))
    d["L2a_o"] = tiles(a["L2_attn_Wo"])
    for e in range(EXPERTS):
        d[f"L3x_in{e}"] = tiles(a["L3_xattn_proj_in"][e].T)
        d[f"L3x_out{e}"] = tiles(a["L3_xattn_proj_out"][e].T)
        d[f"L3f_w1_{e}"], d[f"L3f_w2_{e}"] = tiles(a["L3_ffn_w1"][e]), tiles(a["L3_ffn_w2"][e])
    d[f"L3f_w1_{EXPERTS}"], d[f"L3f_w2_{EXPERTS}"] = tiles(a["L3_ffn_ws1"]), tiles(a["L3_ffn_ws2"])
    return {k: np.ascontiguousarray(v) for k, v in d.items()}


def kernel(**inputs):
    import concourse.bacc as bacc
    from concourse.bass_utils import run_bass_kernel_spmd

    arrays = {f"in_{k}": v for k, v in lay_out(inputs).items()}
    nc = bacc.Bacc("TRN2", target_bir_lowering=False, num_devices=1)
    dram = {k[3:]: nc.dram_tensor(k, v.shape, mybir.dt.from_np(v.dtype), kind="ExternalInput").ap()
            for k, v in arrays.items()}
    out = nc.dram_tensor("out", (P, DM), F32, kind="ExternalOutput").ap()
    build_program(nc, dram, out)
    result = run_bass_kernel_spmd(nc, [arrays], core_ids=[0])
    return result.results[0]["out"].reshape(1, P, DM)
```
